# Optimizing a Trainium2 kernel written in Bass

```python
import numpy as np
import jax
import jax.numpy as jnp

def _softmax(x, axis=-1):
    return jax.nn.softmax(x, axis=axis)

def _gelu(x):
    return jax.nn.gelu(x, approximate=True)

def _silu(x):
    return jax.nn.silu(x)

def _sigmoid(x):
    return jax.nn.sigmoid(x)

def _layernorm(x, axis=-1, eps=1e-05):
    m = jnp.mean(x, axis=axis, keepdims=True)
    v = jnp.var(x, axis=axis, keepdims=True)
    return (x - m) / jnp.sqrt(v + eps)

def _scatter_add(tgt, idx, src, axis=0):
    return tgt.at[idx].add(src)

def _segment_sum(src, seg, n):
    return jax.ops.segment_sum(src, seg, n)
kernel_name = 'mk_adaln_d1_jaxref_r4_c97d4c'

def setup_inputs(seed: int=0):
    np.random.seed(seed)
    _w = jnp.asarray

    def _L0_attn_setup():
        import jax, jax.numpy as jnp
        import numpy as np
        B, S, D, F = (8, 512, 256, 768)
        EPS = 1e-06

        def _rmsnorm(x, w):
            rms = jax.lax.rsqrt(jnp.mean(x * x, axis=-1, keepdims=True) + EPS)
            return x * rms * w

        def _scan_causal(x_scan, a):

            def step(h, inp):
                xs, at = inp
                h = at * h + xs
                return (h, h)
            xs_t = jnp.swapaxes(x_scan, 0, 1)
            a_t = jnp.swapaxes(a, 0, 1)
            h0 = jnp.zeros(x_scan.shape[::2], dtype=x_scan.dtype)
            _, out = jax.lax.scan(step, h0, (xs_t, a_t))
            return jnp.swapaxes(out, 0, 1)
        key = jax.random.key(seed)
        ks = jax.random.split(key, 12)
        sd = 1.0 / np.sqrt(D)
        sf = 1.0 / np.sqrt(F)
        return {'x': jax.random.normal(ks[0], (B, S, D), dtype=jnp.float32), 'rms_mix_w': jnp.ones((D,), jnp.float32), 'rms_ffn_w': jnp.ones((D,), jnp.float32), 'Wg': jax.random.uniform(ks[1], (D, D), jnp.float32, -sd, sd), 'bg': jax.random.uniform(ks[2], (D,), jnp.float32, -sd, sd), 'Wv': jax.random.uniform(ks[3], (D, D), jnp.float32, -sd, sd), 'bv': jax.random.uniform(ks[4], (D,), jnp.float32, -sd, sd), 'Wd': jax.random.uniform(ks[5], (D, D), jnp.float32, -sd, sd), 'bd': jnp.full((D,), 1.0, jnp.float32), 'W_gate': jax.random.uniform(ks[6], (F, D), jnp.float32, -sd, sd), 'W_up': jax.random.uniform(ks[7], (F, D), jnp.float32, -sd, sd), 'W_out': jax.random.uniform(ks[8], (D, F), jnp.float32, -sf, sf)}
    _L0_attn_in = _L0_attn_setup()

    def _L0_ffn_setup():
        import jax, jax.numpy as jnp
        import numpy as np
        D = 256
        F = 704
        E = 8
        TOP_K = 2
        key = jax.random.key(seed)
        ks = jax.random.split(key, 6)
        std = 0.02
        x = jax.random.normal(ks[0], (2, 512, D), dtype=jnp.float32)
        router_w = jax.random.normal(ks[1], (D, E), dtype=jnp.float32) * std
        w1 = jax.random.normal(ks[2], (E, D, F), dtype=jnp.float32) * std
        v1 = jax.random.normal(ks[3], (E, D, F), dtype=jnp.float32) * std
        w2 = jax.random.normal(ks[4], (E, F, D), dtype=jnp.float32) * std
        bias = jnp.zeros((D,), dtype=jnp.float32)
        return {'x': x, 'router_w': router_w, 'w1': w1, 'v1': v1, 'w2': w2, 'bias': bias}
    _L0_ffn_in = _L0_ffn_setup()
    _L0_c = _w((lambda *s: np.random.randn(*s).astype(np.float32) * 0.05)(2, 256))
    _L0_wmod = _w((lambda *s: np.random.randn(*s).astype(np.float32) * 0.05)(256, 6 * 256) * 256 ** (-0.5))
    _d = {'L0_attn_x': _L0_attn_in['x'], 'L0_attn_rms_mix_w': _L0_attn_in['rms_mix_w'], 'L0_attn_rms_ffn_w': _L0_attn_in['rms_ffn_w'], 'L0_attn_Wg': _L0_attn_in['Wg'], 'L0_attn_bg': _L0_attn_in['bg'], 'L0_attn_Wv': _L0_attn_in['Wv'], 'L0_attn_bv': _L0_attn_in['bv'], 'L0_attn_Wd': _L0_attn_in['Wd'], 'L0_attn_bd': _L0_attn_in['bd'], 'L0_attn_W_gate': _L0_attn_in['W_gate'], 'L0_attn_W_up': _L0_attn_in['W_up'], 'L0_attn_W_out': _L0_attn_in['W_out'], 'L0_ffn_router_w': _L0_ffn_in['router_w'], 'L0_ffn_w1': _L0_ffn_in['w1'], 'L0_ffn_v1': _L0_ffn_in['v1'], 'L0_ffn_w2': _L0_ffn_in['w2'], 'L0_ffn_bias': _L0_ffn_in['bias'], 'L0_c': _L0_c, 'L0_wmod': _L0_wmod}
    _x0 = _d['L0_attn_x']
    _d['L0_attn_x'] = jax.random.normal(jax.random.fold_in(jax.random.key(seed), 1), (2, 2048, 256), dtype=_x0.dtype)
    del _x0
    return _d

def reference(L0_attn_x, L0_attn_rms_mix_w, L0_attn_rms_ffn_w, L0_attn_Wg, L0_attn_bg, L0_attn_Wv, L0_attn_bv, L0_attn_Wd, L0_attn_bd, L0_attn_W_gate, L0_attn_W_up, L0_attn_W_out, L0_ffn_router_w, L0_ffn_w1, L0_ffn_v1, L0_ffn_w2, L0_ffn_bias, L0_c, L0_wmod):

    def _L0_attn_ref(x, rms_mix_w, rms_ffn_w, Wg, bg, Wv, bv, Wd, bd, W_gate, W_up, W_out):
        import jax, jax.numpy as jnp
        import numpy as np
        B, S, D, F = (8, 512, 256, 768)
        EPS = 1e-06

        def _rmsnorm(x, w):
            rms = jax.lax.rsqrt(jnp.mean(x * x, axis=-1, keepdims=True) + EPS)
            return x * rms * w

        def _scan_causal(x_scan, a):

            def step(h, inp):
                xs, at = inp
                h = at * h + xs
                return (h, h)
            xs_t = jnp.swapaxes(x_scan, 0, 1)
            a_t = jnp.swapaxes(a, 0, 1)
            h0 = jnp.zeros(x_scan.shape[::2], dtype=x_scan.dtype)
            _, out = jax.lax.scan(step, h0, (xs_t, a_t))
            return jnp.swapaxes(out, 0, 1)
        xn = _rmsnorm(x, rms_mix_w)
        g = jnp.einsum('bsd,ed->bse', xn, Wg) + bg
        v = jnp.einsum('bsd,ed->bse', xn, Wv) + bv
        d = jnp.einsum('bsd,ed->bse', xn, Wd) + bd
        x_scan = jax.nn.sigmoid(g) * jnp.tanh(v)
        a = 0.001 + 0.998 * jax.nn.sigmoid(d)
        x = x + _scan_causal(x_scan, a)
        xn = _rmsnorm(x, rms_ffn_w)
        gate = jax.nn.silu(jnp.einsum('bsd,fd->bsf', xn, W_gate))
        up = jnp.einsum('bsd,fd->bsf', xn, W_up)
        x = x + jnp.einsum('bsf,df->bsd', gate * up, W_out)
        return x

    def _L0_ffn_ref(x, router_w, w1, v1, w2, bias):
        import jax, jax.numpy as jnp
        import numpy as np
        D = 256
        F = 704
        E = 8
        TOP_K = 2
        B, S, d = x.shape
        xt = x.reshape(B * S, d)
        scores = jax.nn.softmax(xt @ router_w, axis=-1)
        expert_weights, expert_idx = jax.lax.top_k(scores, TOP_K)
        h = jax.nn.gelu(jnp.einsum('td,edf->tef', xt, w1), approximate=False) * jnp.einsum('td,edf->tef', xt, v1)
        y = jnp.einsum('tef,efd->ted', h, w2)
        yk = jnp.take_along_axis(y, expert_idx[:, :, None], axis=1)
        out = jnp.sum(expert_weights[:, :, None] * yk, axis=1) + bias
        return out.reshape(B, S, d)
    x = L0_attn_x
    mod = (_silu(L0_c) @ L0_wmod).reshape(L0_c.shape[0], 6, 1, -1)
    sa, ca, ga, sb, cb, gb = (mod[:, 0], mod[:, 1], mod[:, 2], mod[:, 3], mod[:, 4], mod[:, 5])
    ga = (2 * (ga >= 0) - 1) * jnp.maximum(jnp.abs(ga), 0.25)
    gb = (2 * (gb >= 0) - 1) * jnp.maximum(jnp.abs(gb), 0.25)
    h = _layernorm(x, axis=-1) * (1 + ca) + sa
    x = x + ga * _L0_attn_ref(h, L0_attn_rms_mix_w, L0_attn_rms_ffn_w, L0_attn_Wg, L0_attn_bg, L0_attn_Wv, L0_attn_bv, L0_attn_Wd, L0_attn_bd, L0_attn_W_gate, L0_attn_W_up, L0_attn_W_out)
    h = _layernorm(x, axis=-1) * (1 + cb) + sb
    x = x + gb * _L0_ffn_ref(h, L0_ffn_router_w, L0_ffn_w1, L0_ffn_v1, L0_ffn_w2, L0_ffn_bias)
    return x

_drawn_inputs = setup_inputs


def setup_inputs(seed=0):
    import zlib

    import numpy as np

    out = dict(_drawn_inputs(seed))
    spreads = {'L0_attn_rms_mix_w': (1.0, 0.6),
     'L0_attn_rms_ffn_w': (1.0, 0.6),
     'L0_attn_bd': (1.0, 0.6),
     'L0_ffn_bias': (0.0, 1.116)}
    factors = {'L0_attn_bg': 8.0,
     'L0_attn_bv': 4.575,
     'L0_attn_Wd': 3.815,
     'L0_ffn_router_w': 8.0,
     'L0_ffn_w1': 8.0,
     'L0_ffn_v1': 8.0,
     'L0_ffn_w2': 8.0}
    for name, (base, spread) in spreads.items():
        noise = np.random.default_rng([zlib.crc32(name.encode()), seed]).standard_normal(out[name].shape)
        drawn = base * np.exp(spread * noise) if base else spread * noise
        out[name] = jnp.asarray(drawn.astype(out[name].dtype))
    for name, factor in factors.items():
        out[name] = (out[name] * factor).astype(out[name].dtype)
    return out
```

```python
from contextlib import ExitStack

import numpy as np

import concourse.bass as bass
from concourse import mybir

P = 128
B, S, D = 2, 2048, 256
T = B * S
KD = D // P
BLK = 512
TPB = BLK // P
NBLK = T // BLK
FA = 768
KFA = FA // P
E, F, TOPK = 8, 704, 2
KF = -(-F // P)
F_LAST = F - (KF - 1) * P
FH = F // 2
ROW = D + E + 1
REGION = T + P
ROWS = E * REGION + P
MOE_TILES = (TOPK * T + E * (P - 1)) // P
PAD_TILE = MOE_TILES
EXPW = KD * 2 * F + KF * D
EPS_LN, EPS_RMS = 1e-5, 1e-6

ALU = mybir.AluOpType
ACT = mybir.ActivationFunctionType
AX = mybir.AxisListType
F32, F32R = mybir.dt.float32, mybir.dt.float32r
BF16, I32, U32 = mybir.dt.bfloat16, mybir.dt.int32, mybir.dt.uint32

C_ID, C_TRI, C_IOTA, C_OFF, C_TOK, C_PAD = 0, P, 2 * P, 2 * P + TPB * E, 2 * P + TPB * E + E, 2 * P + TPB * E + E + B * TPB
C_TILE = C_PAD + 1
C_N = C_TILE + 1
V_BIAS, V_MIX, V_FFN, V_N = 0, 3 * KD, 4 * KD, 5 * KD
M_S1, M_A1, M_S2, M_A2, M_GBB, M_N = 0, 1, 2, 3, 4, 5


def constants():
    c = np.zeros((P, C_N), np.float32)
    p = np.arange(P)
    c[:, C_ID:C_ID + P] = np.eye(P)
    c[:, C_TRI:C_TRI + P] = p[:, None] < p[None, :]
    c[:, C_IOTA:C_IOTA + TPB * E] = np.tile(np.arange(E), TPB)
    c[:, C_OFF:C_OFF + E] = np.arange(E) * REGION
    for b in range(B):
        for i in range(TPB):
            c[:, C_TOK + b * TPB + i] = b * S + i * P + p
    c[:, C_PAD] = T + p
    c[:, C_TILE] = p
    return c


class Block512:

    def __init__(self, n, turn=None):
        self.n, self.turn = n, turn
        self.par = n % 2
        self.v = n if turn is None else turn * 2 + n
        self.half = n // 2 if turn is None else turn + n // 2

    def near(self, d):
        return Block512(self.n + d, self.turn)


def ring_plan(banks):
    order = []
    for r in range(NBLK + 2):
        if r >= 2:
            order += [("gu", r - 2, k) for k in range(2 * KFA)] + [("out", r - 2, k) for k in range(2)]
        if r < NBLK:
            order += [("gvd", r, k) for k in range(3 * KD)]
    return {u: (n % banks, order[n - banks] if n >= banks else None) for n, u in enumerate(order)}


def adaln_moe_kernel(nc, x, gvd_t, gu_t, out_t, vecs, cond_t, wmod, bias, router, w13, w2, consts, out):
    RING = 5
    ring = ring_plan(RING)
    ctx = ExitStack()
    base = (nc.sbuf_base + 63) // 64 * 64
    place = [base + E * EXPW * 4]

    def at(name, shape, dt, offset=None):
        size = int(np.prod(shape[1:])) * (2 if dt == BF16 else 4)
        if offset is None:
            offset = place[0]
            place[0] = (offset + size + 31) // 32 * 32
        return nc.alloc_sbuf_tensor_at(name, shape, dt, offset=offset)

    with ctx:
        def sem(name):
            return ctx.enter_context(nc.semaphore(name))

        RES = 1
        experts = at("experts", [P, E * EXPW], F32, base)
        keep = ((C_N + B * 2 * D + P + E + ROW + 2) * 4 + 6 * 32 + 31) // 32 * 32
        top_at = nc.sbuf_usable_end // 32 * 32 - keep
        place[0] = top_at
        cn = at("cn", [P, C_N], F32)
        gates = at("gates", [P, B, 2, D], F32)
        tab = at("tab", [P, P], I32)
        counts_i = at("counts_i", [P, E], I32)
        pad_rows = at("pad_rows", [P, ROW], F32)
        g_mark = at("g_mark", [P, 2], F32)
        place[0] = base + E * EXPW * 4
        x_moe = at("x_moe", [P, 2, ROW], F32)
        xT_moe = at("xT_moe", [P, 2, KD, P], F32)
        gelu_moe = at("gelu_moe", [P, 2, FH], F32)
        hid_moe = at("hid_moe", [P, F], F32)
        hidT_moe = at("hidT_moe", [P, KF, P], F32)
        y_moe = at("y_moe", [P, 2, 2, D], F32)
        gate_moe = at("gate_moe", [P, 2, 4], F32)
        tok_moe = at("tok_moe", [P, 2, 1], I32)
        assert place[0] <= top_at
        place[0] = base
        gvd_raw = at("gvd_raw", [P, KD, 3 * D], F32)
        assert place[0] <= base + RES * EXPW * 4
        place[0] = base + RES * EXPW * 4
        gvd_hi, gvd_lo = (at(f"gvd_{s}", [P, KD, 3 * D], F32R) for s in ("hi", "lo"))
        gu_hi, gu_lo = (at(f"gu_{s}", [P, KD, 2 * FA], F32R) for s in ("hi", "lo"))
        out_hi, out_lo = (at(f"out_{s}", [P, KFA, D], F32R) for s in ("hi", "lo"))
        hid_at = place[0]
        hid_hi, hid_lo = (at(f"hid_{s}", [P, KFA, BLK], F32R) for s in ("hi", "lo"))
        gu_raw = at("gu_raw", [P, KD, 2 * FA], F32, hid_at)
        wmod_sb = at("wmod_sb", [P, KD, 6 * D], F32, hid_at + KD * 2 * FA * 4)
        assert hid_at + 2 * KD * 2 * FA * 4 <= place[0]
        xnT_hi, xnT_lo = (at(f"xnT_{s}", [P, KD, BLK], F32R) for s in ("hi", "lo"))
        xn2T_hi, xn2T_lo = (at(f"xn2T_{s}", [P, KD, BLK], F32R) for s in ("hi", "lo"))
        mod = at("mod", [P, B, M_N, D], F32)
        x_sb = at("x_sb", [P, TPB, D], F32)
        x_again = at("x_again", [P, TPB, D], F32)
        h_sb = at("h_sb", [P, 2, TPB, D], F32)
        xa_sb = at("xa_sb", [P, 2, TPB, D], F32)
        g_raw = at("g_raw", [P, B * 2 * D], F32, place[0])
        xo_sb = at("xo_sb", [P, TPB, D], F32)
        xn_sb = at("xn_sb", [P, TPB, D], F32)
        sg_sb = at("sg_sb", [P, KD, BLK], F32)
        tv_sb = at("tv_sb", [P, KD, BLK], F32)
        dec_sb = at("dec_sb", [P, KD, BLK], F32)
        sig_sb = at("sig_sb", [P, 2, BLK], F32)
        gg_sb = at("gg_sb", [P, 2, BLK], F32)
        hf_sb = at("hf_sb", [P, 2, BLK], F32)
        rows = at("rows", [P, 2, TPB, ROW], F32)
        ct_rep = at("ct_rep", [P, KD * B, P], F32, place[0])
        hT_sb = at("hT_sb", [P, KD, BLK], F32)
        squares = at("squares", [P, TPB, D], F32)
        squares2 = at("squares2", [P, TPB, D], F32)
        vec = at("vec", [P, V_N], F32)
        rw_sb = at("rw_sb", [P, KD, E], F32)
        bias_row = at("bias_row", [P, D], F32)
        ct = at("ct", [P, KD, B], F32)
        ct_sig = at("ct_sig", [P, KD, B], F32)
        carry = at("carry", [P, B, KD], F32)
        tri = at("tri", [P, P], BF16)
        ones = at("ones", [P, P], BF16)
        ones_f = at("ones_f", [P, E], F32)
        minus_half = at("minus_half", [P, TPB], F32)
        stats = at("stats", [P, TPB, 6], F32)
        mv = at("mv", [P, TPB, 2], F32)
        ve = at("ve", [P, TPB], F32)
        rstd = at("rstd", [P, TPB], F32)
        ssq = at("ssq", [P, TPB], F32)
        ms = at("ms", [P, TPB], F32)
        rms = at("rms", [P, TPB], F32)
        ssq2 = at("ssq2", [P, TPB], F32)
        ms2 = at("ms2", [P, TPB], F32)
        rms2 = at("rms2", [P, TPB], F32)
        stats2 = at("stats2", [P, TPB, 6], F32)
        mv2 = at("mv2", [P, TPB, 2], F32)
        ve2 = at("ve2", [P, TPB], F32)
        rstd2 = at("rstd2", [P, TPB], F32)
        mx = at("mx", [P, TPB], F32)
        zz = at("zz", [P, TPB, E], F32)
        ee = at("ee", [P, TPB, E], F32)
        pp = at("pp", [P, TPB, E], F32)
        top = at("top", [P, TPB, E], F32)
        top_i = at("top_i", [P, TPB, E], U32)
        top_f = at("top_f", [P, TPB, 2], F32)
        hot = at("hot", [P, 2, TPB, E], F32)
        chosen = at("chosen", [P, TPB, E], F32)
        chosen_b = at("chosen_b", [P, TPB, E], BF16)
        seen = at("seen", [P, E], F32)
        seen_add = at("seen_add", [P, E], F32)
        seen_b = at("seen_b", [P, E], BF16)
        pos = at("pos", [P, TPB, E], F32)
        pos_k = at("pos_k", [P, 2, TPB, E], F32)
        slot_f = at("slot_f", [P, 2, TPB], F32)
        slot_i = at("slot_i", [P, 2, 2, TPB], I32)
        tok_f = at("tok_f", [P, B, TPB], F32)
        counts = at("counts", [P, E], F32)
        tiles_i = at("tiles_i", [P, E], I32)
        tiles_f = at("tiles_f", [P, E], F32)
        tiles_end = at("tiles_end", [P, E], F32)
        step_e = at("step_e", [P, E], F32)
        passed = at("passed", [P, E], F32)
        jump = at("jump", [P, E], F32)
        turn_mark = at("turn_mark", [P, 1], F32)
        tcol = at("tcol", [P, 2], F32)
        tcol2 = at("tcol2", [P, 3], F32)
        assert place[0] <= top_at, place[0] - top_at
        out_raw = h_sb

        ident = cn[:, C_ID:C_ID + P]

        ps = ctx.enter_context(nc.psum_tensor("ps", [P, 8, BLK], F32))
        tp = [ps[:, RING, :], ps[:, RING + 1, :]]
        rt = ps[:, RING + 2, :]
        logits = rt[:, 0:TPB * E].rearrange("p (i e) -> p i e", e=E)
        ranks = rt[:, 64:64 + TPB * E].rearrange("p (i e) -> p i e", e=E)
        total = rt[:, 128:128 + E]

        routed = nc.dram_tensor("routed", [ROWS, ROW], F32, kind="Internal").ap()
        xf = x.rearrange("b s d -> (b s) d")

        consts_in, mod_in, raw_in = sem("consts_in"), sem("mod_in"), [sem(f"raw_in{n}") for n in range(3)]
        small_ready = sem("small_ready")
        cond_sig, cond_act, cond_rep = sem("cond_sig"), sem("cond_act"), sem("cond_rep")
        mod_mm, mod_rows = sem("mod_mm"), sem("mod_rows")
        w_hi, w_lo = sem("w_hi"), sem("w_lo")
        experts_in = sem("experts_in")
        x_in = sem("x_in")
        bn, aggr, var_eps, rstd_r = sem("bn"), sem("aggr"), sem("var_eps"), sem("rstd_r")
        xh, h_scaled, h_ready = sem("xh"), sem("h_scaled"), sem("h_ready")
        ssq_r, ms_r, rms_r, xn_r = sem("ssq_r"), sem("ms_r"), sem("rms_r"), sem("xn_r")
        xnT_t, xnT_h, xnT_l = sem("xnT_t"), sem("xnT_h"), sem("xnT_l")
        gvd_mm, gvd_act = sem("gvd_mm"), sem("gvd_act")
        xs_r, dec_r, scanned, carried = sem("xs_r"), sem("dec_r"), sem("scanned"), sem("carried")
        sT_t, xa_r = sem("sT_t"), sem("xa_r")
        ssq2_r, ms2_r, rms2_r, xn2_r = sem("ssq2_r"), sem("ms2_r"), sem("rms2_r"), sem("xn2_r")
        xn2T_t, xn2T_h, xn2T_l = sem("xn2T_t"), sem("xn2T_h"), sem("xn2T_l")
        gu_mm = sem("gu_mm")
        sig_r, gg_r, hf_r, hid_h, hid_l = (sem(n) for n in ("sig_r", "gg_r", "hf_r", "hid_h", "hid_l"))
        out_mm, xo_r = sem("out_mm"), sem("xo_r")
        x_again_in = sem("x_again_in")
        xg_r, x1_r = sem("xg_r"), sem("x1_r")
        bn2, aggr2, var_eps2, rstd2_r = sem("bn2"), sem("aggr2"), sem("var_eps2"), sem("rstd2_r")
        xh2, h2_scaled, h2_ready = sem("xh2"), sem("h2_scaled"), sem("h2_ready")
        base_r, base_out = sem("base_r"), sem("base_out")
        hT_t, hT_c = sem("hT_t"), sem("hT_c")
        logit_mm, z_r, exp_r, rank_mm = sem("logit_mm"), sem("z_r"), sem("exp_r"), sem("rank_mm")
        route, chosen_r, slots_r = sem("route"), sem("chosen_r"), sem("slots_r")
        scattered = [sem("scattered0"), sem("scattered1")]
        total_mm, tabs, tab_t = sem("total_mm"), sem("tabs"), sem("tab_t")
        TABS = 10
        slot_steps = sem("slot_steps")
        pads_out = sem("pads_out")

        freed = {"gvd": (gvd_act, 3 * KD), "out": (xo_r, 2)}

        def bank(kind, q, k):
            return ps[:, ring[kind, q.n, k][0], :]

        def wait_bank(eng, kind, q, k):
            last = ring[kind, q.n, k][1]
            if last is None:
                return
            lk, ln, i = last
            lq = q.near(ln - q.n)
            if lk == "gu":
                eng.wait_ge((gg_r, hf_r)[i % 2], lq.v * KFA + i // 2 + 1)
            else:
                eng.wait_ge(freed[lk][0], lq.v * freed[lk][1] + i + 1)

        def load_expert(eng, e):
            o = e * EXPW
            eng.dma_start(experts[:, o:o + KD * 2 * F].rearrange("p (k n) -> p k n", k=KD),
                          w13[e].rearrange("(k p) n -> p k n", p=P)).then_inc(experts_in, 16)
            o += KD * 2 * F
            eng.dma_start(experts[:, o:o + (KF - 1) * D].rearrange("p (k n) -> p k n", k=KF - 1),
                          w2[e, 0:(KF - 1) * P, :].rearrange("(k p) n -> p k n", p=P)).then_inc(experts_in, 16)
            eng.dma_start(experts[0:F_LAST, o + (KF - 1) * D:o + KF * D],
                          w2[e, (KF - 1) * P:F, :]).then_inc(experts_in, 16)

        def mark(g):
            g.tensor_tensor(g_mark[:, 0:1], cn[:, 0:1], cn[:, 0:1], ALU.add)

        def f32(ap):
            return ap.bitcast(F32)

        def body(step, stages):
            for r in range(4):
                step(r, None)
            with stages.Fori(0, 2, 1) as turn:
                step(4, turn)
                step(5, turn)
            for r in range(8, NBLK + 3):
                step(r, None)

        with nc.Block() as block:

            @block.sync
            def _(sp):
                def load_x(q):
                    if q.n >= 1:
                        sp.wait_ge(xh, q.v)
                    sp.dma_start(x_sb[:], xf[bass.ds(q.half * BLK + q.par * S, BLK), :]
                                 .rearrange("(i p) d -> p i d", p=P)).then_inc(x_in, 16)

                def load_x_again(q):
                    if q.n >= 1:
                        sp.wait_ge(base_out, q.v * 16)
                    sp.dma_start(x_again[:], xf[bass.ds(q.half * BLK + q.par * S, BLK), :]
                                 .rearrange("(i p) d -> p i d", p=P)).then_inc(x_again_in, 16)

                def store_base(q):
                    sp.wait_ge(base_r, q.v + 1)
                    sp.dma_start(out[bass.ds(q.half * BLK + q.par * S, BLK), :]
                                 .rearrange("(i p) d -> p i d", p=P), x_again[:]).then_inc(base_out, 16)

                sp.dma_start(ct[:], cond_t).then_inc(mod_in, 16)
                sp.dma_start(wmod_sb[:], wmod.rearrange("(k p) n -> p k n", p=P)).then_inc(mod_in, 16)
                sp.dma_start(cn[:], consts).then_inc(consts_in, 16)
                sp.dma_start(vec[:], vecs).then_inc(consts_in, 16)
                sp.dma_start(bias_row[:], bias.partition_broadcast(P)).then_inc(consts_in, 16)
                sp.dma_start(rw_sb[:], router).then_inc(consts_in, 16)
                load_x(Block512(0))
                sp.dma_start(gvd_raw[:], gvd_t.rearrange("(k p) n -> p k n", p=P)).then_inc(raw_in[0], 16)
                sp.dma_start(gu_raw[:], gu_t.rearrange("(k p) n -> p k n", p=P)).then_inc(raw_in[1], 16)
                sp.dma_start(out_raw[:].rearrange("p a i d -> p (a i d)")[:, 0:KFA * D]
                             .rearrange("p (k n) -> p k n", k=KFA),
                             out_t.rearrange("(k p) n -> p k n", p=P)).then_inc(raw_in[2], 16)
                sp.wait_ge(w_lo, 2)
                sp.wait_ge(mod_mm, 6)
                for e in range(RES):
                    load_expert(sp, e)

                def step(r, turn):
                    q = Block512(r, turn)
                    if r >= 3:
                        load_x_again(q.near(-3))
                    if r + 1 < NBLK:
                        load_x(q.near(1))
                    if r >= 3:
                        store_base(q.near(-3))

                body(step, sp)
                sp.wait_ge(base_out, NBLK * 16)

            @block.tensor
            def _(pe):
                def three(dst, a_hi, a_lo, b_hi, b_lo, first, last):
                    pe.matmul(dst, a_hi, b_hi, start=first, stop=False)
                    pe.matmul(dst, a_lo, b_hi, start=False, stop=False)
                    return pe.matmul(dst, a_hi, b_lo, start=False, stop=last)

                pe.wait_ge(mod_in, 32)
                pe.wait_ge(cond_rep, 1)
                for b in range(B):
                    for n in range(3):
                        for k in range(KD):
                            mm = pe.matmul(ps[:, 3 * b + n, :], ct_rep[:, k * B + b, :],
                                           wmod_sb[:, k, n * BLK:(n + 1) * BLK], start=(k == 0), stop=(k == KD - 1))
                        mm.then_inc(mod_mm, 1)

                def xn_transposes(q):
                    pe.wait_ge(xn_r, q.v + 1)
                    for c in range(KD):
                        if q.n >= 1:
                            pe.wait_ge(xa_r, q.v * 2 - 1 + c)
                        for i in range(TPB):
                            mm = pe.transpose(tp[c][:, i * P:(i + 1) * P], xn_sb[:, i, c * P:(c + 1) * P], ident)
                        mm.then_inc(xnT_t, 1)

                def gvd(q):
                    for n in range(3 * KD):
                        kind, c = n % 3, n // 3
                        wait_bank(pe, "gvd", q, n)
                        if n == 0:
                            pe.wait_ge(xnT_l, (q.v + 1) * KD)
                        w = slice(kind * D + c * P, kind * D + (c + 1) * P)
                        for k in range(KD):
                            mm = three(bank("gvd", q, n), gvd_hi[:, k, w], gvd_lo[:, k, w],
                                       xnT_hi[:, k, :], xnT_lo[:, k, :], k == 0, k == KD - 1)
                        mm.then_inc(gvd_mm, 1)

                def state_transposes(q):
                    pe.wait_ge(carried, (q.v + 1) * KD)
                    for u in range(2):
                        if q.n >= 2:
                            pe.wait_ge(hT_c, (q.v - 2) * KD + u + 1)
                        if q.n >= 1:
                            pe.wait_ge(xn2T_l, (q.v - 1) * KD + u + 1)
                        for i in range(2):
                            for c in range(KD):
                                t = (2 * u + i) * P
                                mm = pe.transpose(tp[u][:, i * D + c * P:i * D + (c + 1) * P],
                                                  sg_sb[:, c, t:t + P], ident)
                        mm.then_inc(sT_t, 1)

                def xn2_transposes(q):
                    pe.wait_ge(xn2_r, q.v + 1)
                    for c in range(KD):
                        if q.n + 1 < NBLK:
                            pe.wait_ge(xnT_l, (q.v + 1) * KD + c + 1)
                        for i in range(TPB):
                            mm = pe.transpose(tp[c][:, i * P:(i + 1) * P], xn_sb[:, i, c * P:(c + 1) * P], ident)
                        mm.then_inc(xn2T_t, 1)

                def gate_up(q, m):
                    if m == 0:
                        pe.wait_ge(xn2T_l, (q.v + 1) * KD)
                    for j in range(2):
                        n = 2 * m + j
                        wait_bank(pe, "gu", q, n)
                        w = slice(j * FA + m * P, j * FA + (m + 1) * P)
                        for k in range(KD):
                            mm = three(bank("gu", q, n), gu_hi[:, k, w], gu_lo[:, k, w],
                                       xn2T_hi[:, k, :], xn2T_lo[:, k, :], k == 0, k == KD - 1)
                        mm.then_inc(gu_mm, 1)

                def ffn_out(q, u):
                    wait_bank(pe, "out", q, u)
                    if u == 0:
                        pe.wait_ge(hid_l, (q.v + 1) * KFA)
                    for i in range(2):
                        t = slice((2 * u + i) * P, (2 * u + i + 1) * P)
                        for k in range(KFA):
                            mm = three(bank("out", q, u)[:, i * D:(i + 1) * D], hid_hi[:, k, t], hid_lo[:, k, t],
                                       out_hi[:, k, :], out_lo[:, k, :], k == 0, k == KFA - 1)
                    mm.then_inc(out_mm, 1)

                def h2_transposes(q):
                    pe.wait_ge(h2_ready, q.v + 1)
                    for c in range(KD):
                        pe.wait_ge(xn2T_l, (q.v + 1) * KD + c + 1 if q.n + 1 < NBLK else NBLK * KD)
                        for i in range(TPB):
                            mm = pe.transpose(tp[c][:, i * P:(i + 1) * P], rows[:, q.par, i, c * P:(c + 1) * P], ident)
                        mm.then_inc(hT_t, 1)

                def router_logits(q):
                    pe.wait_ge(hT_c, (q.v + 1) * KD)
                    if q.n >= 1:
                        pe.wait_ge(slots_r, q.v)
                    for i in range(TPB):
                        for k in range(KD):
                            mm = pe.matmul(logits[:, i, :], hT_sb[:, k, i * P:(i + 1) * P], rw_sb[:, k, :],
                                           start=(k == 0), stop=(k == KD - 1))
                    mm.then_inc(logit_mm, 1)

                def rank_tokens(q):
                    pe.wait_ge(chosen_r, q.v + 1)
                    for i in range(TPB):
                        pe.matmul(ranks[:, i, :], tri[:], chosen_b[:, i, :], start=True, stop=False)
                        for j in range(i):
                            pe.matmul(ranks[:, i, :], ones[:], chosen_b[:, j, :], start=False, stop=False)
                        mm = pe.matmul(ranks[:, i, :], ones[:], seen_b[:], start=False, stop=True)
                    mm.then_inc(rank_mm, 1)

                def step(r, turn):
                    q = Block512(r, turn)
                    last, routing, ffn = q.near(-1), q.near(-3), q.near(-2)
                    for m in range(KFA):
                        if 2 <= r < NBLK + 2:
                            gate_up(ffn, m)
                        if m == 0 and r >= 3:
                            h2_transposes(routing)
                        if m == 1 and r >= 3:
                            router_logits(routing)
                        if m == 2 and 1 <= r <= NBLK:
                            state_transposes(last)
                        if m == 3 and r < NBLK:
                            xn_transposes(q)
                        if m == 4 and r >= 3:
                            rank_tokens(routing)
                    if 2 <= r < NBLK + 2:
                        ffn_out(ffn, 0)
                    if 1 <= r <= NBLK:
                        xn2_transposes(last)
                    if 2 <= r < NBLK + 2:
                        ffn_out(ffn, 1)
                    if r < NBLK:
                        gvd(q)

                pe.wait_ge(mod_rows, 1)
                pe.wait_ge(consts_in, 64)
                pe.wait_ge(w_lo, 3)
                body(step, pe)
                pe.wait_ge(slots_r, NBLK)
                pe.matmul(total, ones[:], seen_b[:], start=True, stop=True).then_inc(total_mm, 1)
                pe.wait_ge(tabs, TABS)
                pe.transpose(tp[0][0:3, 0:P], tcol2[:], ident).then_inc(tab_t, 1)

            @block.scalar
            def _(act):
                act.wait_ge(mod_in, 32)
                act.activation(ct_sig[:], ct[:], ACT.Sigmoid).then_inc(cond_sig, 1)
                act.wait_ge(consts_in, 64)
                act.wait_ge(raw_in[0], 16)
                for k in range(KD):
                    i = act.activation(gvd_hi[:, k, :], gvd_raw[:, k, :], ACT.Identity, scale=vec[:, V_MIX + k:V_MIX + k + 1])
                i.then_inc(w_hi, 1)
                act.wait_ge(raw_in[1], 16)
                for k in range(KD):
                    i = act.activation(gu_hi[:, k, :], gu_raw[:, k, :], ACT.Identity, scale=vec[:, V_FFN + k:V_FFN + k + 1])
                i.then_inc(w_hi, 1)
                act.wait_ge(raw_in[2], 16)
                act.activation(out_hi[:].rearrange("p k n -> p (k n)"),
                               out_raw[:].rearrange("p a i d -> p (a i d)")[:, 0:KFA * D], ACT.Identity).then_inc(w_hi, 1)

                def square_sums(q, squares, src, ready, count, dst, done):
                    act.wait_ge(ready, count)
                    for i in range(TPB):
                        a = act.activation(squares[:, i, :], src[:, i, :], ACT.Square, accum_out=dst[:, i:i + 1])
                    a.then_inc(done, 1)

                def front(q):
                    if q.n >= 1:
                        act.wait_ge(ms_r, q.v)
                    square_sums(q, squares, h_sb[:, q.par], h_ready, q.v + 1, ssq, ssq_r)

                def xn_hi(q):
                    for c in range(KD):
                        act.wait_ge(xnT_t, q.v * KD + c + 1)
                        if c == 0 and q.n >= 1:
                            act.wait_ge(gvd_mm, q.v * 3 * KD)
                        act.activation(xnT_hi[:, c, :], tp[c], ACT.Copy).then_inc(xnT_h, 1)

                def gvd_activations(q):
                    for n in range(3 * KD):
                        kind, c = n % 3, n // 3
                        act.wait_ge(gvd_mm, q.v * 3 * KD + n + 1)
                        if q.n >= 1 and kind == 0:
                            act.wait_ge(sT_t, q.v * 2)
                        if q.n >= 1 and kind == 1:
                            act.wait_ge(scanned, (q.v - 1) * KD + c + 1)
                        dst = (sg_sb, tv_sb, dec_sb)[kind]
                        act.activation(dst[:, c, :], bank("gvd", q, n), (ACT.Sigmoid, ACT.Tanh, ACT.Sigmoid)[kind],
                                       bias=vec[:, V_BIAS + kind * KD + c:V_BIAS + kind * KD + c + 1]).then_inc(gvd_act, 1)

                def middle(q):
                    if q.n >= 1:
                        act.wait_ge(ms2_r, q.v)
                    square_sums(q, squares2, xa_sb[:, q.par], xa_r, 2 * q.v + 2, ssq2, ssq2_r)

                def xn2_hi(q):
                    for c in range(KD):
                        act.wait_ge(xn2T_t, q.v * KD + c + 1)
                        if c == 0 and q.n >= 1:
                            act.wait_ge(gu_mm, q.v * 2 * KFA)
                        act.activation(xn2T_hi[:, c, :], tp[c], ACT.Copy).then_inc(xn2T_h, 1)

                def gate_sigmoid(q, m):
                    act.wait_ge(gu_mm, q.v * 2 * KFA + 2 * m + 1)
                    if q.n >= 1 or m >= 2:
                        act.wait_ge(gg_r, q.v * KFA + m - 1)
                    act.activation(sig_sb[:, m % 2, :], bank("gu", q, 2 * m), ACT.Sigmoid).then_inc(sig_r, 1)

                def hidden_hi(q, m):
                    act.wait_ge(hf_r, q.v * KFA + m + 1)
                    if m == 0 and q.n >= 1:
                        act.wait_ge(out_mm, q.v * 2)
                    act.activation(hid_hi[:, m, :], hf_sb[:, m % 2, :], ACT.Copy).then_inc(hid_h, 1)

                def h2_copy(q):
                    for c in range(KD):
                        act.wait_ge(hT_t, q.v * KD + c + 1)
                        if c == 0 and q.n >= 1:
                            act.wait_ge(logit_mm, q.v)
                        act.activation(hT_sb[:, c, :], tp[c], ACT.Copy).then_inc(hT_c, 1)

                def router_exp(q):
                    act.wait_ge(z_r, q.v + 1)
                    act.activation(ee[:], zz[:], ACT.Exp).then_inc(exp_r, 1)

                def step(r, turn):
                    q = Block512(r, turn)
                    last, routing, ffn = q.near(-1), q.near(-3), q.near(-2)
                    if r < NBLK and r < 2:
                        front(q)
                    for m in range(KFA):
                        if 2 <= r < NBLK + 2:
                            gate_sigmoid(ffn, m)
                        if m == 1 and r >= 3:
                            h2_copy(routing)
                        if 2 <= r < NBLK + 2 and m >= 1:
                            hidden_hi(ffn, m - 1)
                        if m == 2 and r >= 3:
                            router_exp(routing)
                        if m == 1 and 2 <= r < NBLK:
                            front(q)
                        if m == 3 and 1 <= r <= NBLK:
                            middle(last)
                        if m == 4 and r < NBLK:
                            xn_hi(q)
                    if 2 <= r < NBLK + 2:
                        hidden_hi(ffn, KFA - 1)
                    if 1 <= r <= NBLK:
                        xn2_hi(last)
                    if r < NBLK:
                        gvd_activations(q)

                body(step, act)

            @block.vector
            def _(v):
                def chain(counter, at_value):
                    n = [0]

                    def link(i):
                        n[0] += 1
                        i.then_inc(counter, 1)
                        v.wait_ge(counter, at_value + n[0])
                    return link

                v.memset(ones[:], 1.0)
                v.memset(ones_f[:], 1.0)
                v.memset(minus_half[:], -0.5)
                v.memset(carry[:], 0.0)
                v.memset(seen[:], 0.0)
                v.memset(seen_b[:], 0.0)
                v.memset(pad_rows[:], 0.0).then_inc(small_ready, 1)
                v.wait_ge(consts_in, 64)
                v.tensor_copy(tri[:], cn[:, C_TRI:C_TRI + P])
                v.tensor_copy(tok_f[:].rearrange("p b i -> p (b i)"), cn[:, C_TOK:C_TOK + B * TPB]).then_inc(small_ready, 1)
                v.wait_ge(small_ready, 2)
                v.tensor_copy(pad_rows[:, ROW - 1:ROW], cn[:, C_PAD:C_PAD + 1]).then_inc(small_ready, 1)
                v.wait_ge(cond_sig, 1)
                v.tensor_tensor(ct_sig[:], ct[:], ct_sig[:], ALU.mult).then_inc(cond_act, 1)
                v.wait_ge(cond_act, 1)
                v.tensor_copy(ct_rep[:], ct_sig[:].rearrange("p k b -> p (k b)").unsqueeze(2).to_broadcast([P, KD * B, P]))\
                    .then_inc(cond_rep, 1)
                v.wait_ge(mod_mm, 6)
                for b in range(B):
                    m = [ps[:, 3 * b + n // 2, (n % 2) * D:(n % 2 + 1) * D] for n in range(6)]
                    v.tensor_copy(mod[:, b, M_S1, :], m[0])
                    v.tensor_scalar(mod[:, b, M_A1, :], m[1], 1.0, None, ALU.add)
                    v.tensor_copy(g_raw[:, (2 * b) * D:(2 * b + 1) * D], m[2])
                    v.tensor_copy(mod[:, b, M_S2, :], m[3])
                    v.tensor_scalar(mod[:, b, M_A2, :], m[4], 1.0, None, ALU.add)
                    i = v.tensor_copy(g_raw[:, (2 * b + 1) * D:(2 * b + 2) * D], m[5])
                i.then_inc(mod_rows, 1)
                gf = gates[:].rearrange("p b g d -> p (b g d)")
                v.wait_ge(mod_rows, 1)
                v.scalar_tensor_tensor(gf, g_raw[:], -1.0, g_raw[:], ALU.mult, ALU.max).then_inc(mod_rows, 1)
                v.tensor_scalar(g_raw[:], g_raw[:], 0.0, 2.0, ALU.is_ge, ALU.mult).then_inc(mod_rows, 1)
                v.wait_ge(mod_rows, 3)
                v.tensor_scalar(gf, gf, 0.25, None, ALU.max).then_inc(mod_rows, 1)
                v.wait_ge(mod_rows, 4)
                v.scalar_tensor_tensor(gf, g_raw[:], -1.0, gf, ALU.add, ALU.mult).then_inc(mod_rows, 1)
                v.wait_ge(mod_rows, 5)
                for b in range(B):
                    i = v.tensor_tensor(mod[:, b, M_GBB, :], gates[:, b, 1, :], bias_row[:], ALU.mult)
                i.then_inc(mod_rows, 1)

                def row(b, m):
                    return mod[:, b, m, :].unsqueeze(1).to_broadcast([P, TPB, D])

                def front(q):
                    v.wait_ge(x_in, (q.v + 1) * 16)
                    for i in range(TPB):
                        v.bn_stats(stats[:, i, :], x_sb[:, i, :]).then_inc(bn, 1)
                    v.wait_ge(bn, (q.v + 1) * TPB)
                    v.memset(turn_mark[:], 0.0)
                    for i in range(TPB):
                        v.bn_aggr(mv[:, i, :], stats[:, i, :]).then_inc(aggr, 1)
                    v.wait_ge(aggr, (q.v + 1) * TPB)
                    v.tensor_scalar(ve[:], mv[:, :, 1], EPS_LN, None, ALU.add).then_inc(var_eps, 1)
                    v.wait_ge(rstd_r, q.v + 1)
                    for i in range(TPB):
                        a = v.tensor_scalar(h_sb[:, q.par, i, :], x_sb[:, i, :], mv[:, i, 0:1], rstd[:, i:i + 1],
                                            ALU.subtract, ALU.mult)
                    a.then_inc(xh, 1)
                    v.wait_ge(xh, q.v + 1)
                    v.tensor_tensor(h_sb[:, q.par], h_sb[:, q.par], row(q.par, M_A1), ALU.mult).then_inc(h_scaled, 1)

                def mean_square(q, src, ready, dst, done):
                    v.wait_ge(ready, q.v + 1)
                    v.tensor_scalar(dst[:], src[:], 1.0 / D, EPS_RMS, ALU.mult, ALU.add).then_inc(done, 1)

                def xn(q):
                    mean_square(q, ssq, ssq_r, ms, ms_r)
                    v.wait_ge(rms_r, q.v + 1)
                    if q.n >= 2:
                        v.wait_ge(xn2T_t, (q.v - 1) * KD)
                    for i in range(TPB):
                        a = v.tensor_scalar(xn_sb[:, i, :], h_sb[:, q.par, i, :], rms[:, i:i + 1], None, ALU.mult)
                    a.then_inc(xn_r, 1)

                def xn_lo(q):
                    for c in range(KD):
                        v.wait_ge(xnT_h, q.v * KD + c + 1)
                        v.tensor_tensor(xnT_lo[:, c, :], tp[c], f32(xnT_hi[:, c, :]), ALU.subtract).then_inc(xnT_l, 1)

                def scan(q):
                    for c in range(KD):
                        v.wait_ge(gvd_act, q.v * 3 * KD + 3 * c + 3)
                        v.tensor_scalar(dec_sb[:, c, :], dec_sb[:, c, :], 0.998, 0.001, ALU.mult, ALU.add).then_inc(dec_r, 1)
                        v.wait_ge(dec_r, q.v * KD + c + 1)
                        v.wait_ge(xs_r, q.v * KD + c + 1)
                        if q.n >= 1:
                            v.wait_ge(carried, q.v * KD)
                        v.tensor_tensor_scan(sg_sb[:, c, :], dec_sb[:, c, :], tv_sb[:, c, :], carry[:, q.par, c:c + 1],
                                             ALU.mult, ALU.add).then_inc(scanned, 1)
                    for c in range(KD):
                        v.wait_ge(scanned, q.v * KD + c + 1)
                        v.tensor_copy(carry[:, q.par, c:c + 1], sg_sb[:, c, BLK - 1:BLK]).then_inc(carried, 1)

                def add_state(q):
                    for u in range(2):
                        v.wait_ge(sT_t, q.v * 2 + u + 1)
                        t = slice(2 * u, 2 * u + 2)
                        v.tensor_tensor(xa_sb[:, q.par, t, :], tp[u].rearrange("p (i d) -> p i d", d=D),
                                        h_sb[:, q.par, t, :], ALU.add).then_inc(xa_r, 1)

                def xn2(q):
                    mean_square(q, ssq2, ssq2_r, ms2, ms2_r)
                    v.wait_ge(rms2_r, q.v + 1)
                    v.wait_ge(xnT_t, (q.v + 2) * KD if q.n + 1 < NBLK else NBLK * KD)
                    for i in range(TPB):
                        a = v.tensor_scalar(xn_sb[:, i, :], xa_sb[:, q.par, i, :], rms2[:, i:i + 1], None, ALU.mult)
                    a.then_inc(xn2_r, 1)

                def xn2_lo(q):
                    for c in range(KD):
                        v.wait_ge(xn2T_h, q.v * KD + c + 1)
                        v.tensor_tensor(xn2T_lo[:, c, :], tp[c], f32(xn2T_hi[:, c, :]), ALU.subtract).then_inc(xn2T_l, 1)

                def hidden(q, m):
                    v.wait_ge(sig_r, q.v * KFA + m + 1)
                    v.tensor_tensor(gg_sb[:, m % 2, :], bank("gu", q, 2 * m), sig_sb[:, m % 2, :], ALU.mult).then_inc(gg_r, 1)
                    v.wait_ge(gu_mm, q.v * 2 * KFA + 2 * m + 2)
                    if q.n >= 1 or m >= 2:
                        v.wait_ge(hid_l, q.v * KFA + m - 1)
                    v.wait_ge(gg_r, q.v * KFA + m + 1)
                    v.tensor_tensor(hf_sb[:, m % 2, :], bank("gu", q, 2 * m + 1), gg_sb[:, m % 2, :], ALU.mult).then_inc(hf_r, 1)

                def add_ffn(q):
                    if q.n >= 1:
                        v.wait_ge(x1_r, q.v)
                    for u in range(2):
                        v.wait_ge(out_mm, q.v * 2 + u + 1)
                        t = slice(2 * u, 2 * u + 2)
                        v.tensor_tensor(xo_sb[:, t, :], bank("out", q, u).rearrange("p (i d) -> p i d", d=D),
                                        xa_sb[:, q.par, t, :], ALU.add).then_inc(xo_r, 1)

                def gate_xo(q):
                    v.wait_ge(xo_r, (q.v + 1) * 2)
                    v.tensor_tensor(xo_sb[:], xo_sb[:], gates[:, q.par, 0, :].unsqueeze(1).to_broadcast([P, TPB, D]),
                                    ALU.mult).then_inc(xg_r, 1)

                def norm2(q):
                    v.wait_ge(x1_r, q.v + 1)
                    for i in range(TPB):
                        v.bn_stats(stats2[:, i, :], x_again[:, i, :]).then_inc(bn2, 1)
                    v.wait_ge(bn2, (q.v + 1) * TPB)
                    v.memset(turn_mark[:], 0.0)
                    for i in range(TPB):
                        v.bn_aggr(mv2[:, i, :], stats2[:, i, :]).then_inc(aggr2, 1)
                    v.wait_ge(aggr2, (q.v + 1) * TPB)
                    v.tensor_scalar(ve2[:], mv2[:, :, 1], EPS_LN, None, ALU.add).then_inc(var_eps2, 1)
                    v.wait_ge(rstd2_r, q.v + 1)
                    if q.n >= 1:
                        v.wait_ge(scattered[q.par], q.half * 32 * TPB + 16)
                    for i in range(TPB):
                        a = v.tensor_scalar(rows[:, q.par, i, 0:D], x_again[:, i, :], mv2[:, i, 0:1], rstd2[:, i:i + 1],
                                            ALU.subtract, ALU.mult)
                    a.then_inc(xh2, 1)
                    v.wait_ge(xh2, q.v + 1)
                    r = rows[:, q.par, :, 0:D]
                    v.tensor_tensor(r, r, row(q.par, M_A2), ALU.mult).then_inc(h2_scaled, 1)

                ROUTE = 11

                def top2(q):
                    v.wait_ge(logit_mm, q.v + 1)
                    link = chain(route, q.v * ROUTE)
                    link(v.tensor_reduce(mx[:], logits, AX.X, ALU.max))
                    v.tensor_tensor(zz[:], logits, mx[:].unsqueeze(2).to_broadcast([P, TPB, E]), ALU.subtract).then_inc(z_r, 1)
                    v.wait_ge(exp_r, q.v + 1)
                    link(v.tensor_reduce(mx[:], ee[:], AX.X, ALU.add))
                    link(v.reciprocal(mx[:], mx[:]))
                    link(v.tensor_tensor(pp[:], ee[:], mx[:].unsqueeze(2).to_broadcast([P, TPB, E]), ALU.mult))
                    v.tensor_copy(rows[:, q.par, :, D + E], tok_f[:, q.par, :])
                    for i in range(TPB):
                        a = v.max(top[:, i, :], pp[:, i, :])
                    link(a)
                    v.tensor_scalar(tok_f[:, q.par, :], tok_f[:, q.par, :], float(BLK), None, ALU.add)
                    for i in range(TPB):
                        a = v.max_index(top_i[:, i, :], top[:, i, :], pp[:, i, :])
                    link(a)
                    link(v.tensor_copy(top_f[:], top_i[:, :, 0:2]))
                    iota = cn[:, C_IOTA:C_IOTA + TPB * E].rearrange("p (i e) -> p i e", e=E)
                    for k in range(2):
                        link(v.tensor_tensor(hot[:, k], iota, top_f[:, :, k:k + 1].to_broadcast([P, TPB, E]), ALU.is_equal))
                    link(v.tensor_tensor(chosen[:], hot[:, 0], hot[:, 1], ALU.add))
                    link(v.tensor_copy(chosen_b[:], chosen[:]))
                    v.tensor_tensor(rows[:, q.par, :, D:D + E], chosen[:], pp[:], ALU.mult).then_inc(chosen_r, 1)

                SLOT = 5

                def slots(q):
                    v.wait_ge(rank_mm, q.v + 1)
                    link = chain(slot_steps, q.v * SLOT)
                    link(v.tensor_tensor(pos[:], ranks, cn[:, C_OFF:C_OFF + E].unsqueeze(1).to_broadcast([P, TPB, E]), ALU.add))
                    for k in range(2):
                        i = v.tensor_tensor(pos_k[:, k], pos[:], hot[:, k], ALU.mult)
                    link(i)
                    link(v.tensor_reduce(slot_f[:], pos_k[:], AX.X, ALU.add))
                    if q.n >= 1:
                        v.wait_ge(scattered[q.par], q.half * 32 * TPB + 16)
                    v.tensor_copy(slot_i[:, q.par], slot_f[:])
                    link(v.tensor_reduce(seen_add[:], chosen[:].rearrange("p i e -> p e i"), AX.X, ALU.add))
                    link(v.tensor_tensor(seen[:], seen[:], seen_add[:], ALU.add))
                    v.tensor_copy(seen_b[:], seen[:]).then_inc(slots_r, 1)

                def step(r, turn):
                    q = Block512(r, turn)
                    last, routing, ffn = q.near(-1), q.near(-3), q.near(-2)
                    if r >= 3:
                        gate_xo(routing)
                    if r >= 3:
                        norm2(routing)
                    if r < NBLK:
                        front(q)
                    for m in range(KFA):
                        if 2 <= r < NBLK + 2:
                            hidden(ffn, m)
                        if m == 1 and r >= 3:
                            top2(routing)
                        if m == 1 and r < NBLK:
                            xn(q)
                        if m == 3 and 1 <= r <= NBLK:
                            add_state(last)
                        if m == 4 and r < NBLK:
                            xn_lo(q)
                        if m == 4 and 1 <= r <= NBLK:
                            xn2(last)
                        if m == 5 and r >= 3:
                            slots(routing)
                    if 1 <= r <= NBLK:
                        xn2_lo(last)
                    if 2 <= r < NBLK + 2:
                        add_ffn(ffn)
                    if r < NBLK:
                        scan(q)

                for k in range(KD):
                    if k == 0:
                        v.wait_ge(w_hi, 1)
                    i = v.scalar_tensor_tensor(gvd_lo[:, k, :], gvd_raw[:, k, :], vec[:, V_MIX + k:V_MIX + k + 1],
                                               f32(gvd_hi[:, k, :]), ALU.mult, ALU.subtract)
                i.then_inc(w_lo, 1)
                v.wait_ge(w_hi, 2)
                for k in range(KD):
                    i = v.scalar_tensor_tensor(gu_lo[:, k, :], gu_raw[:, k, :], vec[:, V_FFN + k:V_FFN + k + 1],
                                               f32(gu_hi[:, k, :]), ALU.mult, ALU.subtract)
                i.then_inc(w_lo, 1)
                v.wait_ge(w_hi, 3)
                v.tensor_tensor(out_lo[:].rearrange("p k n -> p (k n)"),
                                out_raw[:].rearrange("p a i d -> p (a i d)")[:, 0:KFA * D],
                                f32(out_hi[:].rearrange("p k n -> p (k n)")), ALU.subtract).then_inc(w_lo, 1)
                v.wait_ge(mod_rows, 6)
                body(step, v)

                v.wait_ge(total_mm, 1)
                link = chain(tabs, 0)
                link(v.tensor_copy(counts[:], total))
                v.tensor_copy(counts_i[:], counts[:])
                link(v.tensor_scalar(tiles_i[:], counts[:], float(P - 1), None, ALU.add))
                link(v.tensor_scalar(tiles_i[:], tiles_i[:], P.bit_length() - 1, None, ALU.logical_shift_right))
                link(v.tensor_copy(tiles_f[:], tiles_i[:]))
                v.tensor_tensor_scan(tiles_end[:], ones_f[:], tiles_f[:], 0.0, ALU.mult, ALU.add)
                link(v.tensor_scalar(step_e[:], tiles_f[:], -float(P), float(REGION), ALU.mult, ALU.add))
                link(v.tensor_scalar(passed[:], tiles_end[:], cn[:, C_TILE:C_TILE + 1], None, ALU.is_le))
                v.tensor_reduce(tcol[:, 0:1], passed[:], AX.X, ALU.add)
                link(v.tensor_tensor(jump[:], passed[:], step_e[:], ALU.mult))
                link(v.tensor_reduce(tcol[:, 1:2], jump[:], AX.X, ALU.add))
                v.tensor_scalar(tcol2[:, 0:1], tcol[:, 0:1], float(E - 1), None, ALU.min)
                v.tensor_scalar(tcol2[:, 2:3], tcol[:, 0:1], float(RES), 48.0 * (E - RES), ALU.is_ge, ALU.mult)
                link(v.scalar_tensor_tensor(tcol[:, 1:2], cn[:, C_TILE:C_TILE + 1], float(P), tcol[:, 1:2],
                                            ALU.mult, ALU.add))
                v.tensor_scalar(tcol2[:, 2:3], tcol2[:, 2:3], 48.0 * RES, None, ALU.add)
                link(v.tensor_scalar(tcol2[:, 1:2], tcol[:, 1:2], float(E * REGION), None, ALU.min))
                v.wait_ge(tab_t, 1)
                v.tensor_copy(tab[0:3, :], tp[0][0:3, 0:P])

            @block.gpsimd
            def _(g):
                def power(dst, src):
                    return g.tensor_tensor(dst[:], src[:], minus_half[:], ALU.pow)

                def row(b, m):
                    return mod[:, b, m, :].unsqueeze(1).to_broadcast([P, TPB, D])

                def front(q):
                    g.wait_ge(var_eps, q.v + 1)
                    power(rstd, ve).then_inc(rstd_r, 1)
                    g.wait_ge(h_scaled, q.v + 1)
                    g.tensor_tensor(h_sb[:, q.par], h_sb[:, q.par], row(q.par, M_S1), ALU.add).then_inc(h_ready, 1)

                def rms1(q):
                    g.wait_ge(ms_r, q.v + 1)
                    power(rms, ms).then_inc(rms_r, 1)

                def rms_2(q):
                    g.wait_ge(ms2_r, q.v + 1)
                    power(rms2, ms2).then_inc(rms2_r, 1)

                def gated_value(q):
                    for c in range(KD):
                        g.wait_ge(gvd_act, q.v * 3 * KD + 3 * c + 2)
                        g.tensor_tensor(tv_sb[:, c, :], sg_sb[:, c, :], tv_sb[:, c, :], ALU.mult).then_inc(xs_r, 1)

                def hidden_lo(q, m):
                    g.wait_ge(hid_h, q.v * KFA + m + 1)
                    g.tensor_tensor(hid_lo[:, m, :], hf_sb[:, m % 2, :], f32(hid_hi[:, m, :]), ALU.subtract).then_inc(hid_l, 1)

                def late(q):
                    g.wait_ge(xg_r, q.v + 1)
                    g.wait_ge(x_again_in, (q.v + 1) * 16)
                    g.tensor_tensor(x_again[:], x_again[:], xo_sb[:], ALU.add).then_inc(x1_r, 1)
                    g.wait_ge(var_eps2, q.v + 1)
                    power(rstd2, ve2).then_inc(rstd2_r, 1)
                    g.wait_ge(h2_scaled, q.v + 1)
                    r = rows[:, q.par, :, 0:D]
                    g.tensor_tensor(r, r, row(q.par, M_S2), ALU.add).then_inc(h2_ready, 1)
                    g.wait_ge(x1_r, q.v + 1)
                    g.tensor_tensor(x_again[:], x_again[:], row(q.par, M_GBB), ALU.add).then_inc(base_r, 1)

                def scatter(q):
                    g.wait_ge(slots_r, q.v + 1)
                    mark(g)
                    for i in range(TPB):
                        for k in range(2):
                            g.indirect_dma_start(routed, bass.IndirectOffsetOnAxis(ap=slot_i[:, q.par, k, i:i + 1], axis=0),
                                                 rows[:, q.par, i, :], None)\
                                .then_inc(scattered[q.par], 16)

                def step(r, turn):
                    q = Block512(r, turn)
                    last, routing, ffn = q.near(-1), q.near(-3), q.near(-2)
                    if r >= 3:
                        late(routing)
                    if r < NBLK:
                        front(q)
                    for m in range(KFA):
                        if 2 <= r < NBLK + 2:
                            hidden_lo(ffn, m)
                        if m == 0 and r < NBLK:
                            rms1(q)
                        if m == 3 and 1 <= r <= NBLK:
                            rms_2(last)
                    if r >= 3:
                        scatter(routing)
                    if r < NBLK:
                        gated_value(q)

                g.wait_ge(small_ready, 3)
                g.dma_start(routed[E * REGION:ROWS, :], pad_rows[:]).then_inc(scattered[0], 16)
                g.dma_start(out[T:T + P, :], pad_rows[:, 0:D]).then_inc(scattered[1], 16)
                g.wait_ge(mod_rows, 6)
                body(step, g)
                for b in range(2):
                    g.wait_ge(scattered[b], NBLK // 2 * 32 * TPB + 16)

        rows_in = [sem("rows_in0"), sem("rows_in1")]
        xT_t, xT_c, a_mm, b_mm, gelu_r, hid_r = (sem(n) for n in ("xT_t", "xT_c", "a_mm", "b_mm", "gelu_r", "hid_r"))
        hidT_t, hidT_c0, hidT_c1, y_mm, y_r = (sem(n) for n in ("hidT_t", "hidT_c0", "hidT_c1", "y_mm", "y_r"))
        gate_steps, gates_r, y_sum, added = sem("gate_steps"), sem("gates_r"), sem("y_sum"), sem("added")
        TAB_EXPERT, TAB_ROW, TAB_LOADED = 0, 1, 2
        PS_Y, PS_HT, PS_XT = 4, 5, 7
        y_ps, xT_ps = ps[:, PS_Y, 0:D], ps[:, PS_XT, 0:KD * P]

        class Tile:

            def __init__(self, n, turn=None):
                self.n, self.turn, self.par = n, turn, n % 2
                self.v = n if turn is None else turn * 2 + n
                self.half = n // 2 if turn is None else turn + n // 2

            def near(self, d):
                return Tile(self.n + d, self.turn)

        def tiles(engine, first, step, last):
            first(Tile(0))
            step(Tile(1))
            step(Tile(2))
            with engine.Fori(0, (MOE_TILES - 3) // 2, 1) as turn:
                step(Tile(3, turn))
                step(Tile(4, turn))
            last(Tile(MOE_TILES - 1))

        assert (MOE_TILES - 3) % 2 == 0

        def entry(eng, which, t, top):
            return eng.value_load(tab[which:which + 1, bass.ds(t.v, 1)], min_val=0, max_val=top)

        with nc.Block() as block:

            @block.sync
            def _(sp):
                def load_rows(t):
                    row = entry(sp, TAB_ROW, t, E * REGION)
                    if t.n >= 2:
                        sp.wait_ge(gates_r, t.v - 1)
                        sp.wait_ge(xT_t, t.v - 1)
                    sp.dma_start(x_moe[:, t.par, :], routed[bass.ds(row, P), :]).then_inc(rows_in[t.par], 16)

                for e in range(E):
                    n = sp.value_load(counts_i[0:1, e:e + 1], min_val=0, max_val=T)
                    sp.dma_start(routed[bass.ds(n + e * REGION, P), :], pad_rows[:]).then_inc(pads_out, 16)
                sp.wait_ge(pads_out, E * 16)
                load_rows(Tile(0))
                load_rows(Tile(1))
                for e in range(RES, E):
                    load_expert(sp, e)
                load_rows(Tile(2))
                load_rows(Tile(3))
                with sp.Fori(0, (MOE_TILES - 3) // 2, 1) as turn:
                    load_rows(Tile(4, turn))
                    load_rows(Tile(5, turn))

            @block.tensor
            def _(pe):
                def x_transposes(t):
                    pe.wait_ge(rows_in[t.par], t.half * 16 + 16)
                    if t.n >= 1:
                        pe.wait_ge(xT_c, t.v)
                    for k in range(KD):
                        mm = pe.transpose(xT_ps[:, k * P:(k + 1) * P], x_moe[:, t.par, k * P:(k + 1) * P], ident)
                    mm.then_inc(xT_t, 1)

                def first_products(t):
                    e = entry(pe, TAB_EXPERT, t, E - 1)
                    loaded = entry(pe, TAB_LOADED, t, 48 * E)
                    pe.wait_ge(experts_in, loaded)
                    pe.wait_ge(xT_c, t.v + 1)
                    for n in range(4):
                        if t.n >= 1 and n == 0:
                            pe.wait_ge(gelu_r, t.v)
                        if t.n >= 1 and n == 2:
                            pe.wait_ge(hid_r, t.v)
                        for k in range(KD):
                            mm = pe.matmul(ps[:, n, 0:FH], xT_moe[:, t.par, k, :],
                                           experts[:, bass.ds(e * EXPW + (k * 2 * F + n * FH), FH)],
                                           start=(k == 0), stop=(k == KD - 1))
                        if n % 2:
                            mm.then_inc((a_mm, b_mm)[n // 2], 1)

                def hid_transposes(t):
                    pe.wait_ge(hid_r, t.v + 1)
                    if t.n >= 1:
                        pe.wait_ge(hidT_c0, t.v)
                        pe.wait_ge(hidT_c1, t.v)
                    for k in range(KF):
                        m = P if k < KF - 1 else F_LAST
                        mm = pe.transpose(ps[0:m, PS_HT + k // 4, k % 4 * P:(k % 4 + 1) * P],
                                          hid_moe[:, k * P:k * P + m], ident)
                    mm.then_inc(hidT_t, 1)

                def second_product(t):
                    e = entry(pe, TAB_EXPERT, t, E - 1)
                    pe.wait_ge(hidT_c0, t.v + 1)
                    pe.wait_ge(hidT_c1, t.v + 1)
                    if t.n >= 1:
                        pe.wait_ge(y_r, t.v)
                    for k in range(KF):
                        m = P if k < KF - 1 else F_LAST
                        mm = pe.matmul(y_ps, hidT_moe[0:m, k, :],
                                       experts[0:m, bass.ds(e * EXPW + (KD * 2 * F + k * D), D)],
                                       start=(k == 0), stop=(k == KF - 1))
                    mm.then_inc(y_mm, 1)

                def first(t):
                    x_transposes(t)
                    first_products(t)
                    x_transposes(t.near(1))
                    hid_transposes(t)

                def step(t):
                    first_products(t)
                    second_product(t.near(-1))
                    x_transposes(t.near(1))
                    hid_transposes(t)

                tiles(pe, first, step, second_product)

            @block.scalar
            def _(act):
                def copy_xT(t):
                    act.wait_ge(xT_t, t.v + 1)
                    if t.n >= 2:
                        act.wait_ge(b_mm, t.v - 1)
                    act.activation(xT_moe[:, t.par].rearrange("p k n -> p (k n)"), xT_ps, ACT.Copy).then_inc(xT_c, 1)

                def gelu(t):
                    act.wait_ge(a_mm, t.v + 1)
                    if t.n >= 1:
                        act.wait_ge(hid_r, t.v)
                    act.activation(gelu_moe[:], ps[:, 0:2, 0:FH], ACT.Gelu).then_inc(gelu_r, 1)

                def copy_hidT(t):
                    act.wait_ge(hidT_t, t.v + 1)
                    if t.n >= 1:
                        act.wait_ge(y_mm, t.v)
                    act.activation(hidT_moe[:, 0:4, :].rearrange("p k n -> p (k n)"), ps[:, PS_HT, :], ACT.Copy)\
                        .then_inc(hidT_c0, 1)

                def first(t):
                    copy_xT(t)
                    step(t)

                def step(t):
                    gelu(t)
                    copy_xT(t.near(1))
                    copy_hidT(t)

                tiles(act, first, step, lambda t: None)

            @block.vector
            def _(v):
                def take_gates(t):
                    e = entry(v, TAB_EXPERT, t, E - 1)
                    g, tok = gate_moe[:, t.par, :], x_moe[:, t.par, D + E:D + E + 1]
                    v.wait_ge(rows_in[t.par], t.half * 16 + 16)
                    v.tensor_scalar(g[:, 1:2], tok, float(S), None, ALU.is_ge)
                    v.tensor_copy(g[:, 0:1], x_moe[:, t.par, bass.ds(e + D, 1)]).then_inc(gate_steps, 1)
                    v.wait_ge(gate_steps, t.v * 2 + 1)
                    v.tensor_tensor(g[:, 2:3], g[:, 0:1], g[:, 1:2], ALU.mult).then_inc(gate_steps, 1)
                    v.wait_ge(gate_steps, t.v * 2 + 2)
                    v.tensor_tensor(g[:, 3:4], g[:, 0:1], g[:, 2:3], ALU.subtract)
                    if t.n >= 2:
                        v.wait_ge(added, (t.v - 1) * 16)
                    v.tensor_copy(tok_moe[:, t.par, :], tok).then_inc(gates_r, 1)

                def multiply(t):
                    v.wait_ge(gelu_r, t.v + 1)
                    v.wait_ge(b_mm, t.v + 1)
                    if t.n >= 1:
                        v.wait_ge(hidT_t, t.v)
                    v.tensor_tensor(hid_moe[:].rearrange("p (h n) -> p h n", h=2), ps[:, 2:4, 0:FH], gelu_moe[:],
                                    ALU.mult).then_inc(hid_r, 1)

                def gate_y(t):
                    v.wait_ge(y_mm, t.v + 1)
                    v.wait_ge(gates_r, t.v + 1)
                    if t.n >= 2:
                        v.wait_ge(added, (t.v - 1) * 16)
                    for b in range(B):
                        i = v.scalar_tensor_tensor(y_moe[:, t.par, b, :], y_ps, gate_moe[:, t.par, 3 - b:4 - b],
                                                   gates[:, b, 1, :], ALU.mult, ALU.mult)
                    i.then_inc(y_r, 1)

                def copy_hidT(t):
                    v.wait_ge(hidT_t, t.v + 1)
                    v.tensor_copy(hidT_moe[:, 4, :], ps[:, PS_HT + 1, 0:P])
                    v.tensor_copy(hidT_moe[0:F_LAST, 5, :], ps[0:F_LAST, PS_HT + 1, P:2 * P]).then_inc(hidT_c1, 1)

                def first(t):
                    take_gates(t)
                    multiply(t)
                    copy_hidT(t)

                def step(t):
                    take_gates(t)
                    multiply(t)
                    gate_y(t.near(-1))
                    copy_hidT(t)

                tiles(v, first, step, gate_y)

            @block.gpsimd
            def _(g):
                def add_rows(t):
                    g.wait_ge(y_r, t.v + 1)
                    g.tensor_tensor(y_moe[:, t.par, 0, :], y_moe[:, t.par, 0, :], y_moe[:, t.par, 1, :], ALU.add)\
                        .then_inc(y_sum, 1)
                    g.wait_ge(y_sum, t.v + 1)
                    if t.n >= 1:
                        g.wait_ge(added, t.v * 16)
                    mark(g)
                    g.indirect_dma_start(out, bass.IndirectOffsetOnAxis(ap=tok_moe[:, t.par, :], axis=0),
                                         y_moe[:, t.par, 0, :], None,
                                         compute_op=ALU.add).then_inc(added, 16)

                tiles(g, add_rows, add_rows, lambda t: None)
                g.wait_ge(added, MOE_TILES * 16)


def kernel(**inputs):
    import concourse.bacc as bacc
    from concourse.bass_utils import run_bass_kernel_spmd

    a = {k: np.asarray(v) for k, v in inputs.items()}
    col = lambda v: v.reshape(-1, P).T
    arrays = {
        "x": a["L0_attn_x"],
        "gvd_t": np.concatenate([a["L0_attn_Wg"].T, a["L0_attn_Wv"].T, a["L0_attn_Wd"].T], axis=1),
        "gu_t": np.concatenate([a["L0_attn_W_gate"].T, a["L0_attn_W_up"].T], axis=1),
        "out_t": a["L0_attn_W_out"].T,
        "vecs": np.concatenate([col(a["L0_attn_bg"]), col(a["L0_attn_bv"]), col(a["L0_attn_bd"]),
                                col(a["L0_attn_rms_mix_w"]), col(a["L0_attn_rms_ffn_w"])], axis=1),
        "cond_t": a["L0_c"].T.reshape(KD, P, B).transpose(1, 0, 2),
        "wmod": a["L0_wmod"],
        "bias": a["L0_ffn_bias"],
        "router": a["L0_ffn_router_w"].reshape(KD, P, E).transpose(1, 0, 2),
        "w13": np.concatenate([a["L0_ffn_w1"], a["L0_ffn_v1"]], axis=2),
        "w2": a["L0_ffn_w2"],
        "consts": constants(),
    }
    arrays = {f"in_{k}": np.ascontiguousarray(v) for k, v in arrays.items()}
    nc = bacc.Bacc("TRN2", target_bir_lowering=False, num_devices=1)
    args = [nc.dram_tensor(k, v.shape, mybir.dt.from_np(v.dtype), kind="ExternalInput").ap() for k, v in arrays.items()]
    out = nc.dram_tensor("out_rows", (T + P, D), F32, kind="ExternalOutput").ap()
    adaln_moe_kernel(nc, *args, out)
    r = run_bass_kernel_spmd(nc, [arrays], core_ids=[0])
    return r.results[0]["out_rows"][:T].reshape(B, S, D)
```

```python
from contextlib import ExitStack

import numpy as np

import concourse.bass as bass
from concourse import mybir

P = 128
B, S, D = 2, 2048, 256
T = B * S
KD = D // P
BLK = 512
TPB = BLK // P
NBLK = T // BLK
FA = 768
KFA = FA // P
E, F, TOPK = 8, 704, 2
KF = -(-F // P)
F_LAST = F - (KF - 1) * P
FH = F // 2
ROW = D + E + 1
REGION = T + P
ROWS = E * REGION + P
MOE_TILES = (TOPK * T + E * (P - 1)) // P
PAD_TILE = MOE_TILES
W13, W2 = KD * 2 * F, KF * D
EXPW = W13 + W2
EPS_LN, EPS_RMS = 1e-5, 1e-6

ALU = mybir.AluOpType
ACT = mybir.ActivationFunctionType
AX = mybir.AxisListType
F32, F32R = mybir.dt.float32, mybir.dt.float32r
BF16, I32, U32 = mybir.dt.bfloat16, mybir.dt.int32, mybir.dt.uint32

C_ID, C_TRI, C_IOTA, C_OFF, C_TOK, C_PAD = 0, P, 2 * P, 2 * P + TPB * E, 2 * P + TPB * E + E, 2 * P + TPB * E + E + B * TPB
C_TILE = C_PAD + 1
C_ALT = C_TILE + 1
C_N = C_ALT + E
V_BIAS, V_MIX, V_FFN, V_N = 0, 3 * KD, 4 * KD, 5 * KD
TAB_EXPERT, TAB_ROW, TAB_BUF, TAB_SPLIT, TAB_LOAD, TAB_N = 0, 1, 2, 3, 4, 5
M_S1, M_A1, M_S2, M_A2, M_GBB, M_N = 0, 1, 2, 3, 4, 5


def constants():
    c = np.zeros((P, C_N), np.float32)
    p = np.arange(P)
    c[:, C_ID:C_ID + P] = np.eye(P)
    c[:, C_TRI:C_TRI + P] = p[:, None] < p[None, :]
    c[:, C_IOTA:C_IOTA + TPB * E] = np.tile(np.arange(E), TPB)
    c[:, C_OFF:C_OFF + E] = np.arange(E) * REGION
    for b in range(B):
        for i in range(TPB):
            c[:, C_TOK + b * TPB + i] = b * S + i * P + p
    c[:, C_PAD] = T + p
    c[:, C_TILE] = p
    c[:, C_ALT:C_ALT + E] = (-1) ** np.arange(E)
    return c


class Block512:

    def __init__(self, n, turn=None):
        self.n, self.turn = n, turn
        self.par = n % 2
        self.v = n if turn is None else turn * 2 + n
        self.half = n // 2 if turn is None else turn + n // 2

    def near(self, d):
        return Block512(self.n + d, self.turn)


def ring_plan(banks):
    order = []
    for r in range(NBLK + 2):
        if r < NBLK:
            order += [("gvd", r, k) for k in range(3 * KD)]
        if r >= 2:
            order += [("out", r - 2, k) for k in range(2)]
        if 1 <= r <= NBLK:
            order += [("gu", r - 1, k) for k in range(2 * KFA)]
    return {u: (n % banks, order[n - banks] if n >= banks else None) for n, u in enumerate(order)}


def adaln_moe_kernel(nc, x, gvd_t, gu_t, out_t, vecs, cond_t, wmod, bias, router, w13, w2, consts, out):
    RING = 5
    ring = ring_plan(RING)
    ctx = ExitStack()
    base = (nc.sbuf_base + 63) // 64 * 64
    place = [base]

    def at(name, shape, dt, offset=None):
        size = int(np.prod(shape[1:])) * (2 if dt == BF16 else 4)
        if offset is None:
            offset = place[0]
            place[0] = (offset + size + 31) // 32 * 32
        return nc.alloc_sbuf_tensor_at(name, shape, dt, offset=offset)

    with ctx:
        def sem(name):
            return ctx.enter_context(nc.semaphore(name))

        raw = at("raw", [P, 2 * EXPW], F32, base)
        keep = ((C_N + B * 2 * D + P + E + ROW + 2) * 4 + 6 * 32 + 31) // 32 * 32
        top_at = nc.sbuf_usable_end // 32 * 32 - keep
        place[0] = top_at
        cn = at("cn", [P, C_N], F32)
        gates = at("gates", [P, B, 2, D], F32)
        tab = at("tab", [P, P], I32)
        counts_i = at("counts_i", [P, E], I32)
        pad_rows = at("pad_rows", [P, ROW], F32)
        g_mark = at("g_mark", [P, 1], F32)
        place[0] = base + 2 * EXPW * 4
        w_moe_hi, w_moe_lo = (at(f"w_moe_{s}", [P, 2 * EXPW], F32R) for s in ("hi", "lo"))
        x_moe = at("x_moe", [P, 2, ROW], F32)
        xT_moe_hi, xT_moe_lo = (at(f"xT_moe_{s}", [P, 2, KD, P], F32R) for s in ("hi", "lo"))
        gelu_moe = at("gelu_moe", [P, 2, FH], F32)
        hid_moe = at("hid_moe", [P, KF * P], F32)
        hidT_hi, hidT_lo = (at(f"hidT_{s}", [P, KF, P], F32R) for s in ("hi", "lo"))
        y_moe = at("y_moe", [P, 2, 2, D], F32)
        gate_moe = at("gate_moe", [P, 2, 4], F32)
        tok_moe = at("tok_moe", [P, 2, 1], I32)
        assert place[0] <= top_at
        place[0] = base
        gvd_raw = at("gvd_raw", [P, KD, 3 * D], F32)
        assert place[0] <= base + EXPW * 4
        place[0] = base + EXPW * 4
        gvd_hi, gvd_lo = (at(f"gvd_{s}", [P, KD, 3 * D], F32R) for s in ("hi", "lo"))
        gu_hi, gu_lo = (at(f"gu_{s}", [P, KD, 2 * FA], F32R) for s in ("hi", "lo"))
        out_hi, out_lo = (at(f"out_{s}", [P, KFA, D], F32R) for s in ("hi", "lo"))
        hid_at = place[0]
        hid_hi, hid_lo = (at(f"hid_{s}", [P, KFA, BLK], F32R) for s in ("hi", "lo"))
        gu_raw = at("gu_raw", [P, KD, 2 * FA], F32, hid_at)
        wmod_sb = at("wmod_sb", [P, KD, 6 * D], F32, hid_at + KD * 2 * FA * 4)
        out_raw = at("out_raw", [P, KFA * D], F32, base + KD * 3 * D * 4)
        assert hid_at + 2 * KD * 2 * FA * 4 <= place[0]
        xnT_hi, xnT_lo = (at(f"xnT_{s}", [P, KD, BLK], F32R) for s in ("hi", "lo"))
        xn2T_hi, xn2T_lo = (at(f"xn2T_{s}", [P, KD, BLK], F32R) for s in ("hi", "lo"))
        mod = at("mod", [P, B, M_N, D], F32)
        x_sb = at("x_sb", [P, TPB, D], F32)
        x_again = at("x_again", [P, TPB, D], F32)
        h_sb = at("h_sb", [P, 2, TPB, D], F32)
        xa_sb = at("xa_sb", [P, 2, TPB, D], F32)
        g_raw = at("g_raw", [P, B * 2 * D], F32, place[0])
        xo_sb = at("xo_sb", [P, TPB, D], F32)
        xn_sb = at("xn_sb", [P, TPB, D], F32)
        sg_sb = at("sg_sb", [P, KD, BLK], F32)
        tv_sb = at("tv_sb", [P, KD, BLK], F32)
        dec_sb = at("dec_sb", [P, KD, BLK], F32)
        sig_sb = at("sig_sb", [P, 2, BLK], F32)
        gg_sb = at("gg_sb", [P, 2, BLK], F32)
        hf_sb = at("hf_sb", [P, 2, BLK], F32)
        rows = at("rows", [P, 2, TPB, ROW], F32)
        ct_rep = at("ct_rep", [P, KD * B, P], F32, place[0])
        hT_sb = at("hT_sb", [P, KD, BLK], F32)
        squares = at("squares", [P, TPB, D], F32)
        squares2 = at("squares2", [P, TPB, D], F32)
        vec = at("vec", [P, V_N], F32)
        rw_sb = at("rw_sb", [P, KD, E], F32)
        bias_row = at("bias_row", [P, D], F32)
        ct = at("ct", [P, KD, B], F32)
        ct_sig = at("ct_sig", [P, KD, B], F32)
        carry = at("carry", [P, B, KD], F32)
        tri = at("tri", [P, P], BF16)
        ones = at("ones", [P, P], BF16)
        ones_f = at("ones_f", [P, E], F32)
        minus_half = at("minus_half", [P, TPB], F32)
        eps_ln = at("eps_ln", [P, TPB], F32)
        eps_rms = at("eps_rms", [P, TPB], F32)
        stats = at("stats", [P, TPB, 6], F32)
        mv = at("mv", [P, TPB, 2], F32)
        ve = at("ve", [P, TPB], F32)
        rstd = at("rstd", [P, TPB], F32)
        ssq = at("ssq", [P, TPB], F32)
        ms = at("ms", [P, TPB], F32)
        rms = at("rms", [P, TPB], F32)
        ssq2 = at("ssq2", [P, TPB], F32)
        ms2 = at("ms2", [P, TPB], F32)
        rms2 = at("rms2", [P, TPB], F32)
        stats2 = at("stats2", [P, TPB, 6], F32)
        mv2 = at("mv2", [P, TPB, 2], F32)
        ve2 = at("ve2", [P, TPB], F32)
        rstd2 = at("rstd2", [P, TPB], F32)
        mx = at("mx", [P, TPB], F32)
        zz = at("zz", [P, TPB, E], F32)
        ee = at("ee", [P, TPB, E], F32)
        pp = at("pp", [P, TPB, E], F32)
        top = at("top", [P, TPB, E], F32)
        top_i = at("top_i", [P, TPB, E], U32)
        top_f = at("top_f", [P, TPB, 2], F32)
        hot = at("hot", [P, 2, TPB, E], F32)
        chosen = at("chosen", [P, TPB, E], F32)
        chosen_b = at("chosen_b", [P, TPB, E], BF16)
        seen = at("seen", [P, E], F32)
        seen_add = at("seen_add", [P, E], F32)
        seen_b = at("seen_b", [P, E], BF16)
        pos = at("pos", [P, TPB, E], F32)
        pos_k = at("pos_k", [P, 2, TPB, E], F32)
        slot_f = at("slot_f", [P, 2, TPB], F32)
        slot_i = at("slot_i", [P, 2, 2, TPB], I32)
        tok_f = at("tok_f", [P, B, TPB], F32)
        counts = at("counts", [P, E], F32)
        tiles_i = at("tiles_i", [P, E], I32)
        tiles_f = at("tiles_f", [P, E], F32)
        tiles_end = at("tiles_end", [P, E], F32)
        step_e = at("step_e", [P, E], F32)
        passed = at("passed", [P, E], F32)
        jump = at("jump", [P, E], F32)
        turn_mark = at("turn_mark", [P, 1], F32)
        tcol = at("tcol", [P, 2], F32)
        tcol2 = at("tcol2", [P, TAB_N], F32)
        meets = at("meets", [P, E], F32)
        assert place[0] <= top_at, place[0] - top_at

        ident = cn[:, C_ID:C_ID + P]

        ps = ctx.enter_context(nc.psum_tensor("ps", [P, 8, BLK], F32))
        tp = [ps[:, RING, :], ps[:, RING + 1, :]]
        rt = ps[:, RING + 2, :]
        logits = rt[:, 0:TPB * E].rearrange("p (i e) -> p i e", e=E)
        ranks = rt[:, 64:64 + TPB * E].rearrange("p (i e) -> p i e", e=E)
        total = rt[:, 128:128 + E]

        routed = nc.dram_tensor("routed", [ROWS, ROW], F32, kind="Internal").ap()
        xf = x.rearrange("b s d -> (b s) d")

        consts_in, mod_in, raw_in = sem("consts_in"), sem("mod_in"), [sem(f"raw_in{n}") for n in range(3)]
        small_ready = sem("small_ready")
        cond_sig, cond_act, cond_rep = sem("cond_sig"), sem("cond_act"), sem("cond_rep")
        mod_mm, mod_rows = sem("mod_mm"), sem("mod_rows")
        w_hi, w_lo = sem("w_hi"), sem("w_lo")
        raw_loaded = sem("raw_loaded")
        x_in = sem("x_in")
        bn, aggr, var_eps, rstd_r = sem("bn"), sem("aggr"), sem("var_eps"), sem("rstd_r")
        xh, h_scaled, h_ready = sem("xh"), sem("h_scaled"), sem("h_ready")
        ssq_r, ms_r, rms_r, xn_r = sem("ssq_r"), sem("ms_r"), sem("rms_r"), sem("xn_r")
        xnT_t, xnT_h, xnT_l = sem("xnT_t"), sem("xnT_h"), sem("xnT_l")
        gvd_mm, gvd_act = sem("gvd_mm"), sem("gvd_act")
        xs_r, dec_r, scanned, carried = sem("xs_r"), sem("dec_r"), sem("scanned"), sem("carried")
        sT_t, xa_r = sem("sT_t"), sem("xa_r")
        ssq2_r, ms2_r, rms2_r, xn2_r = sem("ssq2_r"), sem("ms2_r"), sem("rms2_r"), sem("xn2_r")
        xn2T_t, xn2T_h, xn2T_l = sem("xn2T_t"), sem("xn2T_h"), sem("xn2T_l")
        gu_mm = sem("gu_mm")
        sig_r, gg_r, hf_r, hid_h, hid_l = (sem(n) for n in ("sig_r", "gg_r", "hf_r", "hid_h", "hid_l"))
        out_mm, xo_r = sem("out_mm"), sem("xo_r")
        x_again_in = sem("x_again_in")
        xg_r, x1_r = sem("xg_r"), sem("x1_r")
        bn2, aggr2, var_eps2, rstd2_r = sem("bn2"), sem("aggr2"), sem("var_eps2"), sem("rstd2_r")
        xh2, h2_scaled, h2_ready = sem("xh2"), sem("h2_scaled"), sem("h2_ready")
        base_r, base_out = sem("base_r"), sem("base_out")
        hT_t, hT_c = sem("hT_t"), sem("hT_c")
        logit_mm, z_r, exp_r, rank_mm = sem("logit_mm"), sem("z_r"), sem("exp_r"), sem("rank_mm")
        route, chosen_r, slots_r = sem("route"), sem("chosen_r"), sem("slots_r")
        scattered = [sem("scattered0"), sem("scattered1")]
        total_mm, tabs, tab_t = sem("total_mm"), sem("tabs"), sem("tab_t")
        TABS = 13
        slot_steps = sem("slot_steps")
        pads_out = sem("pads_out")

        freed = {"gvd": (gvd_act, 3 * KD), "out": (xo_r, 2)}

        def bank(kind, q, k):
            return ps[:, ring[kind, q.n, k][0], :]

        def wait_bank(eng, kind, q, k):
            last = ring[kind, q.n, k][1]
            if last is None:
                return
            lk, ln, i = last
            lq = q.near(ln - q.n)
            if lk == "gu":
                eng.wait_ge((gg_r, hf_r)[i % 2], lq.v * KFA + i // 2 + 1)
            else:
                eng.wait_ge(freed[lk][0], lq.v * freed[lk][1] + i + 1)

        def load_expert(eng, e, buf):
            def halves(ap):
                return ap if isinstance(e, int) else ap.rearrange("e a b -> (e a) b")

            o = buf * EXPW if isinstance(buf, int) else buf
            a = w13[e] if isinstance(e, int) else halves(w13)[bass.ds(e * D, D), :]
            b = w2[e] if isinstance(e, int) else halves(w2)[bass.ds(e * F, F), :]
            eng.dma_start(raw[:, bass.ds(o, W13)].rearrange("p (k n) -> p k n", k=KD),
                          a.rearrange("(k p) n -> p k n", p=P)).then_inc(raw_loaded, 16)
            eng.dma_start(raw[:, bass.ds(o + W13, W2 - D)].rearrange("p (k n) -> p k n", k=KF - 1),
                          b[0:(KF - 1) * P, :].rearrange("(k p) n -> p k n", p=P)).then_inc(raw_loaded, 16)
            eng.dma_start(raw[0:F_LAST, bass.ds(o + EXPW - D, D)], b[(KF - 1) * P:F, :]).then_inc(raw_loaded, 16)

        def mark(g):
            g.tensor_tensor(g_mark[:], cn[:, 0:1], cn[:, 0:1], ALU.add)

        def f32(ap):
            return ap.bitcast(F32)

        def body(step, stages):
            for r in range(-1, 3):
                step(r, None)
            with stages.Fori(0, 2, 1) as turn:
                step(3, turn)
                step(4, turn)
            for r in range(7, NBLK + 3):
                step(r, None)

        with nc.Block() as block:

            @block.sync
            def _(sp):
                def load_x(q):
                    if q.n >= 1:
                        sp.wait_ge(xh, q.v)
                    sp.dma_start(x_sb[:], xf[bass.ds(q.half * BLK + q.par * S, BLK), :]
                                 .rearrange("(i p) d -> p i d", p=P)).then_inc(x_in, 16)

                def load_x_again(q):
                    if q.n >= 1:
                        sp.wait_ge(base_out, q.v * 16)
                    sp.dma_start(x_again[:], xf[bass.ds(q.half * BLK + q.par * S, BLK), :]
                                 .rearrange("(i p) d -> p i d", p=P)).then_inc(x_again_in, 16)

                def store_base(q):
                    sp.wait_ge(base_r, q.v + 1)
                    sp.dma_start(out[bass.ds(q.half * BLK + q.par * S, BLK), :]
                                 .rearrange("(i p) d -> p i d", p=P), x_again[:]).then_inc(base_out, 16)

                sp.dma_start(ct[:], cond_t).then_inc(mod_in, 16)
                sp.dma_start(wmod_sb[:], wmod.rearrange("(k p) n -> p k n", p=P)).then_inc(mod_in, 16)
                sp.dma_start(cn[:], consts).then_inc(consts_in, 16)
                sp.dma_start(vec[:], vecs).then_inc(consts_in, 16)
                sp.dma_start(bias_row[:], bias.partition_broadcast(P)).then_inc(consts_in, 16)
                sp.dma_start(rw_sb[:], router).then_inc(consts_in, 16)
                load_x(Block512(0))
                sp.dma_start(gvd_raw[:], gvd_t.rearrange("(k p) n -> p k n", p=P)).then_inc(raw_in[0], 16)
                sp.dma_start(gu_raw[:], gu_t.rearrange("(k p) n -> p k n", p=P)).then_inc(raw_in[1], 16)
                sp.dma_start(out_raw[:].rearrange("p (k n) -> p k n", k=KFA),
                             out_t.rearrange("(k p) n -> p k n", p=P)).then_inc(raw_in[2], 16)

                def step(r, turn):
                    q = Block512(r, turn)
                    if 1 <= r + 1 < NBLK:
                        load_x(q.near(1))
                    if r == 2:
                        sp.wait_ge(w_lo, 3)
                        load_expert(sp, 0, 0)
                    if 2 <= r < NBLK + 2:
                        load_x_again(q.near(-2))
                        store_base(q.near(-2))

                body(step, sp)
                sp.wait_ge(base_out, NBLK * 16)

            @block.tensor
            def _(pe):
                def three(dst, a_hi, a_lo, b_hi, b_lo, first, last):
                    pe.matmul(dst, a_hi, b_hi, start=first, stop=False)
                    pe.matmul(dst, a_lo, b_hi, start=False, stop=False)
                    return pe.matmul(dst, a_hi, b_lo, start=False, stop=last)

                pe.wait_ge(mod_in, 32)
                pe.wait_ge(cond_rep, 1)
                for b in range(B):
                    for n in range(3):
                        for k in range(KD):
                            mm = pe.matmul(ps[:, 3 * b + n, :], ct_rep[:, k * B + b, :],
                                           wmod_sb[:, k, n * BLK:(n + 1) * BLK], start=(k == 0), stop=(k == KD - 1))
                        mm.then_inc(mod_mm, 1)

                def xn_transposes(q):
                    pe.wait_ge(xn_r, q.v + 1)
                    for c in range(KD):
                        if q.n >= 4:
                            pe.wait_ge(hT_c, (q.v - 4) * KD + c + 1)
                        elif q.n >= 2:
                            pe.wait_ge(xn2T_l, (q.v - 2) * KD + c + 1)
                        elif q.n >= 1:
                            pe.wait_ge(xnT_l, (q.v - 1) * KD + c + 1)
                        for i in range(TPB):
                            mm = pe.transpose(tp[c][:, i * P:(i + 1) * P], xn_sb[:, i, c * P:(c + 1) * P], ident)
                        mm.then_inc(xnT_t, 1)

                def gvd(q, units):
                    for n in units:
                        kind, c = n % 3, n // 3
                        wait_bank(pe, "gvd", q, n)
                        if n == 0:
                            pe.wait_ge(xnT_l, (q.v + 1) * KD)
                        w = slice(kind * D + c * P, kind * D + (c + 1) * P)
                        for k in range(KD):
                            mm = three(bank("gvd", q, n), gvd_hi[:, k, w], gvd_lo[:, k, w],
                                       xnT_hi[:, k, :], xnT_lo[:, k, :], k == 0, k == KD - 1)
                        mm.then_inc(gvd_mm, 1)

                def state_transposes(q):
                    pe.wait_ge(carried, (q.v + 1) * KD)
                    for u in range(2):
                        if q.n + 1 < NBLK:
                            pe.wait_ge(xnT_l, (q.v + 1) * KD + u + 1)
                        else:
                            pe.wait_ge(hT_c, (q.v - 3) * KD + u + 1)
                        for i in range(2):
                            for c in range(KD):
                                t = (2 * u + i) * P
                                mm = pe.transpose(tp[u][:, i * D + c * P:i * D + (c + 1) * P],
                                                  sg_sb[:, c, t:t + P], ident)
                        mm.then_inc(sT_t, 1)

                def xn2_transposes(q):
                    pe.wait_ge(xn2_r, q.v + 1)
                    for c in range(KD):
                        pe.wait_ge(xa_r, q.v * 2 + c + 1)
                        for i in range(TPB):
                            mm = pe.transpose(tp[c][:, i * P:(i + 1) * P], xn_sb[:, i, c * P:(c + 1) * P], ident)
                        mm.then_inc(xn2T_t, 1)

                def gate_up(q, m):
                    if m == 0:
                        pe.wait_ge(xn2T_l, (q.v + 1) * KD)
                    for j in range(2):
                        n = 2 * m + j
                        wait_bank(pe, "gu", q, n)
                        w = slice(j * FA + m * P, j * FA + (m + 1) * P)
                        for k in range(KD):
                            mm = three(bank("gu", q, n), gu_hi[:, k, w], gu_lo[:, k, w],
                                       xn2T_hi[:, k, :], xn2T_lo[:, k, :], k == 0, k == KD - 1)
                        mm.then_inc(gu_mm, 1)

                def ffn_out(q, u):
                    wait_bank(pe, "out", q, u)
                    if u == 0:
                        pe.wait_ge(hid_l, (q.v + 1) * KFA)
                    for i in range(2):
                        t = slice((2 * u + i) * P, (2 * u + i + 1) * P)
                        for k in range(KFA):
                            mm = three(bank("out", q, u)[:, i * D:(i + 1) * D], hid_hi[:, k, t], hid_lo[:, k, t],
                                       out_hi[:, k, :], out_lo[:, k, :], k == 0, k == KFA - 1)
                    mm.then_inc(out_mm, 1)

                def h2_transposes(q):
                    pe.wait_ge(h2_ready, q.v + 1)
                    for c in range(KD):
                        if q.n + 2 < NBLK:
                            pe.wait_ge(xn2T_l, (q.v + 2) * KD + c + 1)
                        else:
                            pe.wait_ge(hT_c, (q.v - 1) * KD + c + 1)
                        for i in range(TPB):
                            mm = pe.transpose(tp[c][:, i * P:(i + 1) * P], rows[:, q.par, i, c * P:(c + 1) * P], ident)
                        mm.then_inc(hT_t, 1)

                def router_logits(q):
                    pe.wait_ge(hT_c, (q.v + 1) * KD)
                    pe.wait_ge(slots_r, q.v + 1)
                    for i in range(TPB):
                        for k in range(KD):
                            mm = pe.matmul(logits[:, i, :], hT_sb[:, k, i * P:(i + 1) * P], rw_sb[:, k, :],
                                           start=(k == 0), stop=(k == KD - 1))
                    mm.then_inc(logit_mm, 1)

                def rank_tokens(q):
                    pe.wait_ge(chosen_r, q.v + 1)
                    for i in range(TPB):
                        pe.matmul(ranks[:, i, :], tri[:], chosen_b[:, i, :], start=True, stop=False)
                        for j in range(i):
                            pe.matmul(ranks[:, i, :], ones[:], chosen_b[:, j, :], start=False, stop=False)
                        mm = pe.matmul(ranks[:, i, :], ones[:], seen_b[:], start=False, stop=True)
                    mm.then_inc(rank_mm, 1)

                def step(r, turn):
                    q = Block512(r, turn)
                    routing, adding, ffn = q.near(-3), q.near(-2), q.near(-1)
                    if r == 0:
                        pe.wait_ge(mod_rows, 1)
                        pe.wait_ge(w_lo, 1)
                    if 0 <= r < NBLK:
                        gvd(q, [0])
                    if r >= 3:
                        h2_transposes(routing)
                    if 0 <= r < NBLK:
                        gvd(q, [1, 2])
                    if r >= 3:
                        router_logits(routing)
                    if 0 <= r < NBLK:
                        gvd(q, range(3, 3 * KD))
                    if 2 <= r < NBLK + 2:
                        if r == 2:
                            pe.wait_ge(w_lo, 3)
                        ffn_out(adding, 0)
                    if r + 1 < NBLK:
                        xn_transposes(q.near(1))
                    if r >= 3:
                        rank_tokens(routing)
                    if 2 <= r < NBLK + 2:
                        ffn_out(adding, 1)
                    if r == 1:
                        pe.wait_ge(w_lo, 2)
                    for m in range(KFA):
                        if m == 1 and 0 <= r < NBLK:
                            state_transposes(q)
                        if m == 4 and 0 <= r < NBLK:
                            xn2_transposes(q)
                        if 1 <= r <= NBLK:
                            gate_up(ffn, m)

                pe.wait_ge(consts_in, 64)
                body(step, pe)
                pe.wait_ge(slots_r, NBLK + 1)
                pe.matmul(total, ones[:], seen_b[:], start=True, stop=True).then_inc(total_mm, 1)
                pe.wait_ge(tabs, TABS)
                pe.transpose(tp[0][0:TAB_N, 0:P], tcol2[:], ident).then_inc(tab_t, 1)

            @block.scalar
            def _(act):
                act.wait_ge(mod_in, 32)
                act.activation(ct_sig[:], ct[:], ACT.Sigmoid).then_inc(cond_sig, 1)
                act.wait_ge(consts_in, 64)
                act.wait_ge(raw_in[0], 16)
                def split_gvd():
                    act.wait_ge(raw_in[0], 16)
                    for k in range(KD):
                        i = act.activation(gvd_hi[:, k, :], gvd_raw[:, k, :], ACT.Identity, scale=vec[:, V_MIX + k:V_MIX + k + 1])
                    i.then_inc(w_hi, 1)

                def split_gu_out():
                    act.wait_ge(raw_in[1], 16)
                    for k in range(KD):
                        i = act.activation(gu_hi[:, k, :], gu_raw[:, k, :], ACT.Identity, scale=vec[:, V_FFN + k:V_FFN + k + 1])
                    i.then_inc(w_hi, 1)
                    act.wait_ge(raw_in[2], 16)
                    act.activation(out_hi[:].rearrange("p k n -> p (k n)"), out_raw[:], ACT.Identity).then_inc(w_hi, 1)

                def mean_squares(q, squares, src, ready, count, dst, done):
                    act.wait_ge(ready, count)
                    for i in range(TPB):
                        a = act.activation(squares[:, i, :], src[:, i, :], ACT.Square, scale=D ** -0.5, accum_out=dst[:, i:i + 1])
                    a.then_inc(done, 1)

                def front(q):
                    if q.n >= 1:
                        act.wait_ge(rms_r, q.v)
                    mean_squares(q, squares, h_sb[:, q.par], h_ready, q.v + 1, ssq, ssq_r)

                def xn(q):
                    act.wait_ge(rms_r, q.v + 1)
                    if q.n >= 2:
                        act.wait_ge(xn2T_t, (q.v - 1) * KD)
                    elif q.n >= 1:
                        act.wait_ge(xnT_t, KD)
                    for i in range(TPB):
                        a = act.activation(xn_sb[:, i, :], h_sb[:, q.par, i, :], ACT.Copy, scale=rms[:, i:i + 1])
                    a.then_inc(xn_r, 1)

                def xn_hi(q):
                    for c in range(KD):
                        act.wait_ge(xnT_t, q.v * KD + c + 1)
                        if c == 0 and q.n >= 1:
                            act.wait_ge(gvd_mm, q.v * 3 * KD)
                        act.activation(xnT_hi[:, c, :], tp[c], ACT.Copy).then_inc(xnT_h, 1)

                def gvd_activations(q, units):
                    for n in units:
                        kind, c = n % 3, n // 3
                        act.wait_ge(gvd_mm, q.v * 3 * KD + n + 1)
                        if q.n >= 1 and kind == 0:
                            act.wait_ge(sT_t, q.v * 2)
                        if q.n >= 1 and kind == 1:
                            act.wait_ge(scanned, (q.v - 1) * KD + c + 1)
                        dst = (sg_sb, tv_sb, dec_sb)[kind]
                        act.activation(dst[:, c, :], bank("gvd", q, n), (ACT.Sigmoid, ACT.Tanh, ACT.Sigmoid)[kind],
                                       bias=vec[:, V_BIAS + kind * KD + c:V_BIAS + kind * KD + c + 1]).then_inc(gvd_act, 1)

                def middle(q):
                    if q.n >= 1:
                        act.wait_ge(rms2_r, q.v)
                    mean_squares(q, squares2, xa_sb[:, q.par], xa_r, 2 * q.v + 2, ssq2, ssq2_r)

                def xn2(q):
                    act.wait_ge(rms2_r, q.v + 1)
                    act.wait_ge(xnT_t, (q.v + 2) * KD if q.n + 1 < NBLK else NBLK * KD)
                    for i in range(TPB):
                        a = act.activation(xn_sb[:, i, :], xa_sb[:, q.par, i, :], ACT.Copy, scale=rms2[:, i:i + 1])
                    a.then_inc(xn2_r, 1)

                def xn2_hi(q):
                    for c in range(KD):
                        act.wait_ge(xn2T_t, q.v * KD + c + 1)
                        if c == 0 and q.n >= 1:
                            act.wait_ge(gu_mm, q.v * 2 * KFA)
                        act.activation(xn2T_hi[:, c, :], tp[c], ACT.Copy).then_inc(xn2T_h, 1)

                def gate_sigmoid(q, m):
                    act.wait_ge(gu_mm, q.v * 2 * KFA + 2 * m + 1)
                    if q.n >= 1 or m >= 2:
                        act.wait_ge(gg_r, q.v * KFA + m - 1)
                    act.activation(sig_sb[:, m % 2, :], bank("gu", q, 2 * m), ACT.Sigmoid).then_inc(sig_r, 1)

                def hidden_hi(q, m):
                    act.wait_ge(hf_r, q.v * KFA + m + 1)
                    if m == 0 and q.n >= 1:
                        act.wait_ge(out_mm, q.v * 2)
                    act.activation(hid_hi[:, m, :], hf_sb[:, m % 2, :], ACT.Copy).then_inc(hid_h, 1)

                def h2_copy(q):
                    for c in range(KD):
                        act.wait_ge(hT_t, q.v * KD + c + 1)
                        if c == 0:
                            act.wait_ge(slots_r, q.v + 1)
                        act.activation(hT_sb[:, c, :], tp[c], ACT.Copy).then_inc(hT_c, 1)

                def router_exp(q):
                    act.wait_ge(z_r, q.v + 1)
                    act.activation(ee[:], zz[:], ACT.Exp).then_inc(exp_r, 1)

                def step(r, turn):
                    q = Block512(r, turn)
                    nxt, routing, ffn = q.near(1), q.near(-3), q.near(-1)
                    gvd_on, ffn_on = 0 <= r < NBLK, 1 <= r <= NBLK
                    if gvd_on:
                        gvd_activations(q, [0])
                    if r >= 3:
                        h2_copy(routing)
                    if gvd_on:
                        gvd_activations(q, [1, 2])
                    if r >= 3:
                        router_exp(routing)
                    if gvd_on:
                        gvd_activations(q, [3, 4])
                    if r + 1 < NBLK:
                        front(nxt)
                    if gvd_on:
                        gvd_activations(q, [5])
                    if r + 1 < NBLK:
                        xn(nxt)
                    if r == -1:
                        split_gvd()
                    if r + 1 < NBLK:
                        xn_hi(nxt)
                    if r == 0:
                        split_gu_out()
                    for m in range(KFA):
                        if ffn_on:
                            gate_sigmoid(ffn, m)
                        if m == 1 and gvd_on:
                            middle(q)
                        if ffn_on and m >= 1:
                            hidden_hi(ffn, m - 1)
                        if m == 2 and gvd_on:
                            xn2(q)
                        if m == 4 and gvd_on:
                            xn2_hi(q)
                    if ffn_on:
                        hidden_hi(ffn, KFA - 1)

                body(step, act)

            @block.vector
            def _(v):
                def chain(counter, at_value):
                    n = [0]

                    def link(i):
                        n[0] += 1
                        i.then_inc(counter, 1)
                        v.wait_ge(counter, at_value + n[0])
                    return link

                v.memset(ones[:], 1.0)
                v.memset(ones_f[:], 1.0)
                v.memset(minus_half[:], -0.5)
                v.memset(eps_ln[:], EPS_LN)
                v.memset(eps_rms[:], EPS_RMS)
                v.memset(carry[:], 0.0)
                v.memset(seen[:], 0.0)
                v.memset(seen_b[:], 0.0).then_inc(slots_r, 1)
                v.memset(pad_rows[:], 0.0).then_inc(small_ready, 1)
                v.wait_ge(consts_in, 64)
                v.tensor_copy(tri[:], cn[:, C_TRI:C_TRI + P])
                v.tensor_copy(tok_f[:].rearrange("p b i -> p (b i)"), cn[:, C_TOK:C_TOK + B * TPB]).then_inc(small_ready, 1)
                v.wait_ge(small_ready, 2)
                v.tensor_copy(pad_rows[:, ROW - 1:ROW], cn[:, C_PAD:C_PAD + 1]).then_inc(small_ready, 1)
                v.wait_ge(cond_sig, 1)
                v.tensor_tensor(ct_sig[:], ct[:], ct_sig[:], ALU.mult).then_inc(cond_act, 1)
                v.wait_ge(cond_act, 1)
                v.tensor_copy(ct_rep[:], ct_sig[:].rearrange("p k b -> p (k b)").unsqueeze(2).to_broadcast([P, KD * B, P]))\
                    .then_inc(cond_rep, 1)
                v.wait_ge(mod_mm, 6)
                for b in range(B):
                    m = [ps[:, 3 * b + n // 2, (n % 2) * D:(n % 2 + 1) * D] for n in range(6)]
                    v.tensor_copy(mod[:, b, M_S1, :], m[0])
                    v.tensor_scalar(mod[:, b, M_A1, :], m[1], 1.0, None, ALU.add)
                    v.tensor_copy(g_raw[:, (2 * b) * D:(2 * b + 1) * D], m[2])
                    v.tensor_copy(mod[:, b, M_S2, :], m[3])
                    v.tensor_scalar(mod[:, b, M_A2, :], m[4], 1.0, None, ALU.add)
                    i = v.tensor_copy(g_raw[:, (2 * b + 1) * D:(2 * b + 2) * D], m[5])
                i.then_inc(mod_rows, 1)
                gf = gates[:].rearrange("p b g d -> p (b g d)")
                v.wait_ge(mod_rows, 1)
                v.scalar_tensor_tensor(gf, g_raw[:], -1.0, g_raw[:], ALU.mult, ALU.max).then_inc(mod_rows, 1)
                v.tensor_scalar(g_raw[:], g_raw[:], 0.0, 2.0, ALU.is_ge, ALU.mult).then_inc(mod_rows, 1)
                v.wait_ge(mod_rows, 3)
                v.tensor_scalar(gf, gf, 0.25, None, ALU.max).then_inc(mod_rows, 1)
                v.wait_ge(mod_rows, 4)
                v.scalar_tensor_tensor(gf, g_raw[:], -1.0, gf, ALU.add, ALU.mult).then_inc(mod_rows, 1)
                v.wait_ge(mod_rows, 5)
                for b in range(B):
                    i = v.tensor_tensor(mod[:, b, M_GBB, :], gates[:, b, 1, :], bias_row[:], ALU.mult)
                i.then_inc(mod_rows, 1)

                def split_gvd():
                    v.wait_ge(w_hi, 1)
                    for k in range(KD):
                        i = v.scalar_tensor_tensor(gvd_lo[:, k, :], gvd_raw[:, k, :], vec[:, V_MIX + k:V_MIX + k + 1],
                                                   f32(gvd_hi[:, k, :]), ALU.mult, ALU.subtract)
                    i.then_inc(w_lo, 1)

                def split_gu_out():
                    v.wait_ge(w_hi, 2)
                    for k in range(KD):
                        i = v.scalar_tensor_tensor(gu_lo[:, k, :], gu_raw[:, k, :], vec[:, V_FFN + k:V_FFN + k + 1],
                                                   f32(gu_hi[:, k, :]), ALU.mult, ALU.subtract)
                    i.then_inc(w_lo, 1)
                    v.wait_ge(w_hi, 3)
                    v.tensor_tensor(out_lo[:].rearrange("p k n -> p (k n)"), out_raw[:],
                                    f32(out_hi[:].rearrange("p k n -> p (k n)")), ALU.subtract).then_inc(w_lo, 1)

                def layer_norm_stats(q, x, stats, mv, bn, aggr):
                    for i in range(TPB):
                        v.bn_stats(stats[:, i, :], x[:, i, :]).then_inc(bn, 1)
                    v.wait_ge(bn, (q.v + 1) * TPB)
                    v.memset(turn_mark[:], 0.0)
                    for i in range(TPB):
                        v.bn_aggr(mv[:, i, :], stats[:, i, :]).then_inc(aggr, 1)
                    v.wait_ge(aggr, (q.v + 1) * TPB)

                def front_centre(q):
                    v.wait_ge(x_in, (q.v + 1) * 16)
                    layer_norm_stats(q, x_sb, stats, mv, bn, aggr)
                    for i in range(TPB):
                        a = v.scalar_tensor_tensor(h_sb[:, q.par, i, :], x_sb[:, i, :], mv[:, i, 0:1],
                                                   mod[:, q.par, M_A1, :], ALU.subtract, ALU.mult)
                    a.then_inc(xh, 1)

                def front_scale(q):
                    v.wait_ge(rstd_r, q.v + 1)
                    v.wait_ge(xh, q.v + 1)
                    for i in range(TPB):
                        a = v.scalar_tensor_tensor(h_sb[:, q.par, i, :], h_sb[:, q.par, i, :], rstd[:, i:i + 1],
                                                   mod[:, q.par, M_S1, :], ALU.mult, ALU.add)
                    a.then_inc(h_ready, 1)

                def xn_lo(q):
                    for c in range(KD):
                        v.wait_ge(xnT_h, q.v * KD + c + 1)
                        v.tensor_tensor(xnT_lo[:, c, :], tp[c], f32(xnT_hi[:, c, :]), ALU.subtract).then_inc(xnT_l, 1)

                def scan(q, c):
                    v.wait_ge(gvd_act, q.v * 3 * KD + 3 * c + 3)
                    v.tensor_scalar(dec_sb[:, c, :], dec_sb[:, c, :], 0.998, 0.001, ALU.mult, ALU.add).then_inc(dec_r, 1)
                    v.wait_ge(dec_r, q.v * KD + c + 1)
                    v.wait_ge(xs_r, q.v * KD + c + 1)
                    if q.n >= 1:
                        v.wait_ge(carried, q.v * KD)
                    v.tensor_tensor_scan(sg_sb[:, c, :], dec_sb[:, c, :], tv_sb[:, c, :], carry[:, q.par, c:c + 1],
                                         ALU.mult, ALU.add).then_inc(scanned, 1)

                def keep_last(q):
                    for c in range(KD):
                        v.wait_ge(scanned, q.v * KD + c + 1)
                        v.tensor_copy(carry[:, q.par, c:c + 1], sg_sb[:, c, BLK - 1:BLK]).then_inc(carried, 1)

                def add_state(q):
                    for u in range(2):
                        v.wait_ge(sT_t, q.v * 2 + u + 1)
                        t = slice(2 * u, 2 * u + 2)
                        v.tensor_tensor(xa_sb[:, q.par, t, :], tp[u].rearrange("p (i d) -> p i d", d=D),
                                        h_sb[:, q.par, t, :], ALU.add).then_inc(xa_r, 1)

                def xn2_lo(q):
                    for c in range(KD):
                        v.wait_ge(xn2T_h, q.v * KD + c + 1)
                        v.tensor_tensor(xn2T_lo[:, c, :], tp[c], f32(xn2T_hi[:, c, :]), ALU.subtract).then_inc(xn2T_l, 1)

                def hidden(q, m):
                    v.wait_ge(sig_r, q.v * KFA + m + 1)
                    v.tensor_tensor(gg_sb[:, m % 2, :], bank("gu", q, 2 * m), sig_sb[:, m % 2, :], ALU.mult).then_inc(gg_r, 1)
                    v.wait_ge(gu_mm, q.v * 2 * KFA + 2 * m + 2)
                    if q.n >= 1 or m >= 2:
                        v.wait_ge(hid_l, q.v * KFA + m - 1)
                    v.wait_ge(gg_r, q.v * KFA + m + 1)
                    v.tensor_tensor(hf_sb[:, m % 2, :], bank("gu", q, 2 * m + 1), gg_sb[:, m % 2, :], ALU.mult).then_inc(hf_r, 1)

                def add_ffn(q, u):
                    if q.n >= 1 and u == 0:
                        v.wait_ge(x1_r, q.v)
                    v.wait_ge(out_mm, q.v * 2 + u + 1)
                    t = slice(2 * u, 2 * u + 2)
                    v.tensor_tensor(xo_sb[:, t, :], bank("out", q, u).rearrange("p (i d) -> p i d", d=D),
                                    xa_sb[:, q.par, t, :], ALU.add).then_inc(xo_r, 1)

                def gate_xo(q):
                    v.wait_ge(xo_r, (q.v + 1) * 2)
                    v.tensor_tensor(xo_sb[:], xo_sb[:], gates[:, q.par, 0, :].unsqueeze(1).to_broadcast([P, TPB, D]),
                                    ALU.mult).then_inc(xg_r, 1)

                def norm2_centre(q):
                    v.wait_ge(x1_r, q.v + 1)
                    layer_norm_stats(q, x_again, stats2, mv2, bn2, aggr2)
                    v.wait_ge(scattered[q.par], q.half * 32 * TPB + 16)
                    for i in range(TPB):
                        a = v.scalar_tensor_tensor(rows[:, q.par, i, 0:D], x_again[:, i, :], mv2[:, i, 0:1],
                                                   mod[:, q.par, M_A2, :], ALU.subtract, ALU.mult)
                    a.then_inc(xh2, 1)

                def norm2_scale(q):
                    v.wait_ge(rstd2_r, q.v + 1)
                    v.wait_ge(xh2, q.v + 1)
                    for i in range(TPB):
                        a = v.scalar_tensor_tensor(rows[:, q.par, i, 0:D], rows[:, q.par, i, 0:D], rstd2[:, i:i + 1],
                                                   mod[:, q.par, M_S2, :], ALU.mult, ALU.add)
                    a.then_inc(h2_ready, 1)

                ROUTE = 11

                def softmax_start(q):
                    v.wait_ge(logit_mm, q.v + 1)
                    link = chain(route, q.v * ROUTE)
                    link(v.tensor_reduce(mx[:], logits, AX.X, ALU.max))
                    v.tensor_tensor(zz[:], logits, mx[:].unsqueeze(2).to_broadcast([P, TPB, E]), ALU.subtract).then_inc(z_r, 1)

                def top2(q):
                    link = chain(route, q.v * ROUTE + 1)
                    v.wait_ge(exp_r, q.v + 1)
                    link(v.tensor_reduce(mx[:], ee[:], AX.X, ALU.add))
                    link(v.reciprocal(mx[:], mx[:]))
                    link(v.tensor_tensor(pp[:], ee[:], mx[:].unsqueeze(2).to_broadcast([P, TPB, E]), ALU.mult))
                    v.tensor_copy(rows[:, q.par, :, D + E], tok_f[:, q.par, :])
                    for i in range(TPB):
                        a = v.max(top[:, i, :], pp[:, i, :])
                    link(a)
                    v.tensor_scalar(tok_f[:, q.par, :], tok_f[:, q.par, :], float(BLK), None, ALU.add)
                    for i in range(TPB):
                        a = v.max_index(top_i[:, i, :], top[:, i, :], pp[:, i, :])
                    link(a)
                    link(v.tensor_copy(top_f[:], top_i[:, :, 0:2]))
                    iota = cn[:, C_IOTA:C_IOTA + TPB * E].rearrange("p (i e) -> p i e", e=E)
                    for k in range(2):
                        link(v.tensor_tensor(hot[:, k], iota, top_f[:, :, k:k + 1].to_broadcast([P, TPB, E]), ALU.is_equal))
                    link(v.tensor_tensor(chosen[:], hot[:, 0], hot[:, 1], ALU.add))
                    link(v.tensor_copy(chosen_b[:], chosen[:]))
                    v.tensor_tensor(rows[:, q.par, :, D:D + E], chosen[:], pp[:], ALU.mult).then_inc(chosen_r, 1)

                SLOT = 5

                def slots(q):
                    v.wait_ge(rank_mm, q.v + 1)
                    link = chain(slot_steps, q.v * SLOT)
                    link(v.tensor_tensor(pos[:], ranks, cn[:, C_OFF:C_OFF + E].unsqueeze(1).to_broadcast([P, TPB, E]), ALU.add))
                    for k in range(2):
                        i = v.tensor_tensor(pos_k[:, k], pos[:], hot[:, k], ALU.mult)
                    link(i)
                    link(v.tensor_reduce(slot_f[:], pos_k[:], AX.X, ALU.add))
                    v.wait_ge(scattered[q.par], q.half * 32 * TPB + 16)
                    v.tensor_copy(slot_i[:, q.par], slot_f[:])
                    link(v.tensor_reduce(seen_add[:], chosen[:].rearrange("p i e -> p e i"), AX.X, ALU.add))
                    link(v.tensor_tensor(seen[:], seen[:], seen_add[:], ALU.add))
                    v.tensor_copy(seen_b[:], seen[:]).then_inc(slots_r, 1)

                def step(r, turn):
                    q = Block512(r, turn)
                    nxt, routing, adding, ffn = q.near(1), q.near(-3), q.near(-2), q.near(-1)
                    gvd_on, add_on, ffn_on, route_on = 0 <= r < NBLK, 2 <= r < NBLK + 2, 1 <= r <= NBLK, r >= 3
                    if r + 1 < NBLK:
                        front_centre(nxt)
                    if route_on:
                        softmax_start(routing)
                    if r + 1 < NBLK:
                        front_scale(nxt)
                    if gvd_on:
                        scan(q, 0)
                    if route_on:
                        top2(routing)
                    if gvd_on:
                        scan(q, 1)
                        keep_last(q)
                    if add_on:
                        add_ffn(adding, 0)
                    if r == -1:
                        split_gvd()
                    if r + 1 < NBLK:
                        xn_lo(nxt)
                    if r == 0:
                        split_gu_out()
                    if route_on:
                        slots(routing)
                    if add_on:
                        add_ffn(adding, 1)
                        gate_xo(adding)
                    if ffn_on:
                        hidden(ffn, 0)
                    if gvd_on:
                        add_state(q)
                    if ffn_on:
                        hidden(ffn, 1)
                    if add_on:
                        norm2_centre(adding)
                    if ffn_on:
                        hidden(ffn, 2)
                    if add_on:
                        norm2_scale(adding)
                    if ffn_on:
                        hidden(ffn, 3)
                    if gvd_on:
                        xn2_lo(q)
                    if ffn_on:
                        hidden(ffn, 4)
                        hidden(ffn, 5)

                body(step, v)

                v.wait_ge(total_mm, 1)
                link = chain(tabs, 0)
                link(v.tensor_copy(counts[:], total))
                v.tensor_copy(counts_i[:], counts[:])
                link(v.tensor_scalar(tiles_f[:], counts[:], 1.0, float(P - 1), ALU.max, ALU.add))
                link(v.tensor_copy(tiles_i[:], tiles_f[:]))
                link(v.tensor_scalar(tiles_i[:], tiles_i[:], P.bit_length() - 1, None, ALU.logical_shift_right))
                link(v.tensor_copy(tiles_f[:], tiles_i[:]))
                v.tensor_tensor_scan(tiles_end[:], ones_f[:], tiles_f[:], 0.0, ALU.mult, ALU.add)
                link(v.tensor_scalar(step_e[:], tiles_f[:], -float(P), float(REGION), ALU.mult, ALU.add))
                v.tensor_scalar(meets[:], tiles_end[:], cn[:, C_TILE:C_TILE + 1], None, ALU.is_equal)
                link(v.tensor_scalar(passed[:], tiles_end[:], cn[:, C_TILE:C_TILE + 1], None, ALU.is_le))
                v.tensor_reduce(tcol2[:, TAB_EXPERT:TAB_EXPERT + 1], passed[:, 0:E - 1], AX.X, ALU.add)
                v.tensor_reduce(tcol2[:, TAB_SPLIT:TAB_SPLIT + 1], meets[:, 0:E - 2], AX.X, ALU.add)
                v.tensor_reduce(tcol2[:, TAB_LOAD:TAB_LOAD + 1], meets[:, 0:E - 4], AX.X, ALU.add)
                link(v.tensor_tensor(jump[:], passed[:], step_e[:], ALU.mult))
                link(v.tensor_reduce(tcol[:, 1:2], jump[:], AX.X, ALU.add))
                link(v.tensor_tensor(passed[:], passed[:], cn[:, C_ALT:C_ALT + E], ALU.mult))
                link(v.tensor_reduce(tcol[:, 0:1], passed[:, 0:E - 1], AX.X, ALU.add))
                v.tensor_scalar(tcol2[:, TAB_BUF:TAB_BUF + 1], tcol[:, 0:1], float(EXPW), None, ALU.mult)
                link(v.scalar_tensor_tensor(tcol[:, 1:2], cn[:, C_TILE:C_TILE + 1], float(P), tcol[:, 1:2],
                                            ALU.mult, ALU.add))
                link(v.tensor_scalar(tcol2[:, TAB_ROW:TAB_ROW + 1], tcol[:, 1:2], float(E * REGION), None, ALU.min))
                v.wait_ge(tab_t, 1)
                v.tensor_copy(tab[0:TAB_N, :], tp[0][0:TAB_N, 0:P])

            @block.gpsimd
            def _(g):
                def power(dst, src):
                    return g.tensor_tensor(dst[:], src[:], minus_half[:], ALU.pow)

                def row(b, m):
                    return mod[:, b, m, :].unsqueeze(1).to_broadcast([P, TPB, D])

                def front(q):
                    g.wait_ge(aggr, (q.v + 1) * TPB)
                    g.tensor_tensor(ve[:], mv[:, :, 1], eps_ln[:], ALU.add).then_inc(var_eps, 1)
                    g.wait_ge(var_eps, q.v + 1)
                    power(rstd, ve).then_inc(rstd_r, 1)

                def rms1(q):
                    g.wait_ge(ssq_r, q.v + 1)
                    g.tensor_tensor(ms[:], ssq[:], eps_rms[:], ALU.add).then_inc(ms_r, 1)
                    g.wait_ge(ms_r, q.v + 1)
                    power(rms, ms).then_inc(rms_r, 1)

                def rms_2(q):
                    g.wait_ge(ssq2_r, q.v + 1)
                    g.tensor_tensor(ms2[:], ssq2[:], eps_rms[:], ALU.add).then_inc(ms2_r, 1)
                    g.wait_ge(ms2_r, q.v + 1)
                    power(rms2, ms2).then_inc(rms2_r, 1)

                def gated_value(q, c):
                    g.wait_ge(gvd_act, q.v * 3 * KD + 3 * c + 2)
                    g.tensor_tensor(tv_sb[:, c, :], sg_sb[:, c, :], tv_sb[:, c, :], ALU.mult).then_inc(xs_r, 1)

                def hidden_lo(q, m):
                    g.wait_ge(hid_h, q.v * KFA + m + 1)
                    g.tensor_tensor(hid_lo[:, m, :], hf_sb[:, m % 2, :], f32(hid_hi[:, m, :]), ALU.subtract).then_inc(hid_l, 1)

                def residual(q):
                    g.wait_ge(xg_r, q.v + 1)
                    g.wait_ge(x_again_in, (q.v + 1) * 16)
                    g.tensor_tensor(x_again[:], x_again[:], xo_sb[:], ALU.add).then_inc(x1_r, 1)

                def norm2(q):
                    g.wait_ge(aggr2, (q.v + 1) * TPB)
                    g.tensor_tensor(ve2[:], mv2[:, :, 1], eps_ln[:], ALU.add).then_inc(var_eps2, 1)
                    g.wait_ge(var_eps2, q.v + 1)
                    power(rstd2, ve2).then_inc(rstd2_r, 1)

                def result_base(q):
                    g.wait_ge(xh2, q.v + 1)
                    g.wait_ge(x1_r, q.v + 1)
                    g.tensor_tensor(x_again[:], x_again[:], row(q.par, M_GBB), ALU.add).then_inc(base_r, 1)

                def scatter(q, tiles_of):
                    if 0 in tiles_of:
                        g.wait_ge(slots_r, q.v + 2)
                        mark(g)
                    for i in tiles_of:
                        for k in range(2):
                            g.indirect_dma_start(routed, bass.IndirectOffsetOnAxis(ap=slot_i[:, q.par, k, i:i + 1], axis=0),
                                                 rows[:, q.par, i, :], None)\
                                .then_inc(scattered[q.par], 16)

                def step(r, turn):
                    q = Block512(r, turn)
                    nxt, routing, adding, ffn = q.near(1), q.near(-3), q.near(-2), q.near(-1)
                    gvd_on, add_on, ffn_on, route_on = 0 <= r < NBLK, 2 <= r < NBLK + 2, 1 <= r <= NBLK, r >= 3
                    if r + 1 < NBLK:
                        front(nxt)
                    if gvd_on:
                        gated_value(q, 0)
                    if r + 1 < NBLK:
                        rms1(nxt)
                    if gvd_on:
                        gated_value(q, 1)
                    if route_on:
                        scatter(routing, [0])
                    if add_on:
                        residual(adding)
                    if ffn_on:
                        hidden_lo(ffn, 0)
                    if route_on:
                        scatter(routing, [1])
                    if gvd_on:
                        rms_2(q)
                    if add_on:
                        norm2(adding)
                    if ffn_on:
                        hidden_lo(ffn, 1)
                    if ffn_on:
                        hidden_lo(ffn, 2)
                    if route_on:
                        scatter(routing, [2])
                    if ffn_on:
                        hidden_lo(ffn, 3)
                    if add_on:
                        result_base(adding)
                    if ffn_on:
                        hidden_lo(ffn, 4)
                    if route_on:
                        scatter(routing, [3])
                    if ffn_on:
                        hidden_lo(ffn, 5)

                g.wait_ge(small_ready, 3)
                g.dma_start(routed[E * REGION:ROWS, :], pad_rows[:]).then_inc(scattered[0], 16)
                g.dma_start(out[T:T + P, :], pad_rows[:, 0:D]).then_inc(scattered[1], 16)
                g.wait_ge(mod_rows, 6)
                body(step, g)
                for b in range(2):
                    g.wait_ge(scattered[b], NBLK // 2 * 32 * TPB + 16)

        rows_in = [sem("rows_in0"), sem("rows_in1")]
        xT_t, xT_h, xT_l, a_mm, b_mm, gelu_r, hid_r = (sem(n) for n in ("xT_t", "xT_h", "xT_l", "a_mm", "b_mm", "gelu_r", "hid_r"))
        hidT_t, hidT_h, hidT_l, y_mm, y_r = (sem(n) for n in ("hidT_t", "hidT_h", "hidT_l", "y_mm", "y_r"))
        gate_steps, gates_r, y_sum, added = sem("gate_steps"), sem("gates_r"), sem("y_sum"), sem("added")
        padding = sem("padding")
        we_hi, w13_lo, w2_lo = sem("we_hi"), sem("w13_lo"), sem("w2_lo")
        PS_Y, PS_HT, PS_XT = 4, 5, 7
        y_ps, xT_ps = ps[:, PS_Y, 0:D], ps[:, PS_XT, 0:KD * P]
        hidT_ps = ps[:, PS_HT:PS_HT + 2, :].rearrange("p a n -> p (a n)")[:, 0:KF * P]
        PIECES = [(0, 2 * F), (2 * F, 2 * F), (W13, W2)]

        class Tile:

            def __init__(self, n, turn=None):
                self.n, self.turn, self.par = n, turn, n % 2
                self.v = n if turn is None else turn * 2 + n
                self.half = n // 2 if turn is None else turn + n // 2

            def near(self, d):
                return Tile(self.n + d, self.turn)

        def tiles(engine, first, step, last):
            first(Tile(0))
            step(Tile(1))
            step(Tile(2))
            with engine.Fori(0, (MOE_TILES - 3) // 2, 1) as turn:
                step(Tile(3, turn))
                step(Tile(4, turn))
            last(Tile(MOE_TILES - 1))

        assert (MOE_TILES - 3) % 2 == 0

        def entry(eng, which, t, top):
            return eng.value_load(tab[which:which + 1, bass.ds(t.v, 1)], min_val=0, max_val=top)

        def split_behind(eng, t, split):
            if t.turn is None and t.n == 0:
                split(1, EXPW, t)
                return
            flag = entry(eng, TAB_SPLIT, t, 1)
            with eng.If(flag > 0):
                e, buf = entry(eng, TAB_EXPERT, t, E - 2), entry(eng, TAB_BUF, t, EXPW)
                split(e + 1, buf * -1 + EXPW, t)

        with nc.Block() as block:

            @block.sync
            def _(sp):
                def load_rows(t):
                    row = entry(sp, TAB_ROW, t, E * REGION)
                    if t.n >= 2:
                        sp.wait_ge(gates_r, t.v - 1)
                        sp.wait_ge(xT_t, t.v - 1)
                    sp.dma_start(x_moe[:, t.par, :], routed[bass.ds(row, P), :]).then_inc(rows_in[t.par], 16)

                def load_weights(e, buf):
                    sp.wait_ge(w13_lo, e - 1)
                    sp.wait_ge(w2_lo, e - 1)
                    sp.wait_ge(raw_loaded, e * 48)
                    sp.wait_ge(raw_loaded, 48)
                    load_expert(sp, e, buf)

                def load_behind(t):
                    flag = entry(sp, TAB_LOAD, t, 1)
                    with sp.If(flag > 0):
                        e, buf = entry(sp, TAB_EXPERT, t, E - 4), entry(sp, TAB_BUF, t, EXPW)
                        load_weights(e + 3, buf * -1 + EXPW)

                sp.wait_ge(raw_loaded, 48)
                load_expert(sp, 1, 1)
                for e in range(E):
                    n = sp.value_load(counts_i[0:1, e:e + 1], min_val=0, max_val=T)
                    sp.dma_start(routed[bass.ds(n + e * REGION, P), :], pad_rows[:]).then_inc(pads_out, 16)
                sp.wait_ge(pads_out, E * 16)
                load_rows(Tile(0))
                load_rows(Tile(1))
                load_weights(2, 0)
                load_rows(Tile(2))
                load_rows(Tile(3))
                load_weights(3, 1)
                with sp.Fori(0, (MOE_TILES - 3) // 2, 1) as turn:
                    for t in (Tile(4, turn), Tile(5, turn)):
                        load_rows(t)
                        load_behind(t.near(-3))

            @block.tensor
            def _(pe):
                def three(dst, a_hi, a_lo, b_hi, b_lo, first, last):
                    pe.matmul(dst, a_hi, b_hi, start=first, stop=False)
                    pe.matmul(dst, a_lo, b_hi, start=False, stop=False)
                    return pe.matmul(dst, a_hi, b_lo, start=False, stop=last)

                def x_transposes(t):
                    pe.wait_ge(rows_in[t.par], t.half * 16 + 16)
                    if t.n >= 1:
                        pe.wait_ge(xT_l, t.v)
                    for k in range(KD):
                        mm = pe.transpose(xT_ps[:, k * P:(k + 1) * P], x_moe[:, t.par, k * P:(k + 1) * P], ident)
                    mm.then_inc(xT_t, 1)

                def first_products(t):
                    e, buf = entry(pe, TAB_EXPERT, t, E - 1), entry(pe, TAB_BUF, t, EXPW)
                    pe.wait_ge(w13_lo, e + 1)
                    pe.wait_ge(xT_l, t.v + 1)
                    for n in range(4):
                        if t.n >= 1 and n == 0:
                            pe.wait_ge(gelu_r, t.v)
                        if t.n >= 1 and n == 2:
                            pe.wait_ge(hid_r, t.v)
                        for k in range(KD):
                            w = bass.ds(buf + (k * 2 * F + n * FH), FH)
                            mm = three(ps[:, n, 0:FH], xT_moe_hi[:, t.par, k, :], xT_moe_lo[:, t.par, k, :],
                                       w_moe_hi[:, w], w_moe_lo[:, w], k == 0, k == KD - 1)
                        if n % 2:
                            mm.then_inc((a_mm, b_mm)[n // 2], 1)

                def hid_transposes(t):
                    pe.wait_ge(hid_r, t.v + 1)
                    if t.n >= 1:
                        pe.wait_ge(hidT_l, t.v)
                    for k in range(KF):
                        mm = pe.transpose(hidT_ps[:, k * P:(k + 1) * P], hid_moe[:, k * P:(k + 1) * P], ident)
                    mm.then_inc(hidT_t, 1)

                def second_product(t):
                    e, buf = entry(pe, TAB_EXPERT, t, E - 1), entry(pe, TAB_BUF, t, EXPW)
                    pe.wait_ge(w2_lo, e + 1)
                    pe.wait_ge(hidT_l, t.v + 1)
                    if t.n >= 1:
                        pe.wait_ge(y_r, t.v)
                    for k in range(KF):
                        w = bass.ds(buf + (W13 + k * D), D)
                        mm = three(y_ps, hidT_hi[:, k, :], hidT_lo[:, k, :], w_moe_hi[:, w], w_moe_lo[:, w],
                                   k == 0, k == KF - 1)
                    mm.then_inc(y_mm, 1)

                def first(t):
                    x_transposes(t)
                    first_products(t)
                    x_transposes(t.near(1))
                    hid_transposes(t)

                def step(t):
                    first_products(t)
                    x_transposes(t.near(1))
                    second_product(t.near(-1))
                    hid_transposes(t)

                tiles(pe, first, step, second_product)

            @block.scalar
            def _(act):
                def split_hi(e, buf, t):
                    act.wait_ge(raw_loaded, e * 48 + 48)
                    if t is not None and t.n >= 1:
                        act.wait_ge(y_mm, t.v)
                    act.wait_ge(raw_loaded, 48)
                    for o, n in PIECES:
                        act.activation(w_moe_hi[:, bass.ds(buf + o, n)], raw[:, bass.ds(buf + o, n)], ACT.Copy).then_inc(we_hi, 1)

                def xT_split(t):
                    act.wait_ge(xT_t, t.v + 1)
                    if t.n >= 2:
                        act.wait_ge(b_mm, t.v - 1)
                    act.activation(xT_moe_hi[:, t.par].rearrange("p k n -> p (k n)"), xT_ps, ACT.Copy).then_inc(xT_h, 1)

                def gelu(t):
                    act.wait_ge(a_mm, t.v + 1)
                    if t.n >= 1:
                        act.wait_ge(hid_r, t.v)
                    act.activation(gelu_moe[:], ps[:, 0:2, 0:FH], ACT.Gelu).then_inc(gelu_r, 1)

                def hidT_split(t):
                    act.wait_ge(hidT_t, t.v + 1)
                    if t.n >= 1:
                        act.wait_ge(y_mm, t.v)
                    act.activation(hidT_hi[:].rearrange("p k n -> p (k n)"), hidT_ps, ACT.Copy).then_inc(hidT_h, 1)

                def first(t):
                    act.wait_ge(padding, 1)
                    split_hi(0, 0, None)
                    xT_split(t)
                    step(t)

                def step(t):
                    gelu(t)
                    xT_split(t.near(1))
                    hidT_split(t)
                    split_behind(act, t, split_hi)

                tiles(act, first, step, lambda t: None)

            @block.vector
            def _(v):
                def split_lo(e, buf, t):
                    for n, (o, size) in enumerate(PIECES[:2]):
                        v.wait_ge(we_hi, e * 3 + n + 1)
                        w = bass.ds(buf + o, size)
                        i = v.tensor_tensor(w_moe_lo[:, w], raw[:, w], f32(w_moe_hi[:, w]), ALU.subtract)
                    i.then_inc(w13_lo, 1)

                def take_gates(t):
                    e = entry(v, TAB_EXPERT, t, E - 1)
                    g, tok = gate_moe[:, t.par, :], x_moe[:, t.par, D + E:D + E + 1]
                    v.wait_ge(rows_in[t.par], t.half * 16 + 16)
                    v.tensor_scalar(g[:, 1:2], tok, float(S), None, ALU.is_ge)
                    v.tensor_copy(g[:, 0:1], x_moe[:, t.par, bass.ds(e + D, 1)]).then_inc(gate_steps, 1)
                    v.wait_ge(gate_steps, t.v * 2 + 1)
                    v.tensor_tensor(g[:, 2:3], g[:, 0:1], g[:, 1:2], ALU.mult).then_inc(gate_steps, 1)
                    v.wait_ge(gate_steps, t.v * 2 + 2)
                    v.tensor_tensor(g[:, 3:4], g[:, 0:1], g[:, 2:3], ALU.subtract)
                    if t.n >= 2:
                        v.wait_ge(added, (t.v - 1) * 16)
                    v.tensor_copy(tok_moe[:, t.par, :], tok).then_inc(gates_r, 1)

                def xT_rest(t):
                    v.wait_ge(xT_h, t.v + 1)
                    v.tensor_tensor(xT_moe_lo[:, t.par].rearrange("p k n -> p (k n)"), xT_ps,
                                    f32(xT_moe_hi[:, t.par].rearrange("p k n -> p (k n)")), ALU.subtract).then_inc(xT_l, 1)

                def multiply(t):
                    v.wait_ge(gelu_r, t.v + 1)
                    v.wait_ge(b_mm, t.v + 1)
                    if t.n >= 1:
                        v.wait_ge(hidT_t, t.v)
                    v.tensor_tensor(hid_moe[:, 0:F].rearrange("p (h n) -> p h n", h=2), ps[:, 2:4, 0:FH], gelu_moe[:],
                                    ALU.mult).then_inc(hid_r, 1)

                def gate_y(t):
                    v.wait_ge(y_mm, t.v + 1)
                    v.wait_ge(gates_r, t.v + 1)
                    if t.n >= 2:
                        v.wait_ge(added, (t.v - 1) * 16)
                    for b in range(B):
                        i = v.scalar_tensor_tensor(y_moe[:, t.par, b, :], y_ps, gate_moe[:, t.par, 3 - b:4 - b],
                                                   gates[:, b, 1, :], ALU.mult, ALU.mult)
                    i.then_inc(y_r, 1)

                def hidT_rest(t):
                    v.wait_ge(hidT_h, t.v + 1)
                    v.tensor_tensor(hidT_lo[:].rearrange("p k n -> p (k n)"), hidT_ps,
                                    f32(hidT_hi[:].rearrange("p k n -> p (k n)")), ALU.subtract).then_inc(hidT_l, 1)

                def first(t):
                    v.memset(hid_moe[:, F:KF * P], 0.0)
                    for b in range(2):
                        i = v.memset(raw[F_LAST:P, (b + 1) * EXPW - D:(b + 1) * EXPW], 0.0)
                    i.then_inc(padding, 1)
                    split_lo(0, 0, None)
                    take_gates(t)
                    xT_rest(t)
                    multiply(t)
                    xT_rest(t.near(1))
                    hidT_rest(t)
                    split_behind(v, t, split_lo)

                def step(t):
                    take_gates(t)
                    multiply(t)
                    xT_rest(t.near(1))
                    gate_y(t.near(-1))
                    hidT_rest(t)
                    split_behind(v, t, split_lo)

                tiles(v, first, step, gate_y)

            @block.gpsimd
            def _(g):
                def split_lo(e, buf, t):
                    g.wait_ge(we_hi, e * 3 + 3)
                    g.wait_ge(we_hi, 3)
                    w = bass.ds(buf + W13, W2)
                    g.tensor_tensor(w_moe_lo[:, w], raw[:, w], f32(w_moe_hi[:, w]), ALU.subtract).then_inc(w2_lo, 1)

                def add_rows(t):
                    g.wait_ge(y_r, t.v + 1)
                    g.tensor_tensor(y_moe[:, t.par, 0, :], y_moe[:, t.par, 0, :], y_moe[:, t.par, 1, :], ALU.add)\
                        .then_inc(y_sum, 1)
                    g.wait_ge(y_sum, t.v + 1)
                    if t.n >= 1:
                        g.wait_ge(added, t.v * 16)
                    mark(g)
                    g.indirect_dma_start(out, bass.IndirectOffsetOnAxis(ap=tok_moe[:, t.par, :], axis=0),
                                         y_moe[:, t.par, 0, :], None,
                                         compute_op=ALU.add).then_inc(added, 16)

                def first(t):
                    split_lo(0, 0, None)
                    step(t)

                def step(t):
                    split_behind(g, t, split_lo)
                    add_rows(t)

                tiles(g, first, step, lambda t: None)
                g.wait_ge(added, MOE_TILES * 16)


def kernel(**inputs):
    import concourse.bacc as bacc
    from concourse.bass_utils import run_bass_kernel_spmd

    a = {k: np.asarray(v) for k, v in inputs.items()}
    col = lambda v: v.reshape(-1, P).T
    arrays = {
        "x": a["L0_attn_x"],
        "gvd_t": np.concatenate([a["L0_attn_Wg"].T, a["L0_attn_Wv"].T, a["L0_attn_Wd"].T], axis=1),
        "gu_t": np.concatenate([a["L0_attn_W_gate"].T, a["L0_attn_W_up"].T], axis=1),
        "out_t": a["L0_attn_W_out"].T,
        "vecs": np.concatenate([col(a["L0_attn_bg"]), col(a["L0_attn_bv"]), col(a["L0_attn_bd"]),
                                col(a["L0_attn_rms_mix_w"]), col(a["L0_attn_rms_ffn_w"])], axis=1),
        "cond_t": a["L0_c"].T.reshape(KD, P, B).transpose(1, 0, 2),
        "wmod": a["L0_wmod"],
        "bias": a["L0_ffn_bias"],
        "router": a["L0_ffn_router_w"].reshape(KD, P, E).transpose(1, 0, 2),
        "w13": np.concatenate([a["L0_ffn_w1"], a["L0_ffn_v1"]], axis=2),
        "w2": a["L0_ffn_w2"],
        "consts": constants(),
    }
    arrays = {f"in_{k}": np.ascontiguousarray(v) for k, v in arrays.items()}
    nc = bacc.Bacc("TRN2", target_bir_lowering=False, num_devices=1)
    args = [nc.dram_tensor(k, v.shape, mybir.dt.from_np(v.dtype), kind="ExternalInput").ap() for k, v in arrays.items()]
    out = nc.dram_tensor("out_rows", (T + P, D), F32, kind="ExternalOutput").ap()
    adaln_moe_kernel(nc, *args, out)
    r = run_bass_kernel_spmd(nc, [arrays], core_ids=[0])
    return r.results[0]["out_rows"][:T].reshape(B, S, D)
```

```python
from contextlib import ExitStack

import numpy as np

import concourse.bass as bass
from concourse import mybir

P = 128
B, S, D = 2, 2048, 256
T = B * S
KD = D // P
BLK = 512
TPB = BLK // P
NBLK = T // BLK
FA = 768
KFA = FA // P
E, F, TOPK = 8, 704, 2
KF = -(-F // P)
F_LAST = F - (KF - 1) * P
assert 2 * F_LAST == P
FH = F // 2
ROW = D + E + 1
REGION = T + P
ROWS = E * REGION + P
MOE_TILES = (TOPK * T + E * (P - 1)) // P
SLOTS = 4
W13, W2 = KD * 2 * F, KF * D
EXPW = W13 + W2
EPS_LN, EPS_RMS = 1e-5, 1e-6

ALU = mybir.AluOpType
ACT = mybir.ActivationFunctionType
AX = mybir.AxisListType
F32, F32R = mybir.dt.float32, mybir.dt.float32r
BF16, I32, U32 = mybir.dt.bfloat16, mybir.dt.int32, mybir.dt.uint32

C_ID, C_TRI, C_IOTA, C_OFF, C_TOK, C_PAD = 0, P, 2 * P, 2 * P + TPB * E, 2 * P + TPB * E + E, 2 * P + TPB * E + E + B * TPB
C_TILE = C_PAD + 1
C_BUF = C_TILE + 1
C_N = C_BUF + E
V_BIAS, V_MIX, V_FFN, V_N = 0, 3 * KD, 4 * KD, 5 * KD
TAB_EXPERT, TAB_ROW, TAB_SPLIT, TAB_LOAD, TAB_BEFORE, TAB_BUF, TAB_N = 0, 1, 2, 3, 4, 5, 6
M_S1, M_A1, M_S2, M_A2, M_GBB, M_N = 0, 1, 2, 3, 4, 5


def constants():
    c = np.zeros((P, C_N), np.float32)
    p = np.arange(P)
    c[:, C_ID:C_ID + P] = np.eye(P)
    c[:, C_TRI:C_TRI + P] = p[:, None] < p[None, :]
    c[:, C_IOTA:C_IOTA + TPB * E] = np.tile(np.arange(E), TPB)
    c[:, C_OFF:C_OFF + E] = np.arange(E) * REGION
    for b in range(B):
        for i in range(TPB):
            c[:, C_TOK + b * TPB + i] = b * S + i * P + p
    c[:, C_PAD] = T + p
    c[:, C_TILE] = p
    c[:, C_BUF:C_BUF + E] = np.arange(E) % 2 * EXPW
    return c


class Block512:

    def __init__(self, n, turn=None):
        self.n, self.turn = n, turn
        self.par = n % 2
        self.v = n if turn is None else turn * 2 + n
        self.half = n // 2 if turn is None else turn + n // 2

    def near(self, d):
        return Block512(self.n + d, self.turn)


def ring_plan(banks):
    order = []
    for r in range(NBLK + 2):
        if r < NBLK:
            order += [("gvd", r, k) for k in range(3 * KD)]
        if r >= 2:
            order += [("out", r - 2, k) for k in range(2)]
        if 1 <= r <= NBLK:
            order += [("gu", r - 1, k) for k in range(2 * KFA)]
    return {u: (n % banks, order[n - banks] if n >= banks else None) for n, u in enumerate(order)}


def adaln_moe_kernel(nc, x, gvd_t, gu_t, out_t, vecs, cond_t, wmod, bias, router, w13, w2, consts, out):
    RING = 5
    ring = ring_plan(RING)
    ctx = ExitStack()
    base = (nc.sbuf_base + 63) // 64 * 64
    place = [base]

    def at(name, shape, dt, offset=None):
        size = int(np.prod(shape[1:])) * (2 if dt == BF16 else 4)
        if offset is None:
            offset = place[0]
            place[0] = (offset + size + 31) // 32 * 32
        return nc.alloc_sbuf_tensor_at(name, shape, dt, offset=offset)

    with ctx:
        def sem(name):
            return ctx.enter_context(nc.semaphore(name))

        raw = at("raw", [P, 2 * EXPW], F32, base)
        keep = ((C_N + B * 2 * D + P + E + ROW + 2) * 4 + 6 * 32 + 31) // 32 * 32
        top_at = nc.sbuf_usable_end // 32 * 32 - keep
        place[0] = top_at
        cn = at("cn", [P, C_N], F32)
        gates = at("gates", [P, B, 2, D], F32)
        tab = at("tab", [P, P], I32)
        counts_i = at("counts_i", [P, E], I32)
        pad_rows = at("pad_rows", [P, ROW], F32)
        g_mark = at("g_mark", [P, 1], F32)
        place[0] = base + 2 * EXPW * 4
        w_moe_hi, w_moe_lo = (at(f"w_moe_{s}", [P, 2 * EXPW], F32R) for s in ("hi", "lo"))
        x_moe = at("x_moe", [P, SLOTS, ROW], F32)
        xT_moe_hi, xT_moe_lo = (at(f"xT_moe_{s}", [P, 2, KD, P], F32R) for s in ("hi", "lo"))
        gelu_moe = at("gelu_moe", [P, 2, FH], F32)
        hid_moe = at("hid_moe", [P, KF * P], F32)
        hidT_hi, hidT_lo = at("hidT_hi", [P, KF, P], F32R), at("hidT_lo", [P, KF - 1, P], F32R)
        y_moe = at("y_moe", [P, SLOTS, 2, D], F32)
        gate_moe = at("gate_moe", [P, SLOTS, 4], F32)
        tok_moe = at("tok_moe", [P, SLOTS, 1], I32)
        assert place[0] <= top_at
        place[0] = base
        gvd_raw = at("gvd_raw", [P, KD, 3 * D], F32)
        assert place[0] <= base + EXPW * 4
        place[0] = base + EXPW * 4
        gvd_hi, gvd_lo = (at(f"gvd_{s}", [P, KD, 3 * D], F32R) for s in ("hi", "lo"))
        gu_hi, gu_lo = (at(f"gu_{s}", [P, KD, 2 * FA], F32R) for s in ("hi", "lo"))
        out_hi, out_lo = (at(f"out_{s}", [P, KFA, D], F32R) for s in ("hi", "lo"))
        hid_at = place[0]
        hid_hi, hid_lo = (at(f"hid_{s}", [P, KFA, BLK], F32R) for s in ("hi", "lo"))
        gu_raw = at("gu_raw", [P, KD, 2 * FA], F32, hid_at)
        wmod_sb = at("wmod_sb", [P, KD, 6 * D], F32, hid_at + KD * 2 * FA * 4)
        out_raw = at("out_raw", [P, KFA * D], F32, base + KD * 3 * D * 4)
        assert hid_at + 2 * KD * 2 * FA * 4 <= place[0]
        xnT_hi, xnT_lo = (at(f"xnT_{s}", [P, KD, BLK], F32R) for s in ("hi", "lo"))
        xn2T_hi, xn2T_lo = (at(f"xn2T_{s}", [P, KD, BLK], F32R) for s in ("hi", "lo"))
        mod = at("mod", [P, B, M_N, D], F32)
        x_sb = at("x_sb", [P, TPB, D], F32)
        x_again = at("x_again", [P, TPB, D], F32)
        h_sb = at("h_sb", [P, 2, TPB, D], F32)
        xa_sb = at("xa_sb", [P, 2, TPB, D], F32)
        g_raw = at("g_raw", [P, B * 2 * D], F32, place[0])
        xo_sb = at("xo_sb", [P, TPB, D], F32)
        xn_sb = at("xn_sb", [P, TPB, D], F32)
        sg_sb = at("sg_sb", [P, KD, BLK], F32)
        tv_sb = at("tv_sb", [P, KD, BLK], F32)
        dec_sb = at("dec_sb", [P, KD, BLK], F32)
        sig_sb = at("sig_sb", [P, 2, BLK], F32)
        gg_sb = at("gg_sb", [P, 2, BLK], F32)
        hf_sb = at("hf_sb", [P, 2, BLK], F32)
        rows = at("rows", [P, 2, TPB, ROW], F32)
        ct_rep = at("ct_rep", [P, KD * B, P], F32, place[0])
        hT_sb = at("hT_sb", [P, KD, BLK], F32)
        squares = at("squares", [P, TPB, D], F32)
        squares2 = at("squares2", [P, TPB, D], F32)
        vec = at("vec", [P, V_N], F32)
        rw_sb = at("rw_sb", [P, KD, E], F32)
        bias_row = at("bias_row", [P, D], F32)
        ct = at("ct", [P, KD, B], F32)
        ct_sig = at("ct_sig", [P, KD, B], F32)
        carry = at("carry", [P, B, KD], F32)
        tri = at("tri", [P, P], BF16)
        ones = at("ones", [P, P], BF16)
        ones_f = at("ones_f", [P, E], F32)
        minus_half = at("minus_half", [P, TPB], F32)
        eps_ln = at("eps_ln", [P, TPB], F32)
        eps_rms = at("eps_rms", [P, TPB], F32)
        stats = at("stats", [P, TPB, 6], F32)
        mv = at("mv", [P, TPB, 2], F32)
        ve = at("ve", [P, TPB], F32)
        rstd = at("rstd", [P, TPB], F32)
        ssq = at("ssq", [P, TPB], F32)
        ms = at("ms", [P, TPB], F32)
        rms = at("rms", [P, TPB], F32)
        ssq2 = at("ssq2", [P, TPB], F32)
        ms2 = at("ms2", [P, TPB], F32)
        rms2 = at("rms2", [P, TPB], F32)
        stats2 = at("stats2", [P, TPB, 6], F32)
        mv2 = at("mv2", [P, TPB, 2], F32)
        ve2 = at("ve2", [P, TPB], F32)
        rstd2 = at("rstd2", [P, TPB], F32)
        mx = at("mx", [P, TPB], F32)
        zz = at("zz", [P, TPB, E], F32)
        ee = at("ee", [P, TPB, E], F32)
        pp = at("pp", [P, TPB, E], F32)
        top = at("top", [P, TPB, E], F32)
        top_i = at("top_i", [P, TPB, E], U32)
        top_f = at("top_f", [P, TPB, 2], F32)
        hot = at("hot", [P, 2, TPB, E], F32)
        chosen = at("chosen", [P, TPB, E], F32)
        chosen_b = at("chosen_b", [P, TPB, E], BF16)
        seen = at("seen", [P, E], F32)
        seen_add = at("seen_add", [P, E], F32)
        seen_b = at("seen_b", [P, E], BF16)
        pos = at("pos", [P, TPB, E], F32)
        pos_k = at("pos_k", [P, 2, TPB, E], F32)
        slot_f = at("slot_f", [P, 2, TPB], F32)
        slot_i = at("slot_i", [P, 2, 2, TPB], I32)
        tok_f = at("tok_f", [P, B, TPB], F32)
        counts = at("counts", [P, E], F32)
        tiles_i = at("tiles_i", [P, E], I32)
        tiles_f = at("tiles_f", [P, E], F32)
        tiles_end = at("tiles_end", [P, E], F32)
        step_e = at("step_e", [P, E], F32)
        passed = at("passed", [P, E], F32)
        jump = at("jump", [P, E], F32)
        turn_mark = at("turn_mark", [P, 1], F32)
        tcol = at("tcol", [P, 2], F32)
        tcol2 = at("tcol2", [P, TAB_N], F32)
        meets, to_split, to_load, load_to = (at(n, [P, E], F32) for n in ("meets", "to_split", "to_load", "load_to"))
        assert place[0] <= top_at

        ident = cn[:, C_ID:C_ID + P]

        ps = ctx.enter_context(nc.psum_tensor("ps", [P, 8, BLK], F32))
        tp = [ps[:, RING, :], ps[:, RING + 1, :]]
        rt = ps[:, RING + 2, :]
        logits = rt[:, 0:TPB * E].rearrange("p (i e) -> p i e", e=E)
        ranks = rt[:, 64:64 + TPB * E].rearrange("p (i e) -> p i e", e=E)
        total = rt[:, 128:128 + E]

        routed = nc.dram_tensor("routed", [ROWS, ROW], F32, kind="Internal").ap()
        xf = x.rearrange("b s d -> (b s) d")

        consts_in, mod_in, raw_in = sem("consts_in"), sem("mod_in"), [sem(f"raw_in{n}") for n in range(3)]
        small_ready = sem("small_ready")
        cond_sig, cond_act, cond_rep = sem("cond_sig"), sem("cond_act"), sem("cond_rep")
        mod_mm, mod_rows = sem("mod_mm"), sem("mod_rows")
        w_hi, w_lo = ([sem(f"{n}_{part}") for n in ("gvd_w", "gu_w", "out_w")] for part in ("hi", "lo"))
        gu_scaled = sem("gu_scaled")
        rows_copied = sem("rows_copied")
        raw_loaded, LOAD = sem("raw_loaded"), 16 * (2 + P // F_LAST)
        x_in = sem("x_in")
        bn, aggr, var_eps, rstd_r = sem("bn"), sem("aggr"), sem("var_eps"), sem("rstd_r")
        xh, h_ready = sem("xh"), sem("h_ready")
        ssq_r, ms_r, rms_r, xn_r = sem("ssq_r"), sem("ms_r"), sem("rms_r"), sem("xn_r")
        xnT_t, xnT_h, xnT_l = sem("xnT_t"), sem("xnT_h"), sem("xnT_l")
        gvd_mm, gvd_act = sem("gvd_mm"), sem("gvd_act")
        xs_r, dec_r, scanned, carried = sem("xs_r"), sem("dec_r"), sem("scanned"), sem("carried")
        sT_t, xa_r = sem("sT_t"), sem("xa_r")
        ssq2_r, ms2_r, rms2_r, xn2_r = sem("ssq2_r"), sem("ms2_r"), sem("rms2_r"), sem("xn2_r")
        xn2T_t, xn2T_h, xn2T_l = sem("xn2T_t"), sem("xn2T_h"), sem("xn2T_l")
        gu_mm = sem("gu_mm")
        sig_r, gg_r, hf_r, hid_h, hid_l = (sem(n) for n in ("sig_r", "gg_r", "hf_r", "hid_h", "hid_l"))
        out_mm, xo_r = sem("out_mm"), sem("xo_r")
        x_again_in = sem("x_again_in")
        xg_r, x1_r = sem("xg_r"), sem("x1_r")
        bn2, aggr2, var_eps2, rstd2_r = sem("bn2"), sem("aggr2"), sem("var_eps2"), sem("rstd2_r")
        xh2, h2_ready = sem("xh2"), sem("h2_ready")
        base_r, base_out = sem("base_r"), sem("base_out")
        hT_t, hT_c = sem("hT_t"), sem("hT_c")
        logit_mm, z_r, exp_r, rank_mm = sem("logit_mm"), sem("z_r"), sem("exp_r"), sem("rank_mm")
        route, chosen_r, slots_r = sem("route"), sem("chosen_r"), sem("slots_r")
        scattered = [sem("scattered0"), sem("scattered1")]
        total_mm, tabs, tab_t, tab_ready = (sem(n) for n in ("total_mm", "tabs", "tab_t", "tab_ready"))
        TABS = 11
        slot_steps = sem("slot_steps")
        counted, pads_out = sem("counted"), sem("pads_out")
        we_hi, w13_lo, w2_lo, y_mm = sem("we_hi"), sem("w13_lo"), sem("w2_lo"), sem("y_mm")

        freed = {"gvd": (gvd_act, 3 * KD), "out": (xo_r, 2)}

        def bank(kind, q, k):
            return ps[:, ring[kind, q.n, k][0], :]

        def wait_bank(eng, kind, q, k):
            last = ring[kind, q.n, k][1]
            if last is None:
                return
            lk, ln, i = last
            lq = q.near(ln - q.n)
            if lk == "gu":
                eng.wait_ge((gg_r, hf_r)[i % 2], lq.v * KFA + i // 2 + 1)
            else:
                eng.wait_ge(freed[lk][0], lq.v * freed[lk][1] + i + 1)

        def load_expert(eng, e, buf):
            def halves(ap):
                return ap if isinstance(e, int) else ap.rearrange("e a b -> (e a) b")

            o = buf * EXPW if isinstance(buf, int) else buf
            a = w13[e] if isinstance(e, int) else halves(w13)[bass.ds(e * D, D), :]
            b = w2[e] if isinstance(e, int) else halves(w2)[bass.ds(e * F, F), :]
            eng.dma_start(raw[:, bass.ds(o, W13)].rearrange("p (k n) -> p k n", k=KD),
                          a.rearrange("(k p) n -> p k n", p=P)).then_inc(raw_loaded, 16)
            eng.dma_start(raw[:, bass.ds(o + W13, W2 - D)].rearrange("p (k n) -> p k n", k=KF - 1),
                          b[0:(KF - 1) * P, :].rearrange("(k p) n -> p k n", p=P)).then_inc(raw_loaded, 16)
            for p in range(0, P, F_LAST):
                eng.dma_start(raw[p:p + F_LAST, bass.ds(o + EXPW - D, D)], b[(KF - 1) * P:F, :]).then_inc(raw_loaded, 16)

        PIECES = [(0, 2 * F), (2 * F, 2 * F), (W13, W2)]

        def split_w13_hi(act, e, buf, t=None):
            act.wait_ge(raw_loaded, e * LOAD + LOAD)
            if t is not None:
                act.wait_ge(y_mm, t.v)
                act.wait_ge(raw_loaded, LOAD)
            for o, n in PIECES[:2]:
                act.activation(w_moe_hi[:, bass.ds(buf + o, n)], raw[:, bass.ds(buf + o, n)], ACT.Copy).then_inc(we_hi, 1)

        def split_w2_hi(act, e, buf, t=None):
            act.activation(w_moe_hi[:, bass.ds(buf + W13, W2)], raw[:, bass.ds(buf + W13, W2)], ACT.Copy).then_inc(we_hi, 1)

        def split_w13_lo(v, e, buf, t=None):
            for n, (o, size) in enumerate(PIECES[:2]):
                v.wait_ge(we_hi, e * 3 + n + 1)
                w = bass.ds(buf + o, size)
                i = v.tensor_tensor(w_moe_lo[:, w], raw[:, w], f32(w_moe_hi[:, w]), ALU.subtract)
            i.then_inc(w13_lo, 1)

        def split_w2_lo(g, e, buf, t=None):
            g.wait_ge(we_hi, e * 3 + 3)
            if t is not None:
                g.wait_ge(we_hi, 3)
            w = bass.ds(buf + W13, W2)
            g.tensor_tensor(w_moe_lo[:, w], raw[:, w], f32(w_moe_hi[:, w]), ALU.subtract).then_inc(w2_lo, 1)

        def load_weights(sp, before, e, buf):
            sp.wait_ge(raw_loaded, e * LOAD)
            sp.wait_ge(w13_lo, before)
            sp.wait_ge(w2_lo, before)
            if not isinstance(e, int):
                sp.wait_ge(raw_loaded, LOAD)
            load_expert(sp, e, buf)

        def hidden_lo(eng, q, m):
            eng.wait_ge(hid_h, q.v * KFA + m + 1)
            eng.tensor_tensor(hid_lo[:, m, :], hf_sb[:, m % 2, :], f32(hid_hi[:, m, :]), ALU.subtract).then_inc(hid_l, 1)

        def pad_experts(eng, experts):
            eng.wait_ge(counted, 1)
            for e in experts:
                n = eng.value_load(counts_i[0:1, e:e + 1], min_val=0, max_val=T)
                eng.dma_start(routed[bass.ds(n + e * REGION, P), :], pad_rows[:]).then_inc(pads_out, 16)

        def mark(g):
            g.tensor_tensor(g_mark[:], cn[:, 0:1], cn[:, 0:1], ALU.add)

        MOD_UNITS = [(0, 0), (1, 0), (0, 1), (0, 2), (1, 1), (1, 2)]

        def mod_ps(b, n):
            return ps[:, 3 * b + n // 2, (n % 2) * D:(n % 2 + 1) * D]

        def f32(ap):
            return ap.bitcast(F32)

        def body(step, stages):
            for r in range(-1, 3):
                step(r, None)
            with stages.Fori(0, 2, 1) as turn:
                step(3, turn)
                step(4, turn)
            for r in range(7, NBLK + 3):
                step(r, None)

        block = ctx.enter_context(nc.Block())

        @block.sync
        def _(sp):
            def load_x(q):
                if q.n >= 1:
                    sp.wait_ge(xh, q.v)
                sp.dma_start(x_sb[:], xf[bass.ds(q.half * BLK + q.par * S, BLK), :]
                             .rearrange("(i p) d -> p i d", p=P)).then_inc(x_in, 16)

            def load_x_again(q):
                if q.n >= 1:
                    sp.wait_ge(base_out, q.v * 16)
                sp.dma_start(x_again[:], xf[bass.ds(q.half * BLK + q.par * S, BLK), :]
                             .rearrange("(i p) d -> p i d", p=P)).then_inc(x_again_in, 16)

            sp.dma_start(ct[:], cond_t).then_inc(mod_in, 16)
            sp.dma_start(wmod_sb[:], wmod.rearrange("(k p) n -> p k n", p=P)).then_inc(mod_in, 16)
            sp.dma_start(cn[:], consts).then_inc(consts_in, 16)
            sp.dma_start(vec[:], vecs).then_inc(consts_in, 16)
            sp.dma_start(bias_row[:], bias.partition_broadcast(P)).then_inc(consts_in, 16)
            sp.dma_start(rw_sb[:], router).then_inc(consts_in, 16)
            load_x(Block512(0))
            sp.dma_start(gvd_raw[:], gvd_t.rearrange("(k p) n -> p k n", p=P)).then_inc(raw_in[0], 16)
            sp.dma_start(gu_raw[:], gu_t.rearrange("(k p) n -> p k n", p=P)).then_inc(raw_in[1], 16)
            sp.dma_start(out_raw[:].rearrange("p (k n) -> p k n", k=KFA),
                         out_t.rearrange("(k p) n -> p k n", p=P)).then_inc(raw_in[2], 16)

            def step(r, turn):
                q = Block512(r, turn)
                if 1 <= r + 1 < NBLK:
                    load_x(q.near(1))
                if r == 2:
                    sp.wait_ge(w_lo[0], 1)
                    sp.wait_ge(w_lo[2], 1)
                    load_expert(sp, 0, 0)
                if 2 <= r < NBLK + 2:
                    load_x_again(q.near(-2))

            body(step, sp)
            sp.wait_ge(out_mm, NBLK * 2)
            sp.wait_ge(raw_loaded, LOAD)
            load_expert(sp, 1, 1)
            load_weights(sp, 1, 2, 0)
            pad_experts(sp, range(0, E, 2))
            sp.wait_ge(base_out, NBLK * 16)
            sp.wait_ge(pads_out, E * 16)

        @block.tensor
        def _(pe):
            def three(dst, a_hi, a_lo, b_hi, b_lo, first, last):
                pe.matmul(dst, a_hi, b_hi, start=first, stop=False)
                pe.matmul(dst, a_lo, b_hi, start=False, stop=False)
                return pe.matmul(dst, a_hi, b_lo, start=False, stop=last)

            pe.wait_ge(mod_in, 32)
            pe.wait_ge(cond_rep, 1)
            for b, n in MOD_UNITS:
                for k in range(KD):
                    mm = pe.matmul(ps[:, 3 * b + n, :], ct_rep[:, k * B + b, :],
                                   wmod_sb[:, k, n * BLK:(n + 1) * BLK], start=(k == 0), stop=(k == KD - 1))
                mm.then_inc(mod_mm, 1)

            def xn_transposes(q):
                pe.wait_ge(xn_r, q.v + 1)
                for c in range(KD):
                    if q.n >= 4:
                        pe.wait_ge(hT_c, (q.v - 4) * KD + c + 1)
                    elif q.n >= 2:
                        pe.wait_ge(xn2T_l, (q.v - 2) * KD + c + 1)
                    elif q.n >= 1:
                        pe.wait_ge(xnT_l, (q.v - 1) * KD + c + 1)
                    for i in range(TPB):
                        mm = pe.transpose(tp[c][:, i * P:(i + 1) * P], xn_sb[:, i, c * P:(c + 1) * P], ident)
                    mm.then_inc(xnT_t, 1)

            def gvd(q, units):
                for n in units:
                    kind, c = n % 3, n // 3
                    wait_bank(pe, "gvd", q, n)
                    if n == 0:
                        pe.wait_ge(xnT_l, (q.v + 1) * KD)
                    w = slice(kind * D + c * P, kind * D + (c + 1) * P)
                    for k in range(KD):
                        mm = three(bank("gvd", q, n), gvd_hi[:, k, w], gvd_lo[:, k, w],
                                   xnT_hi[:, k, :], xnT_lo[:, k, :], k == 0, k == KD - 1)
                    mm.then_inc(gvd_mm, 1)

            def state_transposes(q):
                pe.wait_ge(carried, (q.v + 1) * KD)
                for u in range(2):
                    if q.n + 1 < NBLK:
                        pe.wait_ge(xnT_l, (q.v + 1) * KD + u + 1)
                    else:
                        pe.wait_ge(hT_c, (q.v - 3) * KD + u + 1)
                    for i in range(2):
                        for c in range(KD):
                            t = (2 * u + i) * P
                            mm = pe.transpose(tp[u][:, i * D + c * P:i * D + (c + 1) * P],
                                              sg_sb[:, c, t:t + P], ident)
                    mm.then_inc(sT_t, 1)

            def xn2_transposes(q):
                pe.wait_ge(xn2_r, q.v + 1)
                for c in range(KD):
                    pe.wait_ge(xa_r, q.v * 2 + c + 1)
                    for i in range(TPB):
                        mm = pe.transpose(tp[c][:, i * P:(i + 1) * P], xn_sb[:, i, c * P:(c + 1) * P], ident)
                    mm.then_inc(xn2T_t, 1)

            def gate_up(q, m):
                if m == 0:
                    pe.wait_ge(xn2T_l, (q.v + 1) * KD)
                for j in range(2):
                    n = 2 * m + j
                    wait_bank(pe, "gu", q, n)
                    w = slice(j * FA + m * P, j * FA + (m + 1) * P)
                    for k in range(KD):
                        mm = three(bank("gu", q, n), gu_hi[:, k, w], gu_lo[:, k, w],
                                   xn2T_hi[:, k, :], xn2T_lo[:, k, :], k == 0, k == KD - 1)
                    mm.then_inc(gu_mm, 1)

            def ffn_out(q, u):
                wait_bank(pe, "out", q, u)
                if u == 0:
                    pe.wait_ge(hid_l, (q.v + 1) * KFA)
                for i in range(2):
                    t = slice((2 * u + i) * P, (2 * u + i + 1) * P)
                    for k in range(KFA):
                        mm = three(bank("out", q, u)[:, i * D:(i + 1) * D], hid_hi[:, k, t], hid_lo[:, k, t],
                                   out_hi[:, k, :], out_lo[:, k, :], k == 0, k == KFA - 1)
                mm.then_inc(out_mm, 1)

            def h2_transposes(q):
                pe.wait_ge(h2_ready, q.v + 1)
                for c in range(KD):
                    if q.n + 2 < NBLK:
                        pe.wait_ge(xn2T_l, (q.v + 2) * KD + c + 1)
                    else:
                        pe.wait_ge(hT_c, (q.v - 1) * KD + c + 1)
                    for i in range(TPB):
                        mm = pe.transpose(tp[c][:, i * P:(i + 1) * P], rows[:, q.par, i, c * P:(c + 1) * P], ident)
                    mm.then_inc(hT_t, 1)

            def router_logits(q):
                pe.wait_ge(hT_c, (q.v + 1) * KD)
                pe.wait_ge(slots_r, q.v + 1)
                for i in range(TPB):
                    for k in range(KD):
                        mm = pe.matmul(logits[:, i, :], hT_sb[:, k, i * P:(i + 1) * P], rw_sb[:, k, :],
                                       start=(k == 0), stop=(k == KD - 1))
                mm.then_inc(logit_mm, 1)

            def rank_tokens(q):
                pe.wait_ge(chosen_r, q.v + 1)
                for i in range(TPB):
                    pe.matmul(ranks[:, i, :], tri[:], chosen_b[:, i, :], start=True, stop=False)
                    for j in range(i):
                        pe.matmul(ranks[:, i, :], ones[:], chosen_b[:, j, :], start=False, stop=False)
                    mm = pe.matmul(ranks[:, i, :], ones[:], seen_b[:], start=False, stop=True)
                mm.then_inc(rank_mm, 1)

            def step(r, turn):
                q = Block512(r, turn)
                routing, adding, ffn = q.near(-3), q.near(-2), q.near(-1)
                if r == -1:
                    pe.wait_ge(mod_rows, 3)
                    pe.wait_ge(rows_copied, 1)
                if r == 0:
                    pe.wait_ge(w_lo[0], 1)
                if 0 <= r < NBLK:
                    gvd(q, [0, 1])
                if r >= 3:
                    h2_transposes(routing)
                if 0 <= r < NBLK:
                    gvd(q, [2, 3])
                if r >= 3:
                    router_logits(routing)
                if 0 <= r < NBLK:
                    gvd(q, [4, 5])
                if 2 <= r < NBLK + 2:
                    if r == 2:
                        pe.wait_ge(w_lo[2], 1)
                    ffn_out(adding, 0)
                if r + 1 < NBLK:
                    xn_transposes(q.near(1))
                if r >= 3:
                    rank_tokens(routing)
                if 2 <= r < NBLK + 2:
                    ffn_out(adding, 1)
                if r == 1:
                    pe.wait_ge(w_lo[1], 1)
                for m in range(KFA):
                    if m == 1 and 0 <= r < NBLK:
                        state_transposes(q)
                    if m == 4 and 0 <= r < NBLK:
                        xn2_transposes(q)
                    if 1 <= r <= NBLK:
                        gate_up(ffn, m)

            pe.wait_ge(consts_in, 64)
            body(step, pe)
            pe.wait_ge(slots_r, NBLK + 1)
            pe.matmul(total, ones[:], seen_b[:], start=True, stop=True).then_inc(total_mm, 1)
            pe.wait_ge(tabs, TABS)
            pe.transpose(tp[0][0:TAB_N, 0:P], tcol2[:], ident).then_inc(tab_t, 1)

        @block.scalar
        def _(act):
            act.wait_ge(mod_in, 32)
            act.activation(ct_sig[:], ct[:], ACT.Sigmoid).then_inc(cond_sig, 1)
            def copy_rows():
                act.wait_ge(mod_mm, 5)
                for b in range(B):
                    act.activation(g_raw[:, (2 * b) * D:(2 * b + 1) * D], mod_ps(b, 2), ACT.Copy)
                    i = act.activation(mod[:, b, M_S2, :], mod_ps(b, 3), ACT.Copy)
                i.then_inc(rows_copied, 1)

            def split_gvd():
                act.wait_ge(consts_in, 64)
                act.wait_ge(raw_in[0], 16)
                for k in range(KD):
                    i = act.activation(gvd_hi[:, k, :], gvd_raw[:, k, :], ACT.Identity, scale=vec[:, V_MIX + k:V_MIX + k + 1])
                i.then_inc(w_hi[0], 1)

            def split_gu_out():
                act.wait_ge(raw_in[1], 16)
                for k in range(KD):
                    act.activation(gu_raw[:, k, :], gu_raw[:, k, :], ACT.Identity,
                                   scale=vec[:, V_FFN + k:V_FFN + k + 1]).then_inc(gu_scaled, 1)
                for k in range(KD):
                    act.wait_ge(gu_scaled, k + 1)
                    i = act.activation(gu_hi[:, k, :], gu_raw[:, k, :], ACT.Copy)
                i.then_inc(w_hi[1], 1)
                act.wait_ge(raw_in[2], 16)
                act.activation(out_hi[:].rearrange("p k n -> p (k n)"), out_raw[:], ACT.Copy).then_inc(w_hi[2], 1)

            def mean_squares(q, squares, src, ready, count, dst, done):
                act.wait_ge(ready, count)
                for i in range(TPB):
                    a = act.activation(squares[:, i, :], src[:, i, :], ACT.Square, scale=D ** -0.5, accum_out=dst[:, i:i + 1])
                a.then_inc(done, 1)

            def front(q):
                if q.n >= 1:
                    act.wait_ge(rms_r, q.v)
                mean_squares(q, squares, h_sb[:, q.par], h_ready, q.v + 1, ssq, ssq_r)

            def xn(q):
                act.wait_ge(rms_r, q.v + 1)
                if q.n >= 2:
                    act.wait_ge(xn2T_t, (q.v - 1) * KD)
                elif q.n >= 1:
                    act.wait_ge(xnT_t, KD)
                for i in range(TPB):
                    a = act.activation(xn_sb[:, i, :], h_sb[:, q.par, i, :], ACT.Copy, scale=rms[:, i:i + 1])
                a.then_inc(xn_r, 1)

            def store_base(q):
                act.wait_ge(base_r, q.v + 1)
                act.dma_start(out[bass.ds(q.half * BLK + q.par * S, BLK), :]
                              .rearrange("(i p) d -> p i d", p=P), x_again[:]).then_inc(base_out, 16)

            def xn_hi(q):
                for c in range(KD):
                    act.wait_ge(xnT_t, q.v * KD + c + 1)
                    if c == 0 and q.n >= 1:
                        act.wait_ge(gvd_mm, q.v * 3 * KD)
                    act.activation(xnT_hi[:, c, :], tp[c], ACT.Copy).then_inc(xnT_h, 1)

            def gvd_activations(q, units):
                for n in units:
                    kind, c = n % 3, n // 3
                    act.wait_ge(gvd_mm, q.v * 3 * KD + n + 1)
                    if q.n >= 1 and kind == 0:
                        act.wait_ge(sT_t, q.v * 2)
                    if q.n >= 1 and kind == 1:
                        act.wait_ge(scanned, (q.v - 1) * KD + c + 1)
                    dst = (sg_sb, tv_sb, dec_sb)[kind]
                    act.activation(dst[:, c, :], bank("gvd", q, n), (ACT.Sigmoid, ACT.Tanh, ACT.Sigmoid)[kind],
                                   bias=vec[:, V_BIAS + kind * KD + c:V_BIAS + kind * KD + c + 1]).then_inc(gvd_act, 1)

            def middle(q):
                if q.n >= 1:
                    act.wait_ge(rms2_r, q.v)
                mean_squares(q, squares2, xa_sb[:, q.par], xa_r, 2 * q.v + 2, ssq2, ssq2_r)

            def xn2(q):
                act.wait_ge(rms2_r, q.v + 1)
                act.wait_ge(xnT_t, (q.v + 2) * KD if q.n + 1 < NBLK else NBLK * KD)
                for i in range(TPB):
                    a = act.activation(xn_sb[:, i, :], xa_sb[:, q.par, i, :], ACT.Copy, scale=rms2[:, i:i + 1])
                a.then_inc(xn2_r, 1)

            def xn2_hi(q):
                for c in range(KD):
                    act.wait_ge(xn2T_t, q.v * KD + c + 1)
                    if c == 0 and q.n >= 1:
                        act.wait_ge(gu_mm, q.v * 2 * KFA)
                    act.activation(xn2T_hi[:, c, :], tp[c], ACT.Copy).then_inc(xn2T_h, 1)

            def gate_sigmoid(q, m):
                act.wait_ge(gu_mm, q.v * 2 * KFA + 2 * m + 1)
                if q.n >= 1 or m >= 2:
                    act.wait_ge(gg_r, q.v * KFA + m - 1)
                act.activation(sig_sb[:, m % 2, :], bank("gu", q, 2 * m), ACT.Sigmoid).then_inc(sig_r, 1)

            def hidden_hi(q, m):
                act.wait_ge(hf_r, q.v * KFA + m + 1)
                if m == 0 and q.n >= 1:
                    act.wait_ge(out_mm, q.v * 2)
                act.activation(hid_hi[:, m, :], hf_sb[:, m % 2, :], ACT.Copy).then_inc(hid_h, 1)

            def h2_copy(q):
                for c in range(KD):
                    act.wait_ge(hT_t, q.v * KD + c + 1)
                    if c == 0:
                        act.wait_ge(slots_r, q.v + 1)
                    act.activation(hT_sb[:, c, :], tp[c], ACT.Copy).then_inc(hT_c, 1)

            def router_exp(q):
                act.wait_ge(z_r, q.v + 1)
                act.activation(ee[:], zz[:], ACT.Exp).then_inc(exp_r, 1)

            def step(r, turn):
                q = Block512(r, turn)
                nxt, routing, ffn = q.near(1), q.near(-3), q.near(-1)
                gvd_on, ffn_on = 0 <= r < NBLK, 1 <= r <= NBLK
                if r == -1:
                    split_gvd()
                if gvd_on:
                    gvd_activations(q, [0, 1])
                if r == NBLK + 2:
                    act.wait_ge(out_mm, NBLK * 2)
                    split_w13_hi(act, 0, 0)
                    split_w2_hi(act, 0, 0)
                if r >= 3:
                    h2_copy(routing)
                if gvd_on:
                    gvd_activations(q, [2])
                if r >= 3:
                    store_base(routing)
                if r == NBLK + 2:
                    split_w13_hi(act, 1, EXPW)
                    split_w2_hi(act, 1, EXPW)
                if r >= 3:
                    router_exp(routing)
                if r + 1 < NBLK:
                    front(nxt)
                if gvd_on:
                    gvd_activations(q, [3, 4, 5])
                if r + 1 < NBLK:
                    xn(nxt)
                if r == -1:
                    copy_rows()
                if r + 1 < NBLK:
                    xn_hi(nxt)
                if r == -1:
                    split_gu_out()
                for m in range(KFA):
                    if ffn_on:
                        gate_sigmoid(ffn, m)
                    if m == 1 and gvd_on:
                        middle(q)
                    if ffn_on and m >= 1:
                        hidden_hi(ffn, m - 1)
                    if m == 2 and gvd_on:
                        xn2(q)
                if gvd_on:
                    xn2_hi(q)
                if ffn_on:
                    hidden_hi(ffn, KFA - 1)

            body(step, act)
            pad_experts(act, range(1, E, 2))

        @block.vector
        def _(v):
            def chain(counter, at_value):
                n = [0]

                def link(i):
                    n[0] += 1
                    i.then_inc(counter, 1)
                    v.wait_ge(counter, at_value + n[0])
                return link

            v.memset(ones[:], 1.0)
            v.memset(ones_f[:], 1.0)
            v.memset(minus_half[:], -0.5)
            v.memset(eps_ln[:], EPS_LN)
            v.memset(eps_rms[:], EPS_RMS)
            v.memset(carry[:], 0.0)
            v.memset(seen[:], 0.0)
            v.memset(seen_b[:], 0.0).then_inc(slots_r, 1)
            v.memset(pad_rows[:], 0.0).then_inc(small_ready, 1)
            v.wait_ge(consts_in, 64)
            v.tensor_copy(tri[:], cn[:, C_TRI:C_TRI + P])
            v.tensor_copy(tok_f[:].rearrange("p b i -> p (b i)"), cn[:, C_TOK:C_TOK + B * TPB]).then_inc(small_ready, 1)
            v.wait_ge(small_ready, 2)
            v.tensor_copy(pad_rows[:, ROW - 1:ROW], cn[:, C_PAD:C_PAD + 1]).then_inc(small_ready, 1)
            v.wait_ge(cond_sig, 1)
            v.tensor_tensor(ct_sig[:], ct[:], ct_sig[:], ALU.mult).then_inc(cond_act, 1)
            v.wait_ge(cond_act, 1)
            v.tensor_copy(ct_rep[:], ct_sig[:].rearrange("p k b -> p (k b)").unsqueeze(2).to_broadcast([P, KD * B, P]))\
                .then_inc(cond_rep, 1)
            def first_rows(b):
                v.wait_ge(mod_mm, b + 1)
                v.tensor_copy(mod[:, b, M_S1, :], mod_ps(b, 0))
                v.tensor_scalar(mod[:, b, M_A1, :], mod_ps(b, 1), 1.0, None, ALU.add).then_inc(mod_rows, 1)

            def last_rows():
                v.wait_ge(mod_mm, 6)
                for b in range(B):
                    v.tensor_scalar(mod[:, b, M_A2, :], mod_ps(b, 4), 1.0, None, ALU.add)
                    i = v.tensor_copy(g_raw[:, (2 * b + 1) * D:(2 * b + 2) * D], mod_ps(b, 5))
                i.then_inc(mod_rows, 1)

            def gate_rows():
                gf = gates[:].rearrange("p b g d -> p (b g d)")
                v.wait_ge(rows_copied, 1)
                v.wait_ge(mod_rows, 3)
                v.scalar_tensor_tensor(gf, g_raw[:], -1.0, g_raw[:], ALU.mult, ALU.max).then_inc(mod_rows, 1)
                v.tensor_scalar(g_raw[:], g_raw[:], 0.0, 2.0, ALU.is_ge, ALU.mult).then_inc(mod_rows, 1)
                v.wait_ge(mod_rows, 5)
                v.tensor_scalar(gf, gf, 0.25, None, ALU.max).then_inc(mod_rows, 1)
                v.wait_ge(mod_rows, 6)
                v.scalar_tensor_tensor(gf, g_raw[:], -1.0, gf, ALU.add, ALU.mult).then_inc(mod_rows, 1)
                v.wait_ge(mod_rows, 7)
                for b in range(B):
                    i = v.tensor_tensor(mod[:, b, M_GBB, :], gates[:, b, 1, :], bias_row[:], ALU.mult)
                i.then_inc(mod_rows, 1)

            def split_gvd():
                v.wait_ge(w_hi[0], 1)
                for k in range(KD):
                    i = v.scalar_tensor_tensor(gvd_lo[:, k, :], gvd_raw[:, k, :], vec[:, V_MIX + k:V_MIX + k + 1],
                                               f32(gvd_hi[:, k, :]), ALU.mult, ALU.subtract)
                i.then_inc(w_lo[0], 1)

            def layer_norm_stats(q, x, stats, mv, bn, aggr):
                for i in range(TPB):
                    v.bn_stats(stats[:, i, :], x[:, i, :]).then_inc(bn, 1)
                v.wait_ge(bn, (q.v + 1) * TPB)
                v.memset(turn_mark[:], 0.0)
                for i in range(TPB):
                    v.bn_aggr(mv[:, i, :], stats[:, i, :]).then_inc(aggr, 1)
                v.wait_ge(aggr, (q.v + 1) * TPB)

            def front_centre(q):
                v.wait_ge(x_in, (q.v + 1) * 16)
                layer_norm_stats(q, x_sb, stats, mv, bn, aggr)
                for i in range(TPB):
                    a = v.scalar_tensor_tensor(h_sb[:, q.par, i, :], x_sb[:, i, :], mv[:, i, 0:1],
                                               mod[:, q.par, M_A1, :], ALU.subtract, ALU.mult)
                a.then_inc(xh, 1)

            def front_scale(q):
                v.wait_ge(rstd_r, q.v + 1)
                v.wait_ge(xh, q.v + 1)
                for i in range(TPB):
                    a = v.scalar_tensor_tensor(h_sb[:, q.par, i, :], h_sb[:, q.par, i, :], rstd[:, i:i + 1],
                                               mod[:, q.par, M_S1, :], ALU.mult, ALU.add)
                a.then_inc(h_ready, 1)

            def xn_lo(q):
                for c in range(KD):
                    v.wait_ge(xnT_h, q.v * KD + c + 1)
                    v.tensor_tensor(xnT_lo[:, c, :], tp[c], f32(xnT_hi[:, c, :]), ALU.subtract).then_inc(xnT_l, 1)

            def scan(q, c):
                v.wait_ge(gvd_act, q.v * 3 * KD + 3 * c + 3)
                v.tensor_scalar(dec_sb[:, c, :], dec_sb[:, c, :], 0.998, 0.001, ALU.mult, ALU.add).then_inc(dec_r, 1)
                v.wait_ge(dec_r, q.v * KD + c + 1)
                v.wait_ge(xs_r, q.v * KD + c + 1)
                if q.n >= 1:
                    v.wait_ge(carried, q.v * KD)
                v.tensor_tensor_scan(sg_sb[:, c, :], dec_sb[:, c, :], tv_sb[:, c, :], carry[:, q.par, c:c + 1],
                                     ALU.mult, ALU.add).then_inc(scanned, 1)

            def keep_last(q):
                for c in range(KD):
                    v.wait_ge(scanned, q.v * KD + c + 1)
                    v.tensor_copy(carry[:, q.par, c:c + 1], sg_sb[:, c, BLK - 1:BLK]).then_inc(carried, 1)

            def add_state(q):
                for u in range(2):
                    v.wait_ge(sT_t, q.v * 2 + u + 1)
                    t = slice(2 * u, 2 * u + 2)
                    v.tensor_tensor(xa_sb[:, q.par, t, :], tp[u].rearrange("p (i d) -> p i d", d=D),
                                    h_sb[:, q.par, t, :], ALU.add).then_inc(xa_r, 1)

            def xn2_lo(q):
                for c in range(KD):
                    v.wait_ge(xn2T_h, q.v * KD + c + 1)
                    v.tensor_tensor(xn2T_lo[:, c, :], tp[c], f32(xn2T_hi[:, c, :]), ALU.subtract).then_inc(xn2T_l, 1)

            def hidden(q, m):
                v.wait_ge(sig_r, q.v * KFA + m + 1)
                v.tensor_tensor(gg_sb[:, m % 2, :], bank("gu", q, 2 * m), sig_sb[:, m % 2, :], ALU.mult).then_inc(gg_r, 1)
                v.wait_ge(gu_mm, q.v * 2 * KFA + 2 * m + 2)
                if q.n >= 1 or m >= 2:
                    v.wait_ge(hid_l, q.v * KFA + max(m - 1, 0))
                v.wait_ge(gg_r, q.v * KFA + m + 1)
                v.tensor_tensor(hf_sb[:, m % 2, :], bank("gu", q, 2 * m + 1), gg_sb[:, m % 2, :], ALU.mult).then_inc(hf_r, 1)

            def add_ffn(q, u):
                if q.n >= 1 and u == 0:
                    v.wait_ge(x1_r, q.v)
                v.wait_ge(out_mm, q.v * 2 + u + 1)
                t = slice(2 * u, 2 * u + 2)
                v.tensor_tensor(xo_sb[:, t, :], bank("out", q, u).rearrange("p (i d) -> p i d", d=D),
                                xa_sb[:, q.par, t, :], ALU.add).then_inc(xo_r, 1)

            def gate_xo(q):
                v.wait_ge(xo_r, (q.v + 1) * 2)
                v.tensor_tensor(xo_sb[:], xo_sb[:], gates[:, q.par, 0, :].unsqueeze(1).to_broadcast([P, TPB, D]),
                                ALU.mult).then_inc(xg_r, 1)

            def norm2_centre(q):
                v.wait_ge(x1_r, q.v + 1)
                layer_norm_stats(q, x_again, stats2, mv2, bn2, aggr2)
                v.wait_ge(scattered[q.par], q.half * 32 * TPB + 16)
                for i in range(TPB):
                    a = v.scalar_tensor_tensor(rows[:, q.par, i, 0:D], x_again[:, i, :], mv2[:, i, 0:1],
                                               mod[:, q.par, M_A2, :], ALU.subtract, ALU.mult)
                a.then_inc(xh2, 1)

            def norm2_scale(q):
                v.wait_ge(rstd2_r, q.v + 1)
                v.wait_ge(xh2, q.v + 1)
                for i in range(TPB):
                    a = v.scalar_tensor_tensor(rows[:, q.par, i, 0:D], rows[:, q.par, i, 0:D], rstd2[:, i:i + 1],
                                               mod[:, q.par, M_S2, :], ALU.mult, ALU.add)
                a.then_inc(h2_ready, 1)

            ROUTE = 11

            def softmax_start(q):
                v.wait_ge(logit_mm, q.v + 1)
                link = chain(route, q.v * ROUTE)
                link(v.tensor_reduce(mx[:], logits, AX.X, ALU.max))
                v.tensor_tensor(zz[:], logits, mx[:].unsqueeze(2).to_broadcast([P, TPB, E]), ALU.subtract).then_inc(z_r, 1)

            def top2(q):
                link = chain(route, q.v * ROUTE + 1)
                v.wait_ge(exp_r, q.v + 1)
                link(v.tensor_reduce(mx[:], ee[:], AX.X, ALU.add))
                link(v.reciprocal(mx[:], mx[:]))
                link(v.tensor_tensor(pp[:], ee[:], mx[:].unsqueeze(2).to_broadcast([P, TPB, E]), ALU.mult))
                v.tensor_copy(rows[:, q.par, :, D + E], tok_f[:, q.par, :])
                for i in range(TPB):
                    a = v.max(top[:, i, :], pp[:, i, :])
                link(a)
                v.tensor_scalar(tok_f[:, q.par, :], tok_f[:, q.par, :], float(BLK), None, ALU.add)
                for i in range(TPB):
                    a = v.max_index(top_i[:, i, :], top[:, i, :], pp[:, i, :])
                link(a)
                link(v.tensor_copy(top_f[:], top_i[:, :, 0:2]))
                iota = cn[:, C_IOTA:C_IOTA + TPB * E].rearrange("p (i e) -> p i e", e=E)
                for k in range(2):
                    link(v.tensor_tensor(hot[:, k], iota, top_f[:, :, k:k + 1].to_broadcast([P, TPB, E]), ALU.is_equal))
                link(v.tensor_tensor(chosen[:], hot[:, 0], hot[:, 1], ALU.add))
                link(v.tensor_copy(chosen_b[:], chosen[:]))
                v.tensor_tensor(rows[:, q.par, :, D:D + E], chosen[:], pp[:], ALU.mult).then_inc(chosen_r, 1)

            SLOT = 5

            def slots(q):
                v.wait_ge(rank_mm, q.v + 1)
                link = chain(slot_steps, q.v * SLOT)
                link(v.tensor_tensor(pos[:], ranks, cn[:, C_OFF:C_OFF + E].unsqueeze(1).to_broadcast([P, TPB, E]), ALU.add))
                for k in range(2):
                    i = v.tensor_tensor(pos_k[:, k], pos[:], hot[:, k], ALU.mult)
                link(i)
                link(v.tensor_reduce(slot_f[:], pos_k[:], AX.X, ALU.add))
                v.wait_ge(scattered[q.par], q.half * 32 * TPB + 16)
                v.tensor_copy(slot_i[:, q.par], slot_f[:])
                link(v.tensor_reduce(seen_add[:], chosen[:].rearrange("p i e -> p e i"), AX.X, ALU.add))
                link(v.tensor_tensor(seen[:], seen[:], seen_add[:], ALU.add))
                v.tensor_copy(seen_b[:], seen[:]).then_inc(slots_r, 1)

            def step(r, turn):
                q = Block512(r, turn)
                nxt, routing, adding, ffn = q.near(1), q.near(-3), q.near(-2), q.near(-1)
                gvd_on, add_on, ffn_on, route_on = 0 <= r < NBLK, 2 <= r < NBLK + 2, 1 <= r <= NBLK, r >= 3
                if r == -1:
                    first_rows(0)
                    v.wait_ge(mod_rows, 1)
                if r == 0:
                    v.wait_ge(mod_rows, 2)
                if r + 1 < NBLK:
                    front_centre(nxt)
                if r == NBLK + 2:
                    split_w13_lo(v, 0, 0)
                if r + 1 < NBLK:
                    front_scale(nxt)
                if route_on:
                    softmax_start(routing)
                if gvd_on:
                    scan(q, 0)
                if route_on:
                    top2(routing)
                if gvd_on:
                    scan(q, 1)
                    keep_last(q)
                if add_on:
                    add_ffn(adding, 0)
                if r == -1:
                    first_rows(1)
                    last_rows()
                    split_gvd()
                if r + 1 < NBLK:
                    xn_lo(nxt)
                if route_on:
                    slots(routing)
                if add_on:
                    add_ffn(adding, 1)
                    gate_xo(adding)
                if ffn_on:
                    hidden(ffn, 0)
                if gvd_on:
                    add_state(q)
                if r == 0:
                    gate_rows()
                if ffn_on:
                    hidden(ffn, 1)
                if add_on:
                    norm2_centre(adding)
                if ffn_on:
                    hidden(ffn, 2)
                if add_on:
                    norm2_scale(adding)
                if ffn_on:
                    hidden(ffn, 3)
                if ffn_on:
                    hidden(ffn, 4)
                    hidden(ffn, 5)
                if gvd_on:
                    xn2_lo(q)
                if ffn_on:
                    hidden_lo(v, ffn, 5)

            body(step, v)

            v.wait_ge(total_mm, 1)
            link = chain(tabs, 0)
            link(v.tensor_copy(counts[:], total))
            v.tensor_copy(counts_i[:], counts[:]).then_inc(counted, 1)
            link(v.tensor_scalar(tiles_f[:], counts[:], 1.0, float(P - 1), ALU.max, ALU.add))
            link(v.tensor_copy(tiles_i[:], tiles_f[:]))
            link(v.tensor_scalar(tiles_i[:], tiles_i[:], P.bit_length() - 1, None, ALU.logical_shift_right))
            link(v.tensor_copy(tiles_f[:], tiles_i[:]))
            v.tensor_tensor_scan(tiles_end[:], ones_f[:], tiles_f[:], 0.0, ALU.mult, ALU.add)
            link(v.tensor_scalar(step_e[:], tiles_f[:], -float(P), float(REGION), ALU.mult, ALU.add))
            v.tensor_scalar(meets[:], tiles_end[:], cn[:, C_TILE:C_TILE + 1], None, ALU.is_equal)
            link(v.tensor_scalar(passed[:], tiles_end[:], cn[:, C_TILE:C_TILE + 1], None, ALU.is_le))
            v.tensor_reduce(tcol2[:, TAB_EXPERT:TAB_EXPERT + 1], passed[:, 0:E - 1], AX.X, ALU.add)
            v.scalar_tensor_tensor(to_split[:], cn[:, C_IOTA:C_IOTA + E], 2.0, meets[:], ALU.add, ALU.mult)
            v.scalar_tensor_tensor(to_load[:], cn[:, C_IOTA:C_IOTA + E], 4.0, meets[:], ALU.add, ALU.mult)
            v.tensor_tensor(load_to[:], cn[:, C_BUF:C_BUF + E], meets[:], ALU.mult)
            link(v.tensor_tensor(jump[:], passed[:], step_e[:], ALU.mult))
            v.tensor_reduce(tcol2[:, TAB_SPLIT:TAB_SPLIT + 1], to_split[:, 0:E - 2], AX.X, ALU.add)
            v.tensor_reduce(tcol2[:, TAB_LOAD:TAB_LOAD + 1], to_load[:, 0:E - 4], AX.X, ALU.add)
            v.tensor_reduce(tcol2[:, TAB_BUF:TAB_BUF + 1], load_to[:, 0:E - 4], AX.X, ALU.add)
            link(v.tensor_reduce(tcol[:, 1:2], jump[:], AX.X, ALU.add))
            v.tensor_scalar(tcol2[:, TAB_BEFORE:TAB_BEFORE + 1], tcol2[:, TAB_LOAD:TAB_LOAD + 1], -1.0, 0.0, ALU.add, ALU.max)
            link(v.scalar_tensor_tensor(tcol[:, 1:2], cn[:, C_TILE:C_TILE + 1], float(P), tcol[:, 1:2],
                                        ALU.mult, ALU.add))
            link(v.tensor_scalar(tcol2[:, TAB_ROW:TAB_ROW + 1], tcol[:, 1:2], float(E * REGION), None, ALU.min))
            v.wait_ge(tab_t, 1)
            v.tensor_copy(tab[0:TAB_N, :], tp[0][0:TAB_N, 0:P]).then_inc(tab_ready, 1)
            split_w13_lo(v, 1, EXPW)

        @block.gpsimd
        def _(g):
            def power(dst, src):
                return g.tensor_tensor(dst[:], src[:], minus_half[:], ALU.pow)

            def row(b, m):
                return mod[:, b, m, :].unsqueeze(1).to_broadcast([P, TPB, D])

            def front(q):
                g.wait_ge(aggr, (q.v + 1) * TPB)
                g.tensor_tensor(ve[:], mv[:, :, 1], eps_ln[:], ALU.add).then_inc(var_eps, 1)
                g.wait_ge(var_eps, q.v + 1)
                power(rstd, ve).then_inc(rstd_r, 1)

            def rms1(q):
                g.wait_ge(ssq_r, q.v + 1)
                g.tensor_tensor(ms[:], ssq[:], eps_rms[:], ALU.add).then_inc(ms_r, 1)
                g.wait_ge(ms_r, q.v + 1)
                power(rms, ms).then_inc(rms_r, 1)

            def rms_2(q):
                g.wait_ge(ssq2_r, q.v + 1)
                g.tensor_tensor(ms2[:], ssq2[:], eps_rms[:], ALU.add).then_inc(ms2_r, 1)
                g.wait_ge(ms2_r, q.v + 1)
                power(rms2, ms2).then_inc(rms2_r, 1)

            def split_gu():
                g.wait_ge(w_hi[1], 1)
                g.tensor_tensor(gu_lo[:], gu_raw[:], f32(gu_hi[:]), ALU.subtract).then_inc(w_lo[1], 1)

            def split_out():
                g.wait_ge(w_hi[2], 1)
                g.tensor_tensor(out_lo[:].rearrange("p k n -> p (k n)"), out_raw[:],
                                f32(out_hi[:].rearrange("p k n -> p (k n)")), ALU.subtract).then_inc(w_lo[2], 1)

            def gated_value(q, c):
                g.wait_ge(gvd_act, q.v * 3 * KD + 3 * c + 2)
                g.tensor_tensor(tv_sb[:, c, :], sg_sb[:, c, :], tv_sb[:, c, :], ALU.mult).then_inc(xs_r, 1)

            def residual(q):
                g.wait_ge(xg_r, q.v + 1)
                g.wait_ge(x_again_in, (q.v + 1) * 16)
                g.tensor_tensor(x_again[:], x_again[:], xo_sb[:], ALU.add).then_inc(x1_r, 1)

            def norm2(q):
                g.wait_ge(aggr2, (q.v + 1) * TPB)
                g.tensor_tensor(ve2[:], mv2[:, :, 1], eps_ln[:], ALU.add).then_inc(var_eps2, 1)
                g.wait_ge(var_eps2, q.v + 1)
                power(rstd2, ve2).then_inc(rstd2_r, 1)

            def result_base(q):
                g.wait_ge(xh2, q.v + 1)
                g.wait_ge(x1_r, q.v + 1)
                g.tensor_tensor(x_again[:], x_again[:], row(q.par, M_GBB), ALU.add).then_inc(base_r, 1)

            def scatter(q, tiles_of):
                if 0 in tiles_of:
                    g.wait_ge(slots_r, q.v + 2)
                    mark(g)
                for i in tiles_of:
                    for k in range(2):
                        g.indirect_dma_start(routed, bass.IndirectOffsetOnAxis(ap=slot_i[:, q.par, k, i:i + 1], axis=0),
                                             rows[:, q.par, i, :], None)\
                            .then_inc(scattered[q.par], 16)

            def step(r, turn):
                q = Block512(r, turn)
                nxt, routing, adding, ffn = q.near(1), q.near(-3), q.near(-2), q.near(-1)
                gvd_on, add_on, ffn_on, route_on = 0 <= r < NBLK, 2 <= r < NBLK + 2, 1 <= r <= NBLK, r >= 3
                if r + 1 < NBLK:
                    front(nxt)
                if gvd_on:
                    gated_value(q, 0)
                if r + 1 < NBLK:
                    rms1(nxt)
                if gvd_on:
                    gated_value(q, 1)
                if r == 0:
                    split_gu()
                if r == NBLK + 2:
                    for e in range(2):
                        split_w2_lo(g, e, e * EXPW)
                if route_on:
                    scatter(routing, [0, 1])
                if add_on:
                    residual(adding)
                if gvd_on:
                    rms_2(q)
                if ffn_on:
                    hidden_lo(g, ffn, 0)
                if add_on:
                    norm2(adding)
                if ffn_on:
                    hidden_lo(g, ffn, 1)
                if ffn_on:
                    hidden_lo(g, ffn, 2)
                if route_on:
                    scatter(routing, [2])
                if ffn_on:
                    hidden_lo(g, ffn, 3)
                if r == 1:
                    split_out()
                if r == 2:
                    g.wait_ge(mod_rows, 8)
                if add_on:
                    result_base(adding)
                if ffn_on:
                    hidden_lo(g, ffn, 4)
                if route_on:
                    scatter(routing, [3])

            g.wait_ge(small_ready, 3)
            g.dma_start(routed[E * REGION:ROWS, :], pad_rows[:]).then_inc(scattered[0], 16)
            g.dma_start(out[T:T + P, :], pad_rows[:, 0:D]).then_inc(scattered[1], 16)
            body(step, g)

        rows_in = [sem(f"rows_in{n}") for n in range(SLOTS)]
        xT_t, xT_h, xT_l, a_mm, b_mm, gelu_r, hid_r = (sem(n) for n in ("xT_t", "xT_h", "xT_l", "a_mm", "b_mm", "gelu_r", "hid_r"))
        hidT_t, hidT_h, hidT_l, y_r = (sem(n) for n in ("hidT_t", "hidT_h", "hidT_l", "y_r"))
        gate_steps, gates_r, y_sum, added = sem("gate_steps"), sem("gates_r"), sem("y_sum"), sem("added")
        PS_Y, PS_HT, PS_XT = 4, 5, 7
        y_ps, xT_ps = ps[:, PS_Y, 0:D], ps[:, PS_XT, 0:KD * P]
        hidT_ps = ps[:, PS_HT:PS_HT + 2, :].rearrange("p a n -> p (a n)")[:, 0:KF * P]

        class Tile:

            def __init__(self, n, turn=None):
                self.n, self.turn, self.par, self.slot = n, turn, n % 2, n % SLOTS
                self.v = n if turn is None else turn * SLOTS + n
                self.round = n // SLOTS if turn is None else turn + n // SLOTS

            def near(self, d):
                return Tile(self.n + d, self.turn)

        ALONE = 3

        def tiles(engine, first, step, last):
            engine.wait_ge(tab_ready, 1)
            first(Tile(0))
            for n in range(1, ALONE):
                step(Tile(n))
            with engine.Fori(0, (MOE_TILES - ALONE) // SLOTS, 1) as turn:
                for n in range(ALONE, ALONE + SLOTS):
                    step(Tile(n, turn))
            last(Tile(MOE_TILES - 1))

        assert (MOE_TILES - ALONE) % SLOTS == 0

        def entry(eng, which, t, top):
            return eng.value_load(tab[which:which + 1, bass.ds(t.v, 1)], min_val=0, max_val=top)

        def split_behind(eng, e, t, split):
            with eng.If(e > 0):
                split(eng, e, (e & 1) * EXPW, t)

        def to_be_split(eng, t):
            return entry(eng, TAB_SPLIT, t, E - 1)


        @block.sync
        def _(sp):
            def load_rows(t):
                row = entry(sp, TAB_ROW, t, E * REGION)
                if t.n >= SLOTS:
                    sp.wait_ge(xT_t, t.v - SLOTS + 1)
                    sp.wait_ge(gates_r, t.v - SLOTS + 1)
                sp.dma_start(x_moe[:, t.slot, :], routed[bass.ds(row, P), :]).then_inc(rows_in[t.slot], 16)

            def load_behind(t):
                e = entry(sp, TAB_LOAD, t, E - 1)
                with sp.If(e > 0):
                    load_weights(sp, entry(sp, TAB_BEFORE, t, E - 2), e, entry(sp, TAB_BUF, t, EXPW))

            sp.wait_ge(tab_ready, 1)
            for b in range(2):
                sp.wait_ge(scattered[b], NBLK // 2 * 32 * TPB + 16)
            for n in range(SLOTS + ALONE - 1):
                load_rows(Tile(n))
                if n == 1:
                    load_weights(sp, 2, 3, 1)
            with sp.Fori(0, (MOE_TILES - ALONE) // SLOTS, 1) as turn:
                for n in range(SLOTS):
                    load_rows(Tile(n + SLOTS + ALONE - 1, turn))
                    load_behind(Tile(n + 1, turn))
            for n in range(SLOTS):
                sp.wait_ge(rows_in[n], ((MOE_TILES + SLOTS - 2 - n) // SLOTS + 1) * 16)

        @block.tensor
        def _(pe):
            def three(dst, a_hi, a_lo, b_hi, b_lo, first, last):
                pe.matmul(dst, a_hi, b_hi, start=first, stop=False)
                pe.matmul(dst, a_lo, b_hi, start=False, stop=False)
                return pe.matmul(dst, a_hi, b_lo, start=False, stop=last)

            def x_transposes(t):
                pe.wait_ge(rows_in[t.slot], t.round * 16 + 16)
                if t.n >= 1:
                    pe.wait_ge(xT_l, t.v)
                for k in range(KD):
                    mm = pe.transpose(xT_ps[:, k * P:(k + 1) * P], x_moe[:, t.slot, k * P:(k + 1) * P], ident)
                mm.then_inc(xT_t, 1)

            def first_products(t, e):
                pe.wait_ge(w13_lo, e + 1)
                pe.wait_ge(xT_l, t.v + 1)
                for n in range(4):
                    if t.n >= 1 and n == 0:
                        pe.wait_ge(gelu_r, t.v)
                    if t.n >= 1 and n == 2:
                        pe.wait_ge(hid_r, t.v)
                    for k in range(KD):
                        w = bass.ds((e & 1) * EXPW + (k * 2 * F + n * FH), FH)
                        mm = three(ps[:, n, 0:FH], xT_moe_hi[:, t.par, k, :], xT_moe_lo[:, t.par, k, :],
                                   w_moe_hi[:, w], w_moe_lo[:, w], k == 0, k == KD - 1)
                    if n % 2:
                        mm.then_inc((a_mm, b_mm)[n // 2], 1)

            def hid_transposes(t):
                pe.wait_ge(hid_r, t.v + 1)
                if t.n >= 1:
                    pe.wait_ge(hidT_l, t.v)
                for k in range(KF):
                    mm = pe.transpose(hidT_ps[:, k * P:(k + 1) * P], hid_moe[:, k * P:(k + 1) * P], ident)
                mm.then_inc(hidT_t, 1)

            def second_product(t, e):
                pe.wait_ge(w2_lo, e + 1)
                pe.wait_ge(hidT_l, t.v + 1)
                if t.n >= 1:
                    pe.wait_ge(y_r, t.v)
                for k in range(KF - 1):
                    w = bass.ds((e & 1) * EXPW + (W13 + k * D), D)
                    three(y_ps, hidT_hi[:, k, :], hidT_lo[:, k, :], w_moe_hi[:, w], w_moe_lo[:, w], k == 0, False)
                w = bass.ds((e & 1) * EXPW + (EXPW - D), D)
                pe.matmul(y_ps, hidT_hi[:, KF - 1, :], w_moe_hi[:, w], start=False, stop=False)
                pe.matmul(y_ps, hidT_hi[0:F_LAST, KF - 1, :], w_moe_lo[0:F_LAST, w], start=False, stop=True).then_inc(y_mm, 1)

            kept = pe.alloc_register("expert_of_tile_before")

            def first(t):
                e = entry(pe, TAB_EXPERT, t, E - 1)
                x_transposes(t)
                first_products(t, e)
                x_transposes(t.near(1))
                pe.reg_mov(kept, e)

            def step(t):
                e = entry(pe, TAB_EXPERT, t, E - 1)
                hid_transposes(t.near(-1))
                first_products(t, e)
                x_transposes(t.near(1))
                second_product(t.near(-1), pe.snap(kept, min_val=0, max_val=E - 1))
                pe.reg_mov(kept, e)

            def last(t):
                hid_transposes(t)
                second_product(t, pe.snap(kept, min_val=0, max_val=E - 1))

            tiles(pe, first, step, last)

        @block.scalar
        def _(act):
            def xT_split(t):
                act.wait_ge(xT_t, t.v + 1)
                if t.n >= 2:
                    act.wait_ge(b_mm, t.v - 1)
                act.activation(xT_moe_hi[:, t.par].rearrange("p k n -> p (k n)"), xT_ps, ACT.Copy).then_inc(xT_h, 1)

            def gelu(t):
                act.wait_ge(a_mm, t.v + 1)
                if t.n >= 1:
                    act.wait_ge(hid_r, t.v)
                act.activation(gelu_moe[:], ps[:, 0:2, 0:FH], ACT.Gelu).then_inc(gelu_r, 1)

            def hidT_split(t):
                act.wait_ge(hidT_t, t.v + 1)
                if t.n >= 1:
                    act.wait_ge(y_mm, t.v)
                act.activation(hidT_hi[:].rearrange("p k n -> p (k n)"), hidT_ps, ACT.Copy).then_inc(hidT_h, 1)

            def first(t):
                xT_split(t)
                step(t)

            def step(t):
                if t.n >= 2:
                    e_before = to_be_split(act, t.near(-1))
                if t.n >= 1:
                    e = to_be_split(act, t)
                gelu(t)
                xT_split(t.near(1))
                if t.n >= 2:
                    split_behind(act, e_before, t.near(-1), split_w2_hi)
                hidT_split(t)
                if t.n >= 1:
                    split_behind(act, e, t, split_w13_hi)

            tiles(act, first, step, lambda t: None)

        @block.vector
        def _(v):
            def take_gates(t):
                e = entry(v, TAB_EXPERT, t, E - 1)
                g, tok = gate_moe[:, t.slot, :], x_moe[:, t.slot, D + E:D + E + 1]
                v.wait_ge(rows_in[t.slot], t.round * 16 + 16)
                v.tensor_scalar(g[:, 1:2], tok, float(S), None, ALU.is_ge)
                v.tensor_copy(g[:, 0:1], x_moe[:, t.slot, bass.ds(e + D, 1)]).then_inc(gate_steps, 1)
                v.wait_ge(gate_steps, t.v * 2 + 1)
                v.tensor_tensor(g[:, 2:3], g[:, 0:1], g[:, 1:2], ALU.mult).then_inc(gate_steps, 1)
                v.wait_ge(gate_steps, t.v * 2 + 2)
                v.tensor_tensor(g[:, 3:4], g[:, 0:1], g[:, 2:3], ALU.subtract)
                if t.n >= ALONE:
                    v.wait_ge(added, (t.v - ALONE + 1) * 16)
                v.tensor_copy(tok_moe[:, t.slot, :], tok).then_inc(gates_r, 1)

            def xT_rest(t):
                v.wait_ge(xT_h, t.v + 1)
                v.tensor_tensor(xT_moe_lo[:, t.par].rearrange("p k n -> p (k n)"), xT_ps,
                                f32(xT_moe_hi[:, t.par].rearrange("p k n -> p (k n)")), ALU.subtract).then_inc(xT_l, 1)

            def multiply(t):
                v.wait_ge(gelu_r, t.v + 1)
                v.wait_ge(b_mm, t.v + 1)
                if t.n >= 1:
                    v.wait_ge(hidT_t, t.v)
                v.tensor_tensor(hid_moe[:, F:KF * P], ps[:, 3, FH - F_LAST:FH], gelu_moe[:, 1, FH - F_LAST:FH], ALU.mult)
                v.tensor_tensor(hid_moe[:, 0:F].rearrange("p (h n) -> p h n", h=2), ps[:, 2:4, 0:FH], gelu_moe[:],
                                ALU.mult).then_inc(hid_r, 1)

            def gate_y(t):
                v.wait_ge(y_mm, t.v + 1)
                v.wait_ge(gates_r, t.v + 1)
                if t.n >= 2:
                    v.wait_ge(added, (t.v - 1) * 16)
                for b in range(B):
                    i = v.scalar_tensor_tensor(y_moe[:, t.slot, b, :], y_ps, gate_moe[:, t.slot, 3 - b:4 - b],
                                               gates[:, b, 1, :], ALU.mult, ALU.mult)
                i.then_inc(y_r, 1)

            def hidT_rest(t):
                v.wait_ge(hidT_h, t.v + 1)
                full = (KF - 1) * P
                v.tensor_tensor(hidT_lo[:].rearrange("p k n -> p (k n)"), hidT_ps[:, 0:full],
                                f32(hidT_hi[:, 0:KF - 1, :].rearrange("p k n -> p (k n)")), ALU.subtract)
                v.tensor_tensor(hidT_hi[F_LAST:P, KF - 1, :], hidT_ps[F_LAST:P, full:],
                                f32(hidT_hi[F_LAST:P, KF - 1, :]), ALU.subtract).then_inc(hidT_l, 1)

            def first(t):
                take_gates(t)
                xT_rest(t)
                multiply(t)
                xT_rest(t.near(1))
                hidT_rest(t)
                take_gates(t.near(1))

            def step(t):
                e = to_be_split(v, t)
                multiply(t)
                xT_rest(t.near(1))
                gate_y(t.near(-1))
                hidT_rest(t)
                take_gates(t.near(1))
                split_behind(v, e, t, split_w13_lo)

            tiles(v, first, step, gate_y)

        @block.gpsimd
        def _(g):
            def add_rows(t):
                g.wait_ge(y_r, t.v + 1)
                g.tensor_tensor(y_moe[:, t.slot, 0, :], y_moe[:, t.slot, 0, :], y_moe[:, t.slot, 1, :], ALU.add)\
                    .then_inc(y_sum, 1)
                g.wait_ge(y_sum, t.v + 1)
                if t.n >= 1:
                    g.wait_ge(added, t.v * 16)
                mark(g)
                g.indirect_dma_start(out, bass.IndirectOffsetOnAxis(ap=tok_moe[:, t.slot, :], axis=0),
                                     y_moe[:, t.slot, 0, :], None,
                                     compute_op=ALU.add).then_inc(added, 16)

            def step(t):
                e = to_be_split(g, t)
                split_behind(g, e, t, split_w2_lo)
                add_rows(t)

            tiles(g, add_rows, step, lambda t: None)
            g.wait_ge(added, MOE_TILES * 16)


def kernel(**inputs):
    import concourse.bacc as bacc
    from concourse.bass_utils import run_bass_kernel_spmd

    a = {k: np.asarray(v) for k, v in inputs.items()}
    col = lambda v: v.reshape(-1, P).T
    arrays = {
        "x": a["L0_attn_x"],
        "gvd_t": np.concatenate([a["L0_attn_Wg"].T, a["L0_attn_Wv"].T, a["L0_attn_Wd"].T], axis=1),
        "gu_t": np.concatenate([a["L0_attn_W_gate"].T, a["L0_attn_W_up"].T], axis=1),
        "out_t": a["L0_attn_W_out"].T,
        "vecs": np.concatenate([col(a["L0_attn_bg"]), col(a["L0_attn_bv"]), col(a["L0_attn_bd"]),
                                col(a["L0_attn_rms_mix_w"]), col(a["L0_attn_rms_ffn_w"])], axis=1),
        "cond_t": a["L0_c"].T.reshape(KD, P, B).transpose(1, 0, 2),
        "wmod": a["L0_wmod"],
        "bias": a["L0_ffn_bias"],
        "router": a["L0_ffn_router_w"].reshape(KD, P, E).transpose(1, 0, 2),
        "w13": np.concatenate([a["L0_ffn_w1"], a["L0_ffn_v1"]], axis=2),
        "w2": a["L0_ffn_w2"],
        "consts": constants(),
    }
    arrays = {f"in_{k}": np.ascontiguousarray(v) for k, v in arrays.items()}
    nc = bacc.Bacc("TRN2", target_bir_lowering=False, num_devices=1)
    args = [nc.dram_tensor(k, v.shape, mybir.dt.from_np(v.dtype), kind="ExternalInput").ap() for k, v in arrays.items()]
    out = nc.dram_tensor("out_rows", (T + P, D), F32, kind="ExternalOutput").ap()
    adaln_moe_kernel(nc, *args, out)
    r = run_bass_kernel_spmd(nc, [arrays], core_ids=[0])
    return r.results[0]["out_rows"][:T].reshape(B, S, D)
```
